# Optimizing a Trainium2 kernel written in Bass

```python
import numpy as np
import jax
import jax.numpy as jnp

def _softmax(x, axis=-1):
    return jax.nn.softmax(x, axis=axis)

def _gelu(x):
    return jax.nn.gelu(x, approximate=True)

def _silu(x):
    return jax.nn.silu(x)

def _sigmoid(x):
    return jax.nn.sigmoid(x)

def _layernorm(x, axis=-1, eps=1e-05):
    m = jnp.mean(x, axis=axis, keepdims=True)
    v = jnp.var(x, axis=axis, keepdims=True)
    return (x - m) / jnp.sqrt(v + eps)

def _scatter_add(tgt, idx, src, axis=0):
    return tgt.at[idx].add(src)

def _segment_sum(src, seg, n):
    return jax.ops.segment_sum(src, seg, n)
kernel_name = 'mk_gnn_resnorm_d4_gnn_r8_b541b9'

def setup_inputs(seed: int=0):
    np.random.seed(seed)
    _w = jnp.asarray

    def _rec_inputs():
        import jax
        import jax.numpy as jnp
        _gk = jax.random.key(seed)
        x = 0.4998 + 0.2887 * jax.random.normal(jax.random.fold_in(_gk, 1), (12500, 16), jnp.float32)
        _s = jax.random.randint(jax.random.fold_in(_gk, 2), (200000,), 0, 12500, jnp.int32)
        _d = jax.random.randint(jax.random.fold_in(_gk, 3), (200000,), 0, 12500, jnp.int32)
        _loop = jnp.arange(12500, dtype=jnp.int32)
        src = jnp.concatenate([_s, _d, _loop])
        dst = jnp.concatenate([_d, _s, _loop])
        _o = jnp.argsort(dst, stable=True)
        src = src[_o]
        dst = dst[_o]
        edge_attr_13 = 2.91757e-06 + 0.999892 * jax.random.normal(jax.random.fold_in(_gk, 12), (412500, 13), jnp.float32)
        edge_type_8 = jax.random.randint(jax.random.fold_in(_gk, 14), (412500,), 0, 8, jnp.int32)
        edge_weight = jax.random.uniform(jax.random.fold_in(_gk, 15), (412500,), jnp.float32, 0.0, 1)
        return (x, src, dst, edge_attr_13, edge_type_8, edge_weight)
    x, src, dst, edge_attr_13, edge_type_8, edge_weight = _rec_inputs()

    def _L0_gnn_setup():
        import jax, jax.numpy as jnp
        import numpy as np
        N_NODES = 12500
        key = jax.random.key(seed)
        k1, k2, k3, k4 = jax.random.split(key, 4)
        E = 400000
        D = 16
        x = jax.random.uniform(k1, (N_NODES, D), dtype=jnp.float32)
        edge_index = jax.random.randint(k2, (2, E), 0, N_NODES, dtype=jnp.int64)
        edge_probs = jax.random.uniform(k3, (E,), dtype=jnp.float32)
        weight = jnp.ones((D,), dtype=jnp.float32)
        self_loop_weight = jnp.asarray(0.1, dtype=jnp.float32)
        return {'x': x, 'edge_index': edge_index, 'edge_probs': edge_probs, 'weight': weight, 'self_loop_weight': self_loop_weight}
    _L0_gnn_all = _L0_gnn_setup()
    _L0_gnn_in = {k: v for k, v in _L0_gnn_all.items() if k in ('weight', 'self_loop_weight')}
    del _L0_gnn_all

    def _L1_gnn_setup():
        import jax, jax.numpy as jnp
        import numpy as np
        N = 6250
        E = 100000
        NC = 16
        FDIM = 13
        HID = 32
        NREPEATS = 2

        def _gru_cell(x, h, w_ih, w_hh, b_ih, b_hh):
            gi = x @ w_ih.T + b_ih
            gh = h @ w_hh.T + b_hh
            i_r, i_z, i_n = jnp.split(gi, 3, axis=1)
            h_r, h_z, h_n = jnp.split(gh, 3, axis=1)
            r = jax.nn.sigmoid(i_r + h_r)
            z = jax.nn.sigmoid(i_z + h_z)
            n = jnp.tanh(i_n + r * h_n)
            return (1.0 - z) * n + z * h
        key = jax.random.key(seed)
        ks = jax.random.split(key, 10)
        hx = jax.random.normal(ks[0], (N, NC), dtype=jnp.float32)
        edgefeats = jax.random.normal(ks[1], (E, FDIM), dtype=jnp.float32)
        edge_src = jax.random.randint(ks[2], (E,), 0, N, dtype=jnp.int32)
        edge_dst = jax.random.randint(ks[3], (E,), 0, N, dtype=jnp.int32)
        fnet_w1 = jax.random.normal(ks[4], (FDIM, HID), dtype=jnp.float32) * (1.0 / np.sqrt(FDIM))
        fnet_b1 = jnp.zeros((HID,), dtype=jnp.float32)
        fnet_w2 = jax.random.normal(ks[5], (HID, NC * NC), dtype=jnp.float32) * (0.1 / np.sqrt(HID))
        fnet_b2 = jnp.zeros((NC * NC,), dtype=jnp.float32)
        gru_w_ih = jax.random.normal(ks[6], (3 * NC, NC), dtype=jnp.float32) * (1.0 / np.sqrt(NC))
        gru_w_hh = jax.random.normal(ks[7], (3 * NC, NC), dtype=jnp.float32) * (1.0 / np.sqrt(NC))
        gru_b_ih = jnp.zeros((3 * NC,), dtype=jnp.float32)
        gru_b_hh = jnp.zeros((3 * NC,), dtype=jnp.float32)
        return {'hx': hx, 'edgefeats': edgefeats, 'edge_src': edge_src, 'edge_dst': edge_dst, 'fnet_w1': fnet_w1, 'fnet_b1': fnet_b1, 'fnet_w2': fnet_w2, 'fnet_b2': fnet_b2, 'gru_w_ih': gru_w_ih, 'gru_w_hh': gru_w_hh, 'gru_b_ih': gru_b_ih, 'gru_b_hh': gru_b_hh}
    _L1_gnn_all = _L1_gnn_setup()
    _L1_gnn_in = {k: v for k, v in _L1_gnn_all.items() if k in ('fnet_w1', 'fnet_b1', 'fnet_w2', 'fnet_b2', 'gru_w_ih', 'gru_w_hh', 'gru_b_ih', 'gru_b_hh')}
    del _L1_gnn_all

    def _L2_gnn_setup():
        import jax, jax.numpy as jnp
        import numpy as np
        N = 12500
        E = 100000
        F_IN = 16
        H1, C1 = (3, 32)
        H2, C2 = (1, 32)
        NC = 16
        SLOPE = 0.2

        def _gat_layer(x, src, dst, W, a_s, a_d, b, heads, outc):
            h = (x @ W).reshape(N, heads, outc)
            alpha_s = (h * a_s).sum(-1)
            alpha_d = (h * a_d).sum(-1)
            e = jax.nn.leaky_relu(alpha_s[src] + alpha_d[dst], SLOPE)
            m = jax.ops.segment_max(e, dst, num_segments=N)
            p = jnp.exp(e - m[dst])
            z = jax.ops.segment_sum(p, dst, num_segments=N)
            alpha = p / (z[dst] + 1e-16)
            out = jax.ops.segment_sum(h[src] * alpha[:, :, None], dst, num_segments=N)
            return out.reshape(N, heads * outc) + b
        key = jax.random.key(seed)
        ks = jax.random.split(key, 12)
        s = 0.1
        return {'x': jax.random.normal(ks[0], (N, F_IN), jnp.float32), 'edge_index': jax.random.randint(ks[1], (2, E), 0, N, dtype=jnp.int32), 'W1': jax.random.normal(ks[2], (F_IN, H1 * C1), jnp.float32) * s, 'a_src1': jax.random.normal(ks[3], (H1, C1), jnp.float32) * s, 'a_dst1': jax.random.normal(ks[4], (H1, C1), jnp.float32) * s, 'b1': jnp.zeros((H1 * C1,), jnp.float32), 'W2': jax.random.normal(ks[5], (H1 * C1, H2 * C2), jnp.float32) * s, 'a_src2': jax.random.normal(ks[6], (H2, C2), jnp.float32) * s, 'a_dst2': jax.random.normal(ks[7], (H2, C2), jnp.float32) * s, 'b2': jnp.zeros((H2 * C2,), jnp.float32), 'Wf': jax.random.normal(ks[8], (C2, NC), jnp.float32) * s, 'bf': jnp.zeros((NC,), jnp.float32)}
    _L2_gnn_all = _L2_gnn_setup()
    _L2_gnn_in = {k: v for k, v in _L2_gnn_all.items() if k in ('W1', 'a_src1', 'a_dst1', 'b1', 'W2', 'a_src2', 'a_dst2', 'b2', 'Wf', 'bf')}
    del _L2_gnn_all

    def _L3_gnn_setup():
        import jax, jax.numpy as jnp
        import numpy as np
        N_NODES = 12500
        N_EDGES = 400000
        NUM_REL = 8

        def _rgcn_layer(x, src, dst, edge_type, W, root, bias):
            out = x @ root + bias
            x_src = x[src]
            for r in range(W.shape[0]):
                mask = (edge_type == r).astype(x.dtype)
                s = jax.ops.segment_sum(x_src * mask[:, None], dst, num_segments=x.shape[0])
                cnt = jax.ops.segment_sum(mask, dst, num_segments=x.shape[0])
                agg = s / jnp.clip(cnt, 1.0)[:, None]
                out = out + agg @ W[r]
            return out
        key = jax.random.key(seed)
        ks = jax.random.split(key, 9)
        x = jax.random.normal(ks[0], (N_NODES, 16), dtype=jnp.float32)
        edge_index = jax.random.randint(ks[1], (2, N_EDGES), 0, N_NODES, dtype=jnp.int32)
        edge_type = jax.random.randint(ks[2], (N_EDGES,), 0, NUM_REL, dtype=jnp.int32)
        s1 = 1.0 / np.sqrt(16.0)
        s2 = 1.0 / np.sqrt(32.0)
        W1 = jax.random.normal(ks[3], (NUM_REL, 16, 32), dtype=jnp.float32) * s1
        root1 = jax.random.normal(ks[4], (16, 32), dtype=jnp.float32) * s1
        b1 = jnp.zeros((32,), dtype=jnp.float32)
        W2 = jax.random.normal(ks[5], (NUM_REL, 32, 16), dtype=jnp.float32) * s2
        root2 = jax.random.normal(ks[6], (32, 16), dtype=jnp.float32) * s2
        b2 = jnp.zeros((16,), dtype=jnp.float32)
        return {'x': x, 'edge_index': edge_index, 'edge_type': edge_type, 'W1': W1, 'root1': root1, 'b1': b1, 'W2': W2, 'root2': root2, 'b2': b2}
    _L3_gnn_all = _L3_gnn_setup()
    _L3_gnn_in = {k: v for k, v in _L3_gnn_all.items() if k in ('W1', 'root1', 'b1', 'W2', 'root2', 'b2')}
    del _L3_gnn_all
    return {'x': x, 'src': src, 'dst': dst, 'edge_attr_13': edge_attr_13, 'edge_type_8': edge_type_8, 'edge_weight': edge_weight, 'L0_gnn_weight': _L0_gnn_in['weight'], 'L0_gnn_self_loop_weight': _L0_gnn_in['self_loop_weight'], 'L1_gnn_fnet_w1': _L1_gnn_in['fnet_w1'], 'L1_gnn_fnet_b1': _L1_gnn_in['fnet_b1'], 'L1_gnn_fnet_w2': _L1_gnn_in['fnet_w2'], 'L1_gnn_fnet_b2': _L1_gnn_in['fnet_b2'], 'L1_gnn_gru_w_ih': _L1_gnn_in['gru_w_ih'], 'L1_gnn_gru_w_hh': _L1_gnn_in['gru_w_hh'], 'L1_gnn_gru_b_ih': _L1_gnn_in['gru_b_ih'], 'L1_gnn_gru_b_hh': _L1_gnn_in['gru_b_hh'], 'L2_gnn_W1': _L2_gnn_in['W1'], 'L2_gnn_a_src1': _L2_gnn_in['a_src1'], 'L2_gnn_a_dst1': _L2_gnn_in['a_dst1'], 'L2_gnn_b1': _L2_gnn_in['b1'], 'L2_gnn_W2': _L2_gnn_in['W2'], 'L2_gnn_a_src2': _L2_gnn_in['a_src2'], 'L2_gnn_a_dst2': _L2_gnn_in['a_dst2'], 'L2_gnn_b2': _L2_gnn_in['b2'], 'L2_gnn_Wf': _L2_gnn_in['Wf'], 'L2_gnn_bf': _L2_gnn_in['bf'], 'L3_gnn_W1': _L3_gnn_in['W1'], 'L3_gnn_root1': _L3_gnn_in['root1'], 'L3_gnn_b1': _L3_gnn_in['b1'], 'L3_gnn_W2': _L3_gnn_in['W2'], 'L3_gnn_root2': _L3_gnn_in['root2'], 'L3_gnn_b2': _L3_gnn_in['b2']}

def reference(x, src, dst, edge_attr_13, edge_type_8, edge_weight, L0_gnn_weight, L0_gnn_self_loop_weight, L1_gnn_fnet_w1, L1_gnn_fnet_b1, L1_gnn_fnet_w2, L1_gnn_fnet_b2, L1_gnn_gru_w_ih, L1_gnn_gru_w_hh, L1_gnn_gru_b_ih, L1_gnn_gru_b_hh, L2_gnn_W1, L2_gnn_a_src1, L2_gnn_a_dst1, L2_gnn_b1, L2_gnn_W2, L2_gnn_a_src2, L2_gnn_a_dst2, L2_gnn_b2, L2_gnn_Wf, L2_gnn_bf, L3_gnn_W1, L3_gnn_root1, L3_gnn_b1, L3_gnn_W2, L3_gnn_root2, L3_gnn_b2):
    import jax
    import jax.numpy as jnp

    def _L0_gnn_ref(x, edge_index, edge_probs, weight, self_loop_weight):
        import jax, jax.numpy as jnp
        import numpy as np
        N_NODES = 12500
        src = edge_index[0]
        dst = edge_index[1]
        messages = x[src] * edge_probs[:, None] * weight
        out = jax.ops.segment_sum(messages, dst, num_segments=N_NODES)
        out = out + x * self_loop_weight
        return jnp.clip(x + out, 0.0, 1.0)

    def _L1_gnn_ref(hx, edgefeats, edge_src, edge_dst, fnet_w1, fnet_b1, fnet_w2, fnet_b2, gru_w_ih, gru_w_hh, gru_b_ih, gru_b_hh):
        import jax, jax.numpy as jnp
        import numpy as np
        N = 6250
        E = 100000
        NC = 16
        FDIM = 13
        HID = 32
        NREPEATS = 2

        def _gru_cell(x, h, w_ih, w_hh, b_ih, b_hh):
            gi = x @ w_ih.T + b_ih
            gh = h @ w_hh.T + b_hh
            i_r, i_z, i_n = jnp.split(gi, 3, axis=1)
            h_r, h_z, h_n = jnp.split(gh, 3, axis=1)
            r = jax.nn.sigmoid(i_r + h_r)
            z = jax.nn.sigmoid(i_z + h_z)
            n = jnp.tanh(i_n + r * h_n)
            return (1.0 - z) * n + z * h
        n_nodes, nc = hx.shape
        w = jax.nn.relu(edgefeats @ fnet_w1 + fnet_b1) @ fnet_w2 + fnet_b2
        W = w.reshape(-1, nc, nc)
        deg = jax.ops.segment_sum(jnp.ones((edge_dst.shape[0],), hx.dtype), edge_dst, num_segments=n_nodes)
        inv_deg = 1.0 / jnp.maximum(deg, 1.0)
        for _ in range(NREPEATS):
            xj = hx[edge_src]
            m = jnp.einsum('ei,eio->eo', xj, W)
            agg = jax.ops.segment_sum(m, edge_dst, num_segments=n_nodes)
            agg = agg * inv_deg[:, None]
            hx = _gru_cell(agg, hx, gru_w_ih, gru_w_hh, gru_b_ih, gru_b_hh)
        return hx

    def _L2_gnn_ref(x, edge_index, W1, a_src1, a_dst1, b1, W2, a_src2, a_dst2, b2, Wf, bf):
        import jax, jax.numpy as jnp
        import numpy as np
        N = 12500
        E = 100000
        F_IN = 16
        H1, C1 = (3, 32)
        H2, C2 = (1, 32)
        NC = 16
        SLOPE = 0.2

        def _gat_layer(x, src, dst, W, a_s, a_d, b, heads, outc):
            h = (x @ W).reshape(N, heads, outc)
            alpha_s = (h * a_s).sum(-1)
            alpha_d = (h * a_d).sum(-1)
            e = jax.nn.leaky_relu(alpha_s[src] + alpha_d[dst], SLOPE)
            m = jax.ops.segment_max(e, dst, num_segments=N)
            p = jnp.exp(e - m[dst])
            z = jax.ops.segment_sum(p, dst, num_segments=N)
            alpha = p / (z[dst] + 1e-16)
            out = jax.ops.segment_sum(h[src] * alpha[:, :, None], dst, num_segments=N)
            return out.reshape(N, heads * outc) + b
        loops = jnp.arange(N, dtype=edge_index.dtype)
        src = jnp.concatenate([edge_index[0], loops])
        dst = jnp.concatenate([edge_index[1], loops])
        h = jax.nn.selu(_gat_layer(x, src, dst, W1, a_src1, a_dst1, b1, H1, C1))
        h = jax.nn.selu(_gat_layer(h, src, dst, W2, a_src2, a_dst2, b2, H2, C2))
        return h @ Wf + bf

    def _L3_gnn_ref(x, edge_index, edge_type, W1, root1, b1, W2, root2, b2):
        import jax, jax.numpy as jnp
        import numpy as np
        N_NODES = 12500
        N_EDGES = 400000
        NUM_REL = 8

        def _rgcn_layer(x, src, dst, edge_type, W, root, bias):
            out = x @ root + bias
            x_src = x[src]
            for r in range(W.shape[0]):
                mask = (edge_type == r).astype(x.dtype)
                s = jax.ops.segment_sum(x_src * mask[:, None], dst, num_segments=x.shape[0])
                cnt = jax.ops.segment_sum(mask, dst, num_segments=x.shape[0])
                agg = s / jnp.clip(cnt, 1.0)[:, None]
                out = out + agg @ W[r]
            return out
        src, dst = (edge_index[0], edge_index[1])
        h = _rgcn_layer(x, src, dst, edge_type, W1, root1, b1)
        h = jax.nn.relu(h)
        h = _rgcn_layer(h, src, dst, edge_type, W2, root2, b2)
        return h
    edge_index = jnp.stack([src, dst])
    x = _layernorm(x + _L0_gnn_ref(x, edge_index, edge_weight, L0_gnn_weight, L0_gnn_self_loop_weight), axis=-1)
    x = _layernorm(x + _L1_gnn_ref(x, edge_attr_13, src, dst, L1_gnn_fnet_w1, L1_gnn_fnet_b1, L1_gnn_fnet_w2, L1_gnn_fnet_b2, L1_gnn_gru_w_ih, L1_gnn_gru_w_hh, L1_gnn_gru_b_ih, L1_gnn_gru_b_hh), axis=-1)
    x = _layernorm(x + _L2_gnn_ref(x, edge_index, L2_gnn_W1, L2_gnn_a_src1, L2_gnn_a_dst1, L2_gnn_b1, L2_gnn_W2, L2_gnn_a_src2, L2_gnn_a_dst2, L2_gnn_b2, L2_gnn_Wf, L2_gnn_bf), axis=-1)
    x = _layernorm(x + _L3_gnn_ref(x, edge_index, edge_type_8, L3_gnn_W1, L3_gnn_root1, L3_gnn_b1, L3_gnn_W2, L3_gnn_root2, L3_gnn_b2), axis=-1)
    return x

_drawn_inputs = setup_inputs


def setup_inputs(seed=0):
    import zlib

    import numpy as np

    out = dict(_drawn_inputs(seed))
    spreads = {'L0_gnn_weight': (1.0, 0.2),
     'L1_gnn_fnet_b1': (0.0, 2.0),
     'L1_gnn_fnet_b2': (0.0, 0.34),
     'L1_gnn_gru_b_ih': (0.0, 0.1),
     'L1_gnn_gru_b_hh': (0.0, 0.1),
     'L2_gnn_b1': (0.0, 0.1),
     'L2_gnn_b2': (0.0, 0.1),
     'L2_gnn_bf': (0.0, 0.1),
     'L3_gnn_b1': (0.0, 0.1),
     'L3_gnn_b2': (0.0, 0.1)}
    factors = {'edge_attr_13': 4.464,
     'L1_gnn_fnet_w1': 4.505,
     'L2_gnn_a_dst1': 64.0,
     'L2_gnn_a_src2': 50.325,
     'L2_gnn_a_dst2': 64.0,
     'L2_gnn_a_src1': 2.959}
    for name, (base, spread) in spreads.items():
        noise = np.random.default_rng([zlib.crc32(name.encode()), seed]).standard_normal(out[name].shape)
        drawn = base * np.exp(spread * noise) if base else spread * noise
        out[name] = jnp.asarray(drawn.astype(out[name].dtype))
    for name, factor in factors.items():
        out[name] = (out[name] * factor).astype(out[name].dtype)
    return out
```

```python
from contextlib import ExitStack

import concourse.bass as bass
from concourse import mybir

F32 = mybir.dt.float32
I32 = mybir.dt.int32
ALU = mybir.AluOpType
ACT = mybir.ActivationFunctionType
AX = mybir.AxisListType

N, E = 12500, 412500
P = 128
NJ = 98
NP = P * NJ
T = 3224
EP = P * T
TC = 52
NCH = T // TC
NS, SW = 62, 52
BIG = 1.0e30
SELU_A, SELU_S = 1.6732632423543772, 1.0507009873554805
CI, CB, C8, CN = 0, 128, 129, 137
CW = CN + NJ


class Queue:

    def __init__(self, eng, sem):
        self.eng, self.sem, self.n, self.seen = eng, sem, 0, {}

    def wait(self, *marks):
        for m in marks:
            if m is not None and self.seen.get(id(m[0]), 0) < m[1]:
                self.eng.wait_ge(m[0], m[1])
                self.seen[id(m[0])] = m[1]

    def did(self, ins):
        ins.then_inc(self.sem, 1)
        self.n += 1
        return self.sem, self.n

    def settle(self):
        self.wait((self.sem, self.n) if self.n else None)


class Chan:

    def __init__(self, sem):
        self.sem, self.n = sem, 0

    def did(self, ins):
        ins.then_inc(self.sem, 16)
        self.n += 16
        return self.sem, self.n


def gnn_program(nc, x, src, dst, prv, attrT, typ, ew, consts, l0w, l0s, w1, b1, w2a, gw, l2w, l2blk, as1, ad1, w2s, as2, ad2,
                b2, wf, l3w1, root1, l3w2, root2, out):
    with ExitStack() as ctx:
        def sb(name, shape, dt=F32):
            return ctx.enter_context(nc.sbuf_tensor(name, shape, dt))

        def sem(name):
            return ctx.enter_context(nc.semaphore(name))

        def dram(name, shape, dt=F32):
            return nc.dram_tensor(name, shape, dt).ap()

        V = Queue(nc.vector, sem("s_vec"))
        A = Queue(nc.scalar, sem("s_act"))
        M = Queue(nc.tensor, sem("s_pe"))
        G = Queue(nc.gpsimd, sem("s_pool"))
        S = Queue(nc.sync, None)
        v, a, pe, pool, sp = nc.vector, nc.scalar, nc.tensor, nc.gpsimd, nc.sync

        srci = sb("srci", [P, T], I32)
        typi = sb("typi", [P, T], I32)
        same = sb("same", [P, T])
        wE = sb("wE", [P, T])
        dsti = wE[:, :].bitcast(I32)
        gb = sb("gb", [P, 2 * TC * 36])
        prod = sb("prod", [P, 2944])
        Sb = sb("Sb", [P, 2 * TC * 56])
        ext = sb("ext", [P, NJ * 54])
        exti = ext[:, :].bitcast(I32)
        arena = sb("arena", [P, NJ * 48])
        xcur = sb("xcur", [P, NJ * 16])
        hcur = sb("hcur", [P, NJ * 16])
        XT = sb("XT", [P, NJ * 12])
        hid = sb("hid", [P, 2 * 512])
        xT16 = sb("xT16", [P, 2 * 512])
        xT32 = sb("xT32", [P, 2 * 512])
        xT48 = sb("xT48", [P, 2 * 512])
        ewc = sb("ewc", [P, 2 * TC])
        sub = sb("sub", [P, TC * 22])
        cst = sb("cst", [P, CW])
        zero = sb("zero", [P, TC * 12])
        w1s = sb("w1s", [13, 32])
        b1s = sb("b1s", [32, 1])
        w2as = sb("w2as", [33, 256])
        gws = sb("gws", [34, 64])
        l0wb = sb("l0wb", [P, 16])
        l0sb = sb("l0sb", [P, 1])
        l2ws = sb("l2ws", [16, 96])
        l2bs = sb("l2bs", [49, 96])
        avec = sb("avec", [16, 2 * 96])
        a2vec = sb("a2vec", [96, 64])
        vtmp = sb("vtmp", [96, 96])
        v1 = sb("v1", [16, 6])
        w2x = sb("w2x", [96, 34])
        b2b = sb("b2b", [P, 32])
        wfs = sb("wfs", [33, 16])
        l3w1s = sb("l3w1s", [16, 256])
        r1s = sb("r1s", [17, 32])
        l3w2s = sb("l3w2s", [32, 128])
        r2s = sb("r2s", [33, 16])
        endi = sb("endi", [P, NJ], I32)
        stai = sb("stai", [P, NJ], I32)
        fndi = sb("fndi", [P, NJ], I32)
        mask = sb("mask", [P, NJ])
        nmask = sb("nmask", [P, NJ])
        invdeg = sb("invdeg", [P, NJ])
        nt = sb("nt", [P, 4 * NJ])
        pcol = sb("pcol", [P, 8])
        pcoi = sb("pcoi", [P, 2], I32)
        contT = sb("contT", [64, P])
        nbT = sb("nbT", [4, P])
        fx = sb("fx", [P, 640])
        fC = sb("fC", [P, 129])
        fM = sb("fM", [4, 129])
        x0 = sb("x0", [P, 24])

        psA = [ctx.enter_context(nc.psum_tensor(f"psA{i}", [P, 512], F32)) for i in range(2)]
        psB = [ctx.enter_context(nc.psum_tensor(f"psB{i}", [P, 1024], F32)) for i in range(3)]
        freeA, freeB = [None, None], [None, None, None]

        first_d = dram("first_d", [P, 1], I32)
        samp_d = dram("samp_d", [P, NS], I32)
        cont_d = dram("cont_d", [P, 1])
        end_d = dram("end_d", [NP + 1])
        S0 = dram("S0", [EP, 24])
        S1 = [dram("S1a", [EP, 16]), dram("S1b", [EP, 16])]
        S2a = dram("S2a", [EP, 54])
        S2b = dram("S2b", [EP, 34])
        S3a = dram("S3a", [EP, 32])
        S3b = dram("S3b", [EP, 16])
        tab1 = [dram("tab1a", [NP, 16]), dram("tab1b", [NP, 16])]
        tab2a = dram("tab2a", [NP, 20])
        tab2b = dram("tab2b", [NP, 36])
        tab3a = dram("tab3a", [NP * 8, 32])
        tab3b = dram("tab3b", [NP * 8, 16])
        xn2a = dram("xn2a", [NP, 12])
        xn2b = dram("xn2b", [NP, 1])
        xe2a = dram("xe2a", [EP, 12])
        xe2b = dram("xe2b", [EP, 1])

        c_src, c_dst, c_prv, c_typ, c_w = (Chan(sem(f"c_{n}")) for n in ("src", "dst", "prv", "typ", "w"))
        c_ew = [Chan(sem(f"c_ew{i}")) for i in range(2)]
        c_att = [Chan(sem(f"c_att{i}")) for i in range(3)]
        c_out = [Chan(sem(f"c_out{i}")) for i in range(2)]
        c_xe = [Chan(sem(f"c_xe{i}")) for i in range(2)]
        c_y = [Chan(sem(f"c_y{i}")) for i in range(2)]
        c_fix, c_ext, c_tab, c_set, c_zero, c_sct, c_fin = (Chan(sem(f"c_{n}")) for n in
                                                            ("fix", "ext", "tab", "set", "zero", "sct", "fin"))
        c_g = [[Chan(sem(f"c_g{k}_{i}")) for i in range(2)] for k in range(7)]

        ident = cst[:, CI:CI + P]
        pbase = cst[:, CB:CB + 1]
        io8 = cst[:, C8:C8 + 8]
        nid = cst[:, CN:CN + NJ]

        def rows(d, f):
            return d.rearrange("(p t) f -> p t f", p=P)

        def v3(t, f):
            return t.rearrange("p (t f) -> p t f", f=f)

        def bc(ap, axis, n):
            ap = ap.unsqueeze(axis)
            shape = list(ap.shape)
            shape[axis] = n
            return ap.to_broadcast(shape)

        def vv(ins):
            return V.did(ins)

        m_src = c_src.did(sp.dma_start(srci[:, :], src))
        m_dst = c_dst.did(sp.dma_start(dsti, dst))
        m_prv = c_prv.did(sp.dma_start(typi[:, :], prv))
        for t, d in ((cst[:, :], consts), (w1s[:, :], w1), (b1s[:, :], b1), (w2as[:, :], w2a), (gws[:, :], gw),
                     (l0wb[:, :], l0w.partition_broadcast(P)), (l0sb[:, :], l0s.partition_broadcast(P)),
                     (l2ws[:, :], l2w), (l2bs[:, :], l2blk),
                     (avec[:, 0:96], as1.partition_broadcast(16)), (avec[:, 96:192], ad1.partition_broadcast(16)),
                     (a2vec[:, 0:32], as2.partition_broadcast(96)), (a2vec[:, 32:64], ad2.partition_broadcast(96)),
                     (w2x[:, 0:32], w2s), (b2b[:, :], b2.partition_broadcast(P)), (wfs[:, :], wf),
                     (l3w1s[:, :], l3w1), (r1s[:, :], root1), (l3w2s[:, :], l3w2), (r2s[:, :], root2),
                     (xcur[:, :], x.rearrange("(p j) f -> p (j f)", p=P))):
            m_w = c_w.did(a.dma_start(t, d))

        m_z = vv(v.memset(zero[:, :], 0.0))
        for t in (xT16, xT32, xT48):
            vv(v.memset(t[:, :], 1.0))
        vv(v.memset(hid[:, :], 1.0))
        vv(v.memset(fC[:, :], 0.0))
        vv(v.memset(fM[:, :], -BIG))
        vv(v.memset(pcol[:, 7:8], -1.0))
        V.wait(m_dst, m_prv, m_w)
        m_same = vv(v.tensor_tensor(same[:, :], dsti, typi[:, :], ALU.is_equal))
        samp = hcur[:, 0:NS].bitcast(I32)
        m_samp = vv(v.tensor_copy(samp, wE[:, 0:T:SW].bitcast(I32)))
        firstf, contc, cntf, fixf = (pcol[:, i:i + 1] for i in range(4))
        vv(v.tensor_copy(firstf, dsti[:, 0:1]))
        vv(v.tensor_copy(pcoi[:, 0:1], dsti[:, 0:1]))
        V.settle()
        vv(v.tensor_tensor(contc, firstf, dsti[:, T - 1:T], ALU.is_equal))
        junk = Sb[:, 0:T]
        vv(v.tensor_scalar(junk, dsti, firstf, None, ALU.is_equal))
        V.settle()
        samep = same[:, 0:1]
        vv(v.tensor_tensor(contc, contc, samep, ALU.mult))
        vv(v.tensor_reduce(cntf, junk, AX.X, ALU.add))
        V.settle()
        vv(v.scalar_tensor_tensor(fixf, cntf, -1.0, pbase, ALU.add, ALU.add))
        vv(v.tensor_scalar(pcol[:, 4:5], samep, -1.0, BIG, ALU.add, ALU.mult))
        V.settle()
        m_fix = vv(v.tensor_copy(pcoi[:, 1:2], fixf))
        nsamep = pcol[:, 4:5]
        firsti, fixi = pcoi[:, 0:1], pcoi[:, 1:2]
        S.wait(m_fix, m_samp)
        c_set.did(sp.dma_start(samp_d, samp))
        c_set.did(sp.dma_start(cont_d, contc))
        m_s1 = c_set.did(sp.dma_start(first_d, firsti))
        c_zero.did(sp.dma_start(end_d[0:1].unsqueeze(0), pcol[0:1, 7:8]))
        m_typ = None

        S.wait(m_s1, m_z)
        fr = fx[:, 0:P].bitcast(I32)
        c_set.did(sp.dma_start(fr, first_d.rearrange("p o -> o p")[0].partition_broadcast(P)))
        m_s2 = c_set.did(sp.dma_start(contT[:, :], cont_d.rearrange("p o -> o p")[0].partition_broadcast(64)))
        S.wait(m_same)
        m_typ = c_typ.did(sp.dma_start(typi[:, :], typ))
        for k in range(NCH):
            c_zero.did(sp.dma_start(rows(xe2a, 12)[:, k * TC:(k + 1) * TC, :], v3(zero[:, :], 12)))
        xe2bv = xe2b.rearrange("(p t) f -> p (t f)", p=P)
        for k in range(0, T, TC * 12):
            n = min(TC * 12, T - k)
            m_zero = c_zero.did(sp.dma_start(xe2bv[:, k:k + n], zero[:, 0:n]))

        V.wait(m_s2)
        vv(v.tensor_scalar(nbT[:, :], contT[0:4, :], -1.0, BIG, ALU.add, ALU.mult))
        rank, blk, cum = nt[:, 0:NJ], nt[:, NJ:2 * NJ], nt[:, 2 * NJ:3 * NJ]

        def count_le(dest, j0, nj, width, vals):
            cmp = v3(arena[:, 0:nj * width], width)
            V.settle()
            vv(v.tensor_tensor(cmp, vals, bc(nid[:, j0:j0 + nj], 2, width), ALU.is_le))
            V.settle()
            return vv(v.tensor_reduce(dest[:, j0:j0 + nj], cmp, AX.X, ALU.add))

        def search1():
            for j0 in range(0, NJ, 14):
                count_le(rank, j0, 14, P, bc(fr, 1, 14))
            V.settle()
            vv(v.tensor_scalar(rank, rank, -1.0, 0.0, ALU.add, ALU.max))
            V.settle()
            return vv(v.tensor_copy(fndi[:, :], rank))

        HALF = NJ // 2

        def rows_of(table, width, half, ready):
            G.wait(*ready)
            for j in range(HALF):
                m = c_ext.did(pool.indirect_dma_start(
                    exti[:, j * width:(j + 1) * width], None, table,
                    bass.IndirectOffsetOnAxis(ap=fndi[:, half * HALF + j:half * HALF + j + 1], axis=0)))
            return m

        def count_rows(dest, width, half, arrived):
            V.wait(arrived)
            for j in range(0, HALF, 7):
                m = count_le(dest, half * HALF + j, 7, width, v3(exti[:, j * width:(j + 7) * width], width))
            return m

        def search_blocks(half_marks):
            V.settle()
            vv(v.scalar_tensor_tensor(blk, rank, float(NS), blk, ALU.mult, ALU.add))
            V.settle()
            vv(v.tensor_scalar(blk, blk, -1.0, 0.0, ALU.add, ALU.max))
            V.settle()
            return vv(v.tensor_copy(fndi[:, :], blk))

        def search_ends():
            V.settle()
            vv(v.scalar_tensor_tensor(cum, blk, float(SW), cum, ALU.mult, ALU.add))
            V.settle()
            e = vv(v.tensor_scalar(cum, cum, -1.0, None, ALU.add))
            S.wait(e)
            m = c_set.did(sp.dma_start(end_d[1:NP + 1].rearrange("(p j) -> p j", p=P), cum))
            S.wait(m, m_zero)
            m = c_set.did(sp.dma_start(nt[:, 3 * NJ:4 * NJ], end_d[0:NP].rearrange("(p j) -> p j", p=P)))
            V.wait(m)
            before = nt[:, 3 * NJ:4 * NJ]
            vv(v.tensor_tensor(mask[:, :], cum, before, ALU.subtract))
            vv(v.tensor_scalar(rank, cum, 0.0, None, ALU.max))
            V.settle()
            vv(v.tensor_scalar(mask[:, :], mask[:, :], 1.0, None, ALU.min))
            vv(v.tensor_copy(endi[:, :], rank))
            V.settle()
            vv(v.tensor_scalar(blk, mask[:, :], -1.0e6, 1.0e6 + 1.0, ALU.mult, ALU.add))
            vv(v.tensor_scalar(nmask[:, :], mask[:, :], -1.0, BIG, ALU.add, ALU.mult))
            V.settle()
            vv(v.tensor_tensor(blk, blk, before, ALU.add))
            V.settle()
            return vv(v.tensor_copy(stai[:, :], blk))

        free_g = [None, None]
        sent = [None, None]

        def gather(k, table, idx, width, c, ready):
            s = c % 2
            G.wait(free_g[s], *ready)
            for i in range(TC):
                t = c * TC + i
                o = s * TC * 36 + i * width
                m = c_g[k][s].did(pool.indirect_dma_start(
                    gb[:, o:o + width], None, table, bass.IndirectOffsetOnAxis(ap=idx[:, t:t + 1], axis=0)))
            return m

        def got(c, width):
            o = (c % 2) * TC * 36
            return v3(gb[:, o:o + TC * width], width)

        def state(c, f):
            o = (c % 2) * TC * 56
            return v3(Sb[:, o:o + TC * f], f)

        def put(c, f, dest, done):
            S.wait(done)
            sent[c % 2] = c_out[c % 2].did(sp.dma_start(rows(dest, f)[:, c * TC:(c + 1) * TC, :], state(c, f)))

        def span(c):
            return slice(c * TC, (c + 1) * TC)

        def sums(c, f, data, decay=None, cols=None):
            V.wait(sent[c % 2])
            V.settle()
            now, old = state(c, f), state(c + 1, f)
            for k in (cols or range(f)):
                init = old[:, TC - 1, k:k + 1] if c else 0.0
                d0 = same[:, span(c)] if decay is None else decay(k)
                m = vv(v.tensor_tensor_scan(now[:, :, k], d0, data(k), init, ALU.mult, ALU.add))
            return m

        def message_pass(k, table, idx, width, f, dest, messages, ready, hooks=None):
            arrived = {}
            for c in range(2):
                arrived[c] = gather(k, table, idx, width, c, ready)
            for c in range(NCH):
                V.wait(arrived[c])
                done = messages(c)
                put(c, f, dest, done)
                if c + 2 < NCH:
                    arrived[c + 2] = gather(k, table, idx, width, c + 2, ready)
                if hooks and c in hooks:
                    hooks[c]()

        def turned(dst_ps, col, inp, width):
            return M.did(pe.transpose(dst_ps[0:width, col:col + P], inp, ident))

        def to_rows(f, final, out_cols):
            M.wait(freeA[0], (V.sem, V.n))
            m = turned(psA[0], 0, final, f)
            V.wait(m)
            freeA[0] = vv(v.tensor_copy(fx[0:f, out_cols:out_cols + P], psA[0][0:f, 0:P]))

        def to_cols(f, rows_ap, dest):
            M.wait(freeA[1], (V.sem, V.n))
            m = M.did(pe.transpose(psA[1][0:P, 0:f], rows_ap, ident[0:f, 0:f]))
            V.wait(m)
            freeA[1] = vv(v.tensor_copy(dest, psA[1][0:P, 0:f]))

        W0 = 256

        def fix_gather(f, dest):
            row = fx[:, W0:W0 + f]
            G.wait(sent[0], sent[1], m_fix, (V.sem, V.n))
            return c_fix.did(pool.indirect_dma_start(row, None, dest, bass.IndirectOffsetOnAxis(ap=fixi, axis=0)))

        def fix_scatter(f, dest):
            G.wait((V.sem, V.n))
            return c_fix.did(pool.indirect_dma_start(dest, bass.IndirectOffsetOnAxis(ap=fixi, axis=0),
                                                     fx[:, W0:W0 + f], None))

        def fix_sums(f, dest):
            m = fix_gather(f, dest)
            final = state(NCH - 1, f)[:, TC - 1, :]
            to_rows(f, final, 128)
            V.settle()
            vv(v.tensor_tensor_scan(fC[0:f, 1:129], contT[0:f, :], fx[0:f, 128:256], 0.0, ALU.mult, ALU.add))
            V.settle()
            carry = fx[:, W0 + 64:W0 + 64 + f]
            to_cols(f, fC[0:f, 0:P], carry)
            V.wait(m)
            V.settle()
            vv(v.scalar_tensor_tensor(fx[:, W0:W0 + f], carry, samep, fx[:, W0:W0 + f], ALU.mult, ALU.add))
            return fix_scatter(f, dest)

        def fix_softmax(H, D, dest):
            f, w = H * (2 + D), 1 + D
            m = fix_gather(f, dest)
            final = state(NCH - 1, f)[:, TC - 1, :]
            mrow, arow = fx[:, W0:W0 + H], fx[:, W0 + H:W0 + f]
            o = W0 + 64
            mx, mp, f1, f0, bb = (fx[:, o + 4 * i:o + 4 * i + H] for i in range(5))
            d0, d1 = fx[:, o + 32:o + 32 + H * w], fx[:, o + 96:o + 96 + H * w]
            cprev = fx[:, o + 160:o + 160 + H * w]
            to_rows(H, final[:, 0:H], 128)
            V.settle()
            vv(v.tensor_tensor_scan(fM[0:H, 1:129], nbT[0:H, :], fx[0:H, 128:256], -BIG, ALU.add, ALU.max))
            V.settle()
            to_cols(H, fM[0:H, 1:129], mx)
            V.settle()
            to_cols(H, fM[0:H, 0:P], mp)
            V.settle()
            vv(v.tensor_tensor(f1, final[:, 0:H], mx, ALU.subtract))
            vv(v.tensor_tensor(f0, mp, mx, ALU.subtract))
            V.settle()
            e = vv(v.tensor_scalar(f0, f0, 0.0, None, ALU.min))
            A.wait(e)
            A.did(a.activation(f1, f1, ACT.Exp))
            e = A.did(a.activation(f0, f0, ACT.Exp))
            V.wait(e)
            vv(v.tensor_scalar(f0, f0, contc, None, ALU.mult))
            V.settle()
            vv(v.tensor_tensor(v3(d1, w), v3(final[:, H:f], w), bc(f1, 2, w), ALU.mult))
            vv(v.tensor_copy(v3(d0, w), bc(f0, 2, w)))
            V.settle()
            to_rows(H * w, d0, 0)
            to_rows(H * w, d1, 128)
            V.settle()
            vv(v.tensor_tensor_scan(fC[0:H * w, 1:129], fx[0:H * w, 0:P], fx[0:H * w, 128:256], 0.0, ALU.mult, ALU.add))
            V.settle()
            to_cols(H * w, fC[0:H * w, 0:P], cprev)
            V.wait(m)
            V.settle()
            vv(v.tensor_scalar(mp, mp, nsamep, None, ALU.add))
            V.settle()
            vv(v.tensor_tensor(mx, mrow, mp, ALU.max))
            V.settle()
            vv(v.tensor_tensor(f1, mrow, mx, ALU.subtract))
            vv(v.tensor_tensor(bb, mp, mx, ALU.subtract))
            V.settle()
            vv(v.tensor_copy(mrow, mx))
            A.wait((V.sem, V.n))
            A.did(a.activation(f1, f1, ACT.Exp))
            e = A.did(a.activation(bb, bb, ACT.Exp))
            V.wait(e)
            vv(v.tensor_scalar(bb, bb, samep, None, ALU.mult))
            vv(v.tensor_tensor(v3(arow, w), v3(arow, w), bc(f1, 2, w), ALU.mult))
            V.settle()
            vv(v.tensor_tensor(v3(cprev, w), v3(cprev, w), bc(bb, 2, w), ALU.mult))
            V.settle()
            vv(v.tensor_tensor(arow, arow, cprev, ALU.add))
            return fix_scatter(f, dest)

        def node_rows(f, dest, fixed):
            G.wait(fixed, (V.sem, V.n), (M.sem, M.n))
            for j in range(NJ):
                m = c_ext.did(pool.indirect_dma_start(
                    ext[:, j * f:(j + 1) * f], None, dest,
                    bass.IndirectOffsetOnAxis(ap=endi[:, j:j + 1], axis=0)))
            V.wait(m)
            return v3(ext[:, 0:NJ * f], f)

        def node_product(inp, K, ones, xT, W, width, evac):
            per = 512 // width
            n = min(4, 2 * per)
            groups = [(j, min(n, NJ - j)) for j in range(0, NJ, n)]
            M.wait((V.sem, V.n), (A.sem, A.n))
            copied, used = {}, [None, None]
            for g in range(len(groups) + 1):
                if g < len(groups):
                    j0, cnt = groups[g]
                    M.wait(freeA[g % 2])
                    for i in range(cnt):
                        m = turned(psA[g % 2], i * P, inp(j0 + i), K)
                    A.wait(m, used[g % 2])
                    o = (g % 2) * 512
                    copied[g] = A.did(a.activation(xT[0:K, o:o + cnt * P], psA[g % 2][0:K, 0:cnt * P], ACT.Copy))
                    freeA[g % 2] = copied[g]
                if g > 0:
                    j0, cnt = groups[g - 1]
                    b = (g - 1) % 3
                    M.wait(copied[g - 1], freeB[b])
                    o = ((g - 1) % 2) * 512
                    for i in range(cnt):
                        at = (i // per) * 512 + (i % per) * width
                        m = M.did(pe.matmul(psB[b][:, at:at + width], xT[0:K + ones, o + i * P:o + (i + 1) * P], W,
                                            start=True, stop=True))
                    used[(g - 1) % 2] = m
                    for i in range(0, cnt, per):
                        q = min(per, cnt - i)
                        at = (i // per) * 512
                        freeB[b] = evac(j0 + i, q, psB[b][:, at:at + q * width].rearrange("p (j w) -> p j w", w=width), m)

        def layernorm(dest, r):
            d = v3(Sb[:, 0:NJ * 16], 16)
            q = v3(Sb[:, NJ * 16:NJ * 32], 16)
            s, t = nt[:, 0:NJ], nt[:, NJ:2 * NJ]
            V.wait(sent[0], sent[1])
            V.settle()
            vv(v.tensor_reduce(s, r, AX.X, ALU.add))
            V.settle()
            vv(v.tensor_scalar(s, s, 1.0 / 16, None, ALU.mult))
            V.settle()
            vv(v.tensor_tensor(d, r, bc(s, 2, 16), ALU.subtract))
            V.settle()
            vv(v.tensor_tensor(q, d, d, ALU.mult))
            V.settle()
            vv(v.tensor_reduce(t, q, AX.X, ALU.add))
            V.settle()
            e = vv(v.tensor_scalar(t, t, 1.0 / 16, 1.0e-5, ALU.mult, ALU.add))
            A.wait(e)
            e = A.did(a.activation(s, t, ACT.Sqrt))
            V.wait(e)
            vv(v.reciprocal(t, s))
            V.settle()
            vv(v.tensor_tensor(dest, d, bc(t, 2, 16), ALU.mult))
            V.settle()

        def save(table, tile, f):
            S.wait((V.sem, V.n), (A.sem, A.n))
            return c_tab.did(sp.dma_start(table.rearrange("(p j) f -> p (j f)", p=P), tile[:, 0:NJ * f]))

        xv, hv = v3(xcur[:, :], 16), v3(hcur[:, :], 16)
        work = v3(prod[:, 0:NJ * 16], 16)

        m_fnd = search1()

        def messages0(c):
            s = c % 2
            V.wait(m_ew[s], m_typ)
            V.settle()
            pr = v3(prod[:, 0:TC * 24], 24)
            vv(v.tensor_tensor(pr[:, :, 16:24], bc(typi[:, span(c)], 2, 8), bc(io8, 1, TC), ALU.is_equal))
            free_g[s] = vv(v.tensor_tensor(pr[:, :, 0:16], got(c, 16), bc(ewc[:, s * TC:(s + 1) * TC], 2, 16), ALU.mult))
            if c + 2 < NCH:
                S.wait(free_g[s])
                m_ew[s] = c_ew[s].did(sp.dma_start(ewc[:, s * TC:(s + 1) * TC], ew[:, span(c + 2)]))
            return sums(c, 24, lambda k: pr[:, :, k])

        m_ew = [c_ew[i].did(sp.dma_start(ewc[:, i * TC:(i + 1) * TC], ew[:, span(i)])) for i in range(2)]
        st = {}

        def hook(fn, *args):
            return lambda: st.__setitem__(fn.__name__ + str(len(st)), fn(*args))

        def h1():
            st["a"] = rows_of(samp_d, NS, 0, (m_fnd, m_s1))

        def h2():
            st["a"] = count_rows(blk, NS, 0, st["a"])

        def h3():
            st["b"] = rows_of(samp_d, NS, 1, (st["a"],))

        def h4():
            st["b"] = search_blocks(count_rows(blk, NS, 1, st["b"]))

        def h5():
            st["a"] = rows_of(dst.rearrange("p (s w) -> (p s) w", w=SW), SW, 0, (st["b"],))

        def h6():
            st["a"] = count_rows(cum, SW, 0, st["a"])

        def h7():
            st["b"] = rows_of(dst.rearrange("p (s w) -> (p s) w", w=SW), SW, 1, (st["a"],))

        def h8():
            count_rows(cum, SW, 1, st["b"])
            st["e"] = search_ends()

        message_pass(0, x, srci, 16, 24, S0, messages0, (m_src,),
                     {4 + 2 * i: h for i, h in enumerate((h1, h2, h3, h4, h5, h6, h7, h8))})
        ends = st["e"]
        G.wait(ends)
        ex = node_rows(24, S0, fix_sums(24, S0))
        vv(v.tensor_tensor(ex, ex, bc(mask[:, :], 2, 24), ALU.mult))
        V.settle()
        vv(v.tensor_reduce(invdeg[:, :], ex[:, :, 16:24], AX.X, ALU.add))
        xt12 = v3(XT[:, :], 12)
        vv(v.memset(XT[:, :], 0.0))
        vv(v.tensor_tensor(work, ex[:, :, 0:16], bc(l0wb[:, :], 1, NJ), ALU.mult))
        V.settle()
        vv(v.tensor_scalar(invdeg[:, :], invdeg[:, :], 1.0, None, ALU.max))
        vv(v.tensor_scalar(xt12[:, :, 4:12], ex[:, :, 16:24], 1.0, None, ALU.max))
        vv(v.scalar_tensor_tensor(prod[:, 0:NJ * 16], xcur[:, :], l0sb[:, 0:1], prod[:, 0:NJ * 16], ALU.mult, ALU.add))
        V.settle()
        vv(v.reciprocal(invdeg[:, :], invdeg[:, :]))
        vv(v.reciprocal(xt12[:, :, 4:12], xt12[:, :, 4:12]))
        vv(v.tensor_tensor(work, work, xv, ALU.add))
        V.settle()
        vv(v.tensor_scalar(work, work, 0.0, 1.0, ALU.max, ALU.min))
        V.settle()
        vv(v.tensor_tensor(work, work, xv, ALU.add))
        layernorm(xv, work)
        ready = save(tab1[0], xcur, 16)
        vv(v.tensor_copy(hcur[:, :], xcur[:, :]))

        NG = T // 4
        AT = 8
        atts = [ext[0:13, i * AT * P:(i + 1) * AT * P] for i in range(3)]
        pr1 = [prod[:, i * 1024:(i + 1) * 1024] for i in range(2)]
        msg = v3(prod[:, 2048:2048 + TC * 16], 16)

        for rep in range(2):
            M.wait((V.sem, V.n))
            m_att, used_att = {}, {}
            hid_ready, hid_used, w_ready, w_free = {}, {}, {}, {}

            def att_load(q):
                S.wait(used_att.get(q - 3), (V.sem, V.n) if q == 0 else None)
                m_att[q] = c_att[q % 3].did(sp.dma_start(v3(atts[q % 3], P), attrT[:, q * AT:(q + 1) * AT, :]))

            def hidden(k):
                q, o = k // 2, (k % 2) * 512
                M.wait(m_att[q], freeA[k % 2])
                m = M.did(pe.matmul(psA[k % 2][0:32, :], w1s[:, :], atts[q % 3][:, o:o + 512], start=True, stop=True))
                if k % 2:
                    used_att[q] = m
                A.wait(m, hid_used.get(k - 2))
                o = (k % 2) * 512
                hid_ready[k] = freeA[k % 2] = A.did(a.activation(hid[0:32, o:o + 512], psA[k % 2][0:32, :], ACT.Relu,
                                                                 bias=b1s[:, 0:1]))

            def weights(k):
                M.wait(hid_ready[k], freeB[k % 3])
                for i in range(4):
                    o = (k % 2) * 512 + i * P
                    m = M.did(pe.matmul(psB[k % 3][:, i * 256:(i + 1) * 256], hid[0:33, o:o + P], w2as[:, :],
                                        start=True, stop=True))
                hid_used[k] = w_ready[k] = m

            def step(k):
                if k + 1 < NG:
                    if (k + 1) % 2 == 0 and (k + 1) // 2 + 2 < T // AT:
                        att_load((k + 1) // 2 + 2)
                    hidden(k + 1)
                weights(k)

            def messages1(c):
                gv = got(c, 16)
                base = c * TC // 4
                reduced = [None, None]
                V.settle()

                def reduce(i):
                    V.wait(multiplied[i])
                    reduced[i % 2] = vv(v.tensor_reduce(msg[:, 4 * i:4 * i + 4, :], pr1[i % 2].rearrange(
                        "p (t o i) -> p t o i", t=4, o=16), AX.X, ALU.add))

                multiplied = {}
                for i in range(TC // 4):
                    k = base + i
                    step(k)
                    V.wait(w_ready[k], reduced[i % 2])
                    multiplied[i] = vv(v.tensor_tensor(
                        pr1[i % 2].rearrange("p (t o i) -> p t o i", t=4, o=16),
                        psB[k % 3][:, :].rearrange("p (t o i) -> p t o i", t=4, o=16),
                        bc(gv[:, 4 * i:4 * i + 4, :], 2, 16), ALU.mult))
                    freeB[k % 3] = multiplied[i]
                    if i:
                        reduce(i - 1)
                reduce(TC // 4 - 1)
                free_g[c % 2] = multiplied[TC // 4 - 1]
                return sums(c, 16, lambda k: msg[:, :, k])

            for q in range(3):
                att_load(q)
            hidden(0)
            message_pass(1 + rep, tab1[rep], srci, 16, 16, S1[rep], messages1, (ready,))
            ex = node_rows(16, S1[rep], fix_sums(16, S1[rep]))
            cat = v3(gb[:, 0:NJ * 32], 32)
            vv(v.tensor_tensor(cat[:, :, 0:16], ex, bc(mask[:, :], 2, 16), ALU.mult))
            vv(v.tensor_copy(cat[:, :, 16:32], hv))
            V.settle()
            vv(v.tensor_tensor(cat[:, :, 0:16], cat[:, :, 0:16], bc(invdeg[:, :], 2, 16), ALU.mult))
            rz = v3(arena[:, 0:NJ * 32], 32)
            nn = v3(arena[:, NJ * 32:NJ * 48], 16)

            def gru_evac(j0, q, ps, m):
                A.wait(m)
                e = A.did(a.activation(rz[:, j0:j0 + q, :], ps[:, :, 0:32], ACT.Sigmoid))
                V.wait(e)
                vv(v.tensor_tensor(nn[:, j0:j0 + q, :], rz[:, j0:j0 + q, 0:16], ps[:, :, 48:64], ALU.mult))
                V.settle()
                return vv(v.tensor_tensor(nn[:, j0:j0 + q, :], nn[:, j0:j0 + q, :], ps[:, :, 32:48], ALU.add))

            node_product(lambda j: cat[:, j, :], 32, 2, xT32, gws[:, :], 64, gru_evac)
            A.wait((V.sem, V.n))
            e = A.did(a.activation(nn, nn, ACT.Tanh))
            V.wait(e)
            vv(v.tensor_tensor(hv, hv, nn, ALU.subtract))
            V.settle()
            vv(v.tensor_tensor(hv, hv, rz[:, :, 16:32], ALU.mult))
            V.settle()
            vv(v.tensor_tensor(hv, hv, nn, ALU.add))
            if rep == 0:
                ready = save(tab1[1], hcur, 16)
        V.settle()
        vv(v.tensor_tensor(work, xv, hv, ALU.add))
        layernorm(xv, work)

        for i in range(2):
            vv(v.tensor_tensor(vtmp[0:16, :], l2ws[:, :], avec[:, 96 * i:96 * i + 96], ALU.mult))
            V.settle()
            vv(v.tensor_reduce(v1[:, 3 * i:3 * i + 3], v3(vtmp[0:16, :], 32), AX.X, ALU.add))
            V.settle()
        for i in range(2):
            vv(v.tensor_tensor(vtmp[:, 0:32], w2x[:, 0:32], a2vec[:, 32 * i:32 * i + 32], ALU.mult))
            V.settle()
            vv(v.tensor_reduce(w2x[:, 32 + i:33 + i], vtmp[:, 0:32], AX.X, ALU.add))
            V.settle()
        t2 = v3(gb[:, 0:NJ * 20], 20)
        vv(v.tensor_copy(t2[:, :, 0:16], xv))
        vv(v.memset(t2[:, :, 19:20], 0.0))
        selfe = hcur[:, 0:NJ * 3]

        def alpha_evac(j0, q, ps, m):
            V.wait(m)
            vv(v.tensor_copy(t2[:, j0:j0 + q, 16:19], ps[:, :, 0:3]))
            return vv(v.tensor_copy(xt12[:, j0:j0 + q, 0:3], ps[:, :, 3:6]))

        node_product(lambda j: xv[:, j, :], 16, 0, xT16, v1[:, :], 6, alpha_evac)

        def self_logits(dest, s, d):
            V.settle()
            vv(v.tensor_tensor(dest, s, d, ALU.add))
            V.settle()
            vv(v.scalar_tensor_tensor(dest, dest, 0.2, dest, ALU.mult, ALU.max))
            V.settle()

        self_logits(v3(selfe, 3), t2[:, :, 16:19], xt12[:, :, 0:3])

        def spread(nodes, tile, f, edges, start):
            G.wait((V.sem, V.n), ends, m_zero)
            for j in range(NJ):
                m = c_sct.did(pool.indirect_dma_start(
                    edges, bass.IndirectOffsetOnAxis(ap=stai[:, j:j + 1], axis=0), tile[:, j * f:(j + 1) * f], None,
                    bounds_check=EP - 1, oob_is_err=False))
            G.wait(start)
            return c_sct.did(pool.indirect_dma_start(x0[:, 0:f], None, nodes,
                                                     bass.IndirectOffsetOnAxis(ap=firsti, axis=0)))

        def softmax_pass(k, table, H, D, width, dest, edges, ef, used, spread_done, ready, extra=None):
            f, w = H * (2 + D), 1 + D
            zz, d0, nb = sub[:, 0:TC * H], sub[:, TC * H:2 * TC * H], sub[:, 2 * TC * H:2 * TC * H + TC]
            da = sub[:, TC * 7:TC * (7 + 2 * H)]
            e, p = da[:, 0:TC * H], da[:, TC * H:2 * TC * H]
            xes = [arena[:, i * TC * 12:i * TC * 12 + TC * ef] for i in range(2)]
            exs = [arena[:, (2 + i) * TC * 12:(2 + i) * TC * 12 + TC * ef] for i in range(2)]
            ev = rows(edges, ef)
            m_xe = [None, None]

            def load(c):
                m_xe[c % 2] = c_xe[c % 2].did(sp.dma_start(v3(xes[c % 2], ef), ev[:, span(c), :]))

            S.wait((V.sem, V.n), (A.sem, A.n), (M.sem, M.n), spread_done)
            load(0)
            load(1)

            def messages(c):
                s = c % 2
                xe, xs, xo = v3(xes[s], ef), v3(exs[s], ef), v3(exs[1 - s], ef)
                gv, now, old = got(c, width), state(c, f), state(c + 1, f)
                pr = v3(prod[:, 0:TC * H * w], H * w)
                V.wait(m_xe[s], sent[s], spread_done)
                V.settle()
                for i in used:
                    m = vv(v.tensor_tensor_scan(xs[:, :, i], same[:, span(c)], xe[:, :, i],
                                                xo[:, TC - 1, i:i + 1] if c else x0[:, i:i + 1], ALU.mult, ALU.add))
                if c + 2 < NCH:
                    S.wait(m)
                    load(c + 2)
                vv(v.tensor_scalar(nb, same[:, span(c)], -1.0, BIG, ALU.add, ALU.mult))
                V.settle()
                vv(v.tensor_tensor(v3(zz, H), gv[:, :, D:D + H], xs[:, :, 0:H], ALU.add))
                if extra:
                    extra(c, xs)
                V.settle()
                vv(v.scalar_tensor_tensor(e, zz, 0.2, zz, ALU.mult, ALU.max))
                V.settle()
                for h in range(H):
                    vv(v.tensor_tensor_scan(now[:, :, h], nb, v3(e, H)[:, :, h], old[:, TC - 1, h:h + 1] if c else -BIG,
                                            ALU.add, ALU.max))
                V.settle()
                z3 = v3(zz, H)
                vv(v.tensor_tensor(z3[:, 1:TC, :], now[:, 0:TC - 1, 0:H], now[:, 1:TC, 0:H], ALU.subtract))
                if c:
                    vv(v.tensor_tensor(z3[:, 0, :], old[:, TC - 1, 0:H], now[:, 0, 0:H], ALU.subtract))
                else:
                    vv(v.memset(z3[:, 0, :], 0.0))
                vv(v.tensor_tensor(v3(p, H), v3(e, H), now[:, :, 0:H], ALU.subtract))
                V.settle()
                m = vv(v.tensor_scalar(e, zz, 0.0, None, ALU.min))
                A.wait(m)
                m = A.did(a.activation(da, da, ACT.Exp))
                V.wait(m)
                vv(v.tensor_tensor(v3(d0, H), v3(e, H), bc(same[:, span(c)], 2, H), ALU.mult))
                for h in range(H):
                    vv(v.tensor_copy(pr[:, :, h * w], v3(p, H)[:, :, h]))
                    free_g[s] = vv(v.tensor_tensor(pr[:, :, h * w + 1:(h + 1) * w], gv[:, :, 0:D],
                                                   bc(v3(p, H)[:, :, h], 2, D), ALU.mult))
                return sums(c, f, lambda i: pr[:, :, i - H], lambda i: v3(d0, H)[:, :, (i - H) // w], range(H, f))

            message_pass(k, table, srci, width, f, dest, messages, ready)

        def softmax_nodes(H, D, ex, logits, feats):
            f, w = H * (2 + D), 1 + D
            m, z = ex[:, :, 0:H], ex[:, :, H:f].rearrange("p j (h w) -> p j h w", w=w)
            t = [v3(Sb[:, i * NJ * H:(i + 1) * NJ * H], H) for i in range(3)]
            l3 = v3(logits, H)
            V.settle()
            vv(v.tensor_tensor(ex, ex, bc(mask[:, :], 2, f), ALU.mult))
            V.settle()
            vv(v.tensor_tensor(m, m, bc(nmask[:, :], 2, H), ALU.add))
            V.settle()
            vv(v.tensor_tensor(t[0], m, l3, ALU.max))
            V.settle()
            vv(v.tensor_tensor(t[1], m, t[0], ALU.subtract))
            vv(v.tensor_tensor(t[2], l3, t[0], ALU.subtract))
            A.wait((V.sem, V.n))
            e = A.did(a.activation(Sb[:, NJ * H:3 * NJ * H], Sb[:, NJ * H:3 * NJ * H], ACT.Exp))
            V.wait(e)
            for h in range(H):
                vv(v.tensor_tensor(z[:, :, h, :], z[:, :, h, :], bc(t[1][:, :, h], 2, w), ALU.mult))
            V.settle()
            tmp = v3(prod[:, 0:NJ * D], D)
            for h in range(H):
                vv(v.tensor_tensor(z[:, :, h, 0], z[:, :, h, 0], t[2][:, :, h], ALU.add))
                vv(v.tensor_tensor(tmp, feats, bc(t[2][:, :, h], 2, D), ALU.mult))
                V.settle()
                vv(v.tensor_tensor(z[:, :, h, 1:w], z[:, :, h, 1:w], tmp, ALU.add))
                vv(v.tensor_scalar(t[0][:, :, h], z[:, :, h, 0], 1.0e-16, None, ALU.add))
                V.settle()
                vv(v.reciprocal(t[0][:, :, h], t[0][:, :, h]))
                V.settle()
            return z, t[0]

        save(tab2a, gb, 20)
        ready = at_nodes = save(xn2a, XT, 12)
        spread_done = spread(xn2a, XT, 12, xe2a, at_nodes)

        def edge_weight(c, xs):
            oh = v3(prod[:, 0:TC * 8], 8)
            tc = typi[:, span(c)]
            vv(v.tensor_tensor(oh, bc(tc, 2, 8), bc(io8, 1, TC), ALU.is_equal))
            V.settle()
            vv(v.tensor_tensor(oh, oh, xs[:, :, 4:12], ALU.mult))
            vv(v.scalar_tensor_tensor(tc, srci[:, span(c)], 8.0, tc, ALU.mult, ALU.add))
            V.settle()
            vv(v.tensor_reduce(wE[:, span(c)], oh, AX.X, ALU.add))

        softmax_pass(3, tab2a, 3, 16, 20, S2a, xe2a, 12, (0, 1, 2) + tuple(range(4, 12)), spread_done, (ready,), edge_weight)
        ex = node_rows(54, S2a, fix_softmax(3, 16, S2a))
        z, rz2 = softmax_nodes(3, 16, ex, selfe, xv)
        an = v3(arena[:, :], 48)
        for h in range(3):
            vv(v.tensor_tensor(an[:, :, 16 * h:16 * h + 16], z[:, :, h, 1:17], bc(rz2[:, :, h], 2, 16), ALU.mult))
        V.settle()
        t2b = v3(gb[:, 0:NJ * 36], 36)
        ad2t = XT[:, 0:NJ]
        vv(v.memset(t2b[:, :, 33:36], 0.0))

        def selu(dest, src_ap, tmp, settle):
            e = vv(v.tensor_scalar(tmp, src_ap, 0.0, None, ALU.min))
            A.wait(e)
            e = A.did(a.activation(tmp, tmp, ACT.Exp))
            vv(v.tensor_scalar(dest, src_ap, 0.0, SELU_S, ALU.max, ALU.mult))
            V.wait(e)
            vv(v.tensor_scalar(tmp, tmp, SELU_S * SELU_A, -SELU_S * SELU_A, ALU.mult, ALU.add))
            V.settle()
            e = vv(v.tensor_tensor(dest, dest, tmp, ALU.add))
            V.settle()
            return e

        hT = [prod[0:96, i * 512:(i + 1) * 512] for i in range(2)]
        hE = [prod[0:96, (2 + i) * 512:(3 + i) * 512] for i in range(2)]
        groups = [(j, min(4, NJ - j)) for j in range(0, NJ, 4)]
        M.wait((V.sem, V.n), (A.sem, A.n))
        used = [None, None]
        for g, (j0, cnt) in enumerate(groups):
            s = g % 2
            M.wait(freeA[s])
            for i in range(cnt):
                m = turned(psA[s], i * P, an[:, j0 + i, :], 48)
            A.wait(m, used[s])
            freeA[s] = A.did(a.activation(xT48[0:48, s * 512:s * 512 + cnt * P], psA[s][0:48, 0:cnt * P], ACT.Copy))
            M.wait(freeA[s], freeB[0])
            m = M.did(pe.matmul(psB[0][0:96, 0:cnt * P], l2bs[:, :], xT48[0:49, s * 512:s * 512 + cnt * P], start=True, stop=True))
            V.wait(m, used[s])
            freeB[0] = selu(hT[s][:, 0:cnt * P], psB[0][0:96, 0:cnt * P], hE[s][:, 0:cnt * P], None)
            b = 1 + g % 2
            M.wait(freeB[0], freeB[b])
            for i in range(cnt):
                m = M.did(pe.matmul(psB[b][:, i * 34:(i + 1) * 34], hT[s][:, i * P:(i + 1) * P], w2x[:, :], start=True, stop=True))
            used[s] = m
            V.wait(m)
            pv = psB[b][:, 0:cnt * 34].rearrange("p (j w) -> p j w", w=34)
            vv(v.tensor_copy(t2b[:, j0:j0 + cnt, 0:33], pv[:, :, 0:33]))
            freeB[b] = vv(v.tensor_copy(ad2t[:, j0:j0 + cnt], pv[:, :, 33]))
        self_logits(hcur[:, 0:NJ], t2b[:, :, 32], ad2t)
        save(tab2b, gb, 36)
        ready = at_nodes = save(xn2b, XT, 1)
        spread_done = spread(xn2b, XT, 1, xe2b, at_nodes)
        softmax_pass(4, tab2b, 1, 32, 36, S2b, xe2b, 1, (0,), spread_done, (ready,))
        ex = node_rows(34, S2b, fix_softmax(1, 32, S2b))
        f32v = v3(gb[:, 0:NJ * 32], 32)
        S.wait((V.sem, V.n), ready)
        V.wait(c_tab.did(sp.dma_start(f32v, tab2b.rearrange("(p j) f -> p j f", p=P)[:, :, 0:32])))
        V.wait(sent[0], sent[1])
        zc = ex[:, :, 1:34]
        t0, t1, t3 = (Sb[:, i * NJ:(i + 1) * NJ] for i in range(3))
        le = hcur[:, 0:NJ]
        V.settle()
        vv(v.tensor_tensor(ex, ex, bc(mask[:, :], 2, 34), ALU.mult))
        V.settle()
        mm = ex[:, :, 0]
        vv(v.tensor_tensor(mm, mm, nmask[:, :], ALU.add))
        V.settle()
        vv(v.tensor_tensor(t0, mm, le, ALU.max))
        V.settle()
        vv(v.tensor_tensor(t1, mm, t0, ALU.subtract))
        vv(v.tensor_tensor(t3, le, t0, ALU.subtract))
        A.wait((V.sem, V.n))
        e = A.did(a.activation(Sb[:, NJ:3 * NJ], Sb[:, NJ:3 * NJ], ACT.Exp))
        V.wait(e)
        vv(v.tensor_tensor(zc, zc, bc(t1, 2, 33), ALU.mult))
        vv(v.tensor_tensor(f32v, f32v, bc(t3, 2, 32), ALU.mult))
        V.settle()
        vv(v.tensor_tensor(t0, ex[:, :, 1], t3, ALU.add))
        vv(v.tensor_tensor(f32v, f32v, ex[:, :, 2:34], ALU.add))
        V.settle()
        vv(v.tensor_scalar(t0, t0, 1.0e-16, None, ALU.add))
        V.settle()
        vv(v.reciprocal(t0, t0))
        V.settle()
        vv(v.tensor_tensor(f32v, f32v, bc(t0, 2, 32), ALU.mult))
        V.settle()
        vv(v.tensor_tensor(f32v, f32v, bc(b2b[:, :], 1, NJ), ALU.add))
        V.settle()
        h2 = v3(arena[:, 0:NJ * 32], 32)
        selu(arena[:, 0:NJ * 32], gb[:, 0:NJ * 32], ext[:, 0:NJ * 32], None)

        def add_x(j0, q, ps, m):
            V.wait(m)
            return vv(v.tensor_tensor(hv[:, j0:j0 + q, :], ps, xv[:, j0:j0 + q, :], ALU.add))

        node_product(lambda j: h2[:, j, :], 32, 1, xT32, wfs[:, :], 16, add_x)
        V.settle()
        layernorm(xv, hv)

        stage = [arena[:, i * 2048:(i + 1) * 2048] for i in range(2)]

        def table3(inp, K, W, width, xT, table):
            tv = table.rearrange("(p j r) w -> p j (r w)", p=P, r=8)
            JB = 2 * (512 // (8 * width)) if width == 32 else 8
            m_y = [None, None]
            fill = {"n": 0}

            def evac(j0, q, ps, m):
                b, o = (j0 // JB) % 2, (j0 % JB) * 8 * width
                V.wait(m, m_y[b])
                e = vv(v.tensor_copy(stage[b][:, o:o + q * 8 * width].rearrange("p (j w) -> p j w", j=q), ps))
                if (j0 + q) % JB == 0 or j0 + q == NJ:
                    lo = j0 // JB * JB
                    S.wait(e)
                    m_y[b] = c_y[b].did(sp.dma_start(tv[:, lo:j0 + q, :], stage[b][:, 0:(j0 + q - lo) * 8 * width].rearrange(
                        "p (j w) -> p j w", w=8 * width)))
                return e

            node_product(inp, K, 0, xT, W, 8 * width, evac)
            return m_y

        m_y = table3(lambda j: xv[:, j, :], 16, l3w1s[:, :], 32, xT16, tab3a)

        def messages3(width):
            def messages(c):
                V.settle()
                pr = v3(prod[:, 0:TC * width], width)
                free_g[c % 2] = vv(v.tensor_tensor(pr, got(c, width), bc(wE[:, span(c)], 2, width), ALU.mult))
                return sums(c, width, lambda k: pr[:, :, k])
            return messages

        message_pass(5, tab3a, typi, 32, 32, S3a, messages3(32), tuple(m_y))
        ex = node_rows(32, S3a, fix_sums(32, S3a))
        vv(v.tensor_tensor(ex, ex, bc(mask[:, :], 2, 32), ALU.mult))
        V.settle()
        h3 = v3(gb[:, 0:NJ * 32], 32)

        def add_root(j0, q, ps, m):
            V.wait(m)
            return vv(v.tensor_tensor(h3[:, j0:j0 + q, :], ps, ex[:, j0:j0 + q, :], ALU.add))

        node_product(lambda j: xv[:, j, :], 16, 1, xT16, r1s[:, :], 32, add_root)
        V.settle()
        vv(v.tensor_scalar(gb[:, 0:NJ * 32], gb[:, 0:NJ * 32], 0.0, None, ALU.max))
        V.settle()

        def add_root2(j0, q, ps, m):
            V.wait(m)
            return vv(v.tensor_tensor(hv[:, j0:j0 + q, :], ps, xv[:, j0:j0 + q, :], ALU.add))

        m_y = table3(lambda j: h3[:, j, :], 32, l3w2s[:, :], 16, xT32, tab3b)
        node_product(lambda j: h3[:, j, :], 32, 1, xT32, r2s[:, :], 16, add_root2)
        message_pass(6, tab3b, typi, 16, 16, S3b, messages3(16), tuple(m_y) + ((M.sem, M.n),))
        ex = node_rows(16, S3b, fix_sums(16, S3b))
        vv(v.tensor_tensor(ex, ex, bc(mask[:, :], 2, 16), ALU.mult))
        V.settle()
        vv(v.tensor_tensor(hv, hv, ex, ALU.add))
        V.settle()
        layernorm(xv, hv)
        full = N // NJ
        S.wait((V.sem, V.n))
        c_fin.did(sp.dma_start(out[0:full * NJ, :].rearrange("(p j) f -> p (j f)", p=full), xcur[0:full, :]))
        m = c_fin.did(sp.dma_start(out[full * NJ:N, :].rearrange("(p j) f -> p (j f)", p=1),
                                   xcur[full:full + 1, 0:(N - full * NJ) * 16]))
        S.wait(m, *((c.sem, c.n) for c in [c_fix, c_ext, c_tab, c_set, c_zero, c_sct] + c_out + c_y))


def kernel(**inputs):
    import numpy as np
    import concourse.bacc as bacc
    from concourse.bass_utils import run_bass_kernel_spmd as run

    i = {k: np.asarray(v) for k, v in inputs.items()}

    def padded(a, fill):
        return np.concatenate([a, np.full((EP - E,) + a.shape[1:], fill, a.dtype)])

    d = padded(i["dst"], N)
    f32 = np.float32
    z = lambda *s: np.zeros(s, f32)
    consts = np.concatenate([np.eye(P, dtype=f32), np.arange(0, EP, T, dtype=f32)[:, None],
                             np.broadcast_to(np.arange(8, dtype=f32), (P, 8)),
                             np.arange(NP, dtype=f32).reshape(P, NJ)], 1)
    ih, hh = i["L1_gnn_gru_w_ih"].T, i["L1_gnn_gru_w_hh"].T
    bi, bh = i["L1_gnn_gru_b_ih"][None], i["L1_gnn_gru_b_hh"][None]
    gru = np.concatenate([np.concatenate([ih, z(16, 16)], 1),
                          np.concatenate([hh[:, 0:32], z(16, 16), hh[:, 32:48]], 1),
                          np.concatenate([bi, z(1, 16)], 1),
                          np.concatenate([bh[:, 0:32], z(1, 16), bh[:, 32:48]], 1)])
    oi = lambda a: a.reshape(-1, 16, 16).transpose(0, 2, 1).reshape(-1, 256)
    w1 = i["L2_gnn_W1"]
    blk = z(49, 96)
    for h in range(3):
        blk[16 * h:16 * h + 16, 32 * h:32 * h + 32] = w1[:, 32 * h:32 * h + 32]
    blk[48] = i["L2_gnn_b1"]
    arrays = {
        "x": np.concatenate([i["x"], z(NP - N, 16)]),
        "src": padded(i["src"], 0).reshape(P, T), "dst": d.reshape(P, T),
        "prv": np.concatenate([np.full(1, -1, d.dtype), d[:-1]]).reshape(P, T),
        "attrT": padded(i["edge_attr_13"], 0).reshape(P, T, 13).transpose(2, 1, 0),
        "typ": padded(i["edge_type_8"], 0).reshape(P, T), "ew": padded(i["edge_weight"], 0).reshape(P, T),
        "consts": consts, "l0w": i["L0_gnn_weight"], "l0s": i["L0_gnn_self_loop_weight"].reshape(1),
        "w1": i["L1_gnn_fnet_w1"], "b1": i["L1_gnn_fnet_b1"].reshape(32, 1),
        "w2a": np.concatenate([oi(i["L1_gnn_fnet_w2"]), oi(i["L1_gnn_fnet_b2"])]), "gw": gru,
        "l2w": w1, "l2blk": blk, "as1": i["L2_gnn_a_src1"].reshape(96), "ad1": i["L2_gnn_a_dst1"].reshape(96),
        "w2s": i["L2_gnn_W2"], "as2": i["L2_gnn_a_src2"].reshape(32), "ad2": i["L2_gnn_a_dst2"].reshape(32),
        "b2": i["L2_gnn_b2"], "wf": np.concatenate([i["L2_gnn_Wf"], i["L2_gnn_bf"][None]]),
        "l3w1": i["L3_gnn_W1"].transpose(1, 0, 2).reshape(16, 256),
        "root1": np.concatenate([i["L3_gnn_root1"], i["L3_gnn_b1"][None]]),
        "l3w2": i["L3_gnn_W2"].transpose(1, 0, 2).reshape(32, 128),
        "root2": np.concatenate([i["L3_gnn_root2"], i["L3_gnn_b2"][None]]),
    }
    arrays = {k: np.ascontiguousarray(v) for k, v in arrays.items()}
    nc = bacc.Bacc("TRN2", target_bir_lowering=False, num_devices=1)
    args = [nc.dram_tensor("in_" + k, v.shape, mybir.dt.from_np(v.dtype), kind="ExternalInput").ap() for k, v in arrays.items()]
    out = nc.dram_tensor("out", (N, 16), F32, kind="ExternalOutput").ap()
    gnn_program(nc, *args, out)
    r = run(nc, [{"in_" + k: v for k, v in arrays.items()}], core_ids=[0])
    return r.results[0]["out"]
```

```python
from contextlib import ExitStack

import concourse.bass as bass
from concourse import mybir

F32 = mybir.dt.float32
I32 = mybir.dt.int32
ALU = mybir.AluOpType
ACT = mybir.ActivationFunctionType
AX = mybir.AxisListType

N, E = 12500, 412500
P = 128
NJ = 98
NP = P * NJ
T = 3224
EP = P * T
TC = 52
NCH = T // TC
NS, SW = 62, 52
BIG = 1.0e30
NB = 7
JB = NJ // NB
SELU_A, SELU_S = 1.6732632423543772, 1.0507009873554805
CI, CB, C8, CN = 0, 128, 129, 137
CW = CN + NJ


class Queue:

    def __init__(self, eng, sem):
        self.eng, self.sem, self.n, self.seen = eng, sem, 0, {}

    def wait(self, *marks):
        for m in marks:
            if m is not None and self.seen.get(id(m[0]), 0) < m[1]:
                self.eng.wait_ge(m[0], m[1])
                self.seen[id(m[0])] = m[1]

    def did(self, ins):
        ins.then_inc(self.sem, 1)
        self.n += 1
        return self.sem, self.n

    def settle(self):
        self.wait((self.sem, self.n) if self.n else None)


class Chan:

    def __init__(self, sem):
        self.sem, self.n = sem, 0

    def did(self, ins):
        ins.then_inc(self.sem, 16)
        self.n += 16
        return self.sem, self.n


def gnn_program(nc, x, src, dst, prv, attrT, typ, ew, consts, l0w, l0s, w1, b1, w2a, gw, l2w, l2blk, as1, ad1, w2s, as2, ad2,
                b2, wf, l3w1, root1, l3w2, root2, out):
    with ExitStack() as ctx:
        def sb(name, shape, dt=F32):
            return ctx.enter_context(nc.sbuf_tensor(name, shape, dt))

        def sem(name):
            return ctx.enter_context(nc.semaphore(name))

        def dram(name, shape, dt=F32):
            return nc.dram_tensor(name, shape, dt).ap()

        V = Queue(nc.vector, sem("s_vec"))
        A = Queue(nc.scalar, sem("s_act"))
        M = Queue(nc.tensor, sem("s_pe"))
        G = Queue(nc.gpsimd, sem("s_pool"))
        S = Queue(nc.sync, None)
        v, a, pe, pool, sp = nc.vector, nc.scalar, nc.tensor, nc.gpsimd, nc.sync

        srci = sb("srci", [P, T], I32)
        typi = sb("typi", [P, T], I32)
        same = sb("same", [P, T])
        wE = sb("wE", [P, T])
        dsti = wE[:, :].bitcast(I32)
        gb = sb("gb", [P, 2 * TC * 36])
        prod = sb("prod", [P, 2944])
        Sb = sb("Sb", [P, 2 * TC * 56])
        ext = sb("ext", [P, NJ * 54])
        exti = ext[:, :].bitcast(I32)
        arena = sb("arena", [P, NJ * 48])
        xcur = sb("xcur", [P, NJ * 16])
        hcur = sb("hcur", [P, NJ * 16])
        XT = sb("XT", [P, NJ * 12])
        lg = sb("lg", [P, NJ * 4])
        hid = sb("hid", [P, 2 * 512])
        xT16 = sb("xT16", [P, 2 * 512])
        xT32 = sb("xT32", [P, 2 * 512])
        xT48 = sb("xT48", [P, 2 * 512])
        ewc = sb("ewc", [P, 2 * TC])
        sub = sb("sub", [P, TC * 22])
        cst = sb("cst", [P, CW])
        zero = sb("zero", [P, TC * 12])
        w1s = sb("w1s", [26, P])
        b1s = sb("b1s", [P, 1])
        w2as = sb("w2as", [97, 256])
        gws = sb("gws", [34, 64])
        l0wb = sb("l0wb", [P, 16])
        l0sb = sb("l0sb", [P, 1])
        l2ws = sb("l2ws", [16, 96])
        l2bs = sb("l2bs", [49, 96])
        avec = sb("avec", [16, 2 * 96])
        a2vec = sb("a2vec", [96, 64])
        vtmp = sb("vtmp", [96, 96])
        v1 = sb("v1", [16, 6])
        w2x = sb("w2x", [96, 34])
        b2b = sb("b2b", [P, 32])
        wfs = sb("wfs", [33, 16])
        l3w1s = sb("l3w1s", [16, 256])
        r1s = sb("r1s", [17, 32])
        l3w2s = sb("l3w2s", [32, 128])
        r2s = sb("r2s", [33, 16])
        endi = sb("endi", [P, NJ], I32)
        stai = sb("stai", [P, NJ], I32)
        fndi = sb("fndi", [P, NJ], I32)
        mask = sb("mask", [P, NJ])
        nmask = sb("nmask", [P, NJ])
        invdeg = sb("invdeg", [P, NJ])
        nt = sb("nt", [P, 4 * NJ])
        pcol = sb("pcol", [P, 8])
        pcoi = sb("pcoi", [P, 2], I32)
        contT = sb("contT", [64, P])
        nbT = sb("nbT", [4, P])
        fx = sb("fx", [P, 640])
        fC = sb("fC", [P, 129])
        fM = sb("fM", [4, 129])
        x0 = sb("x0", [P, 24])

        psA = [ctx.enter_context(nc.psum_tensor(f"psA{i}", [P, 512], F32)) for i in range(2)]
        psB = [ctx.enter_context(nc.psum_tensor(f"psB{i}", [P, 1024], F32)) for i in range(3)]
        freeA, freeB = [None, None], [None, None, None]

        first_d = dram("first_d", [P, 1], I32)
        samp_d = dram("samp_d", [P, NS], I32)
        cont_d = dram("cont_d", [P, 1])
        end_d = dram("end_d", [NP + 1])
        S0 = dram("S0", [EP, 24])
        S1 = [dram("S1a", [EP, 16]), dram("S1b", [EP, 16])]
        S2a = dram("S2a", [EP, 54])
        S2b = dram("S2b", [EP, 34])
        S3a = dram("S3a", [EP, 32])
        S3b = dram("S3b", [EP, 16])
        tab1 = [dram("tab1a", [NP, 16]), dram("tab1b", [NP, 16])]
        tab2a = dram("tab2a", [NP, 20])
        tab2b = dram("tab2b", [NP, 36])
        tab3a = dram("tab3a", [NP * 8, 32])
        tab3b = dram("tab3b", [NP * 8, 16])
        xn2a = dram("xn2a", [NP, 12])
        xn2b = dram("xn2b", [NP, 1])
        xe2a = dram("xe2a", [EP, 12])
        xe2b = dram("xe2b", [EP, 1])

        c_src, c_dst, c_prv, c_typ, c_w = (Chan(sem(f"c_{n}")) for n in ("src", "dst", "prv", "typ", "w"))
        c_ew = [Chan(sem(f"c_ew{i}")) for i in range(2)]
        c_att = [Chan(sem(f"c_att{i}")) for i in range(3)]
        c_out = [Chan(sem(f"c_out{i}")) for i in range(2)]
        c_xe = [Chan(sem(f"c_xe{i}")) for i in range(2)]
        c_y = [Chan(sem(f"c_y{i}")) for i in range(2)]
        c_fix, c_srch, c_tab, c_set, c_zero, c_sct, c_fin = (Chan(sem(f"c_{n}")) for n in
                                                            ("fix", "srch", "tab", "set", "zero", "sct", "fin"))
        c_ext = [Chan(sem(f"c_ext{i}")) for i in range(NB)]
        c_g = [[Chan(sem(f"c_g{k}_{i}")) for i in range(2)] for k in range(7)]

        ident = cst[:, CI:CI + P]
        pbase = cst[:, CB:CB + 1]
        io8 = cst[:, C8:C8 + 8]
        nid = cst[:, CN:CN + NJ]

        def rows(d, f):
            return d.rearrange("(p t) f -> p t f", p=P)

        def v3(t, f):
            return t.rearrange("p (t f) -> p t f", f=f)

        def bc(ap, axis, n):
            ap = ap.unsqueeze(axis)
            shape = list(ap.shape)
            shape[axis] = n
            return ap.to_broadcast(shape)

        def vv(ins):
            return V.did(ins)

        m_src = c_src.did(sp.dma_start(srci[:, :], src))
        m_dst = c_dst.did(sp.dma_start(dsti, dst))
        m_prv = c_prv.did(sp.dma_start(typi[:, :], prv))
        for t, d in ((cst[:, :], consts), (w1s[:, :], w1), (b1s[:, :], b1), (w2as[:, :], w2a), (gws[:, :], gw),
                     (l0wb[:, :], l0w.partition_broadcast(P)), (l0sb[:, :], l0s.partition_broadcast(P)),
                     (l2ws[:, :], l2w), (l2bs[:, :], l2blk),
                     (avec[:, 0:96], as1.partition_broadcast(16)), (avec[:, 96:192], ad1.partition_broadcast(16)),
                     (a2vec[:, 0:32], as2.partition_broadcast(96)), (a2vec[:, 32:64], ad2.partition_broadcast(96)),
                     (w2x[:, 0:32], w2s), (b2b[:, :], b2.partition_broadcast(P)), (wfs[:, :], wf),
                     (l3w1s[:, :], l3w1), (r1s[:, :], root1), (l3w2s[:, :], l3w2), (r2s[:, :], root2),
                     (xcur[:, :], x.rearrange("(p j) f -> p (j f)", p=P))):
            m_w = c_w.did(a.dma_start(t, d))

        m_z = vv(v.memset(zero[:, :], 0.0))
        for t in (xT16, xT32, xT48):
            vv(v.memset(t[:, :], 1.0))
        vv(v.memset(hid[:, :], 1.0))
        vv(v.memset(fC[:, :], 0.0))
        vv(v.memset(fM[:, :], -BIG))
        vv(v.memset(pcol[:, 7:8], -1.0))
        V.wait(m_dst, m_prv, m_w)
        m_same = vv(v.tensor_tensor(same[:, :], dsti, typi[:, :], ALU.is_equal))
        samp = hcur[:, 0:NS].bitcast(I32)
        m_samp = vv(v.tensor_copy(samp, wE[:, 0:T:SW].bitcast(I32)))
        firstf, contc, cntf, fixf = (pcol[:, i:i + 1] for i in range(4))
        vv(v.tensor_copy(firstf, dsti[:, 0:1]))
        vv(v.tensor_copy(pcoi[:, 0:1], dsti[:, 0:1]))
        V.settle()
        vv(v.tensor_tensor(contc, firstf, dsti[:, T - 1:T], ALU.is_equal))
        junk = Sb[:, 0:T]
        vv(v.tensor_scalar(junk, dsti, firstf, None, ALU.is_equal))
        V.settle()
        samep = same[:, 0:1]
        vv(v.tensor_tensor(contc, contc, samep, ALU.mult))
        vv(v.tensor_reduce(cntf, junk, AX.X, ALU.add))
        V.settle()
        vv(v.scalar_tensor_tensor(fixf, cntf, -1.0, pbase, ALU.add, ALU.add))
        vv(v.tensor_scalar(pcol[:, 4:5], samep, -1.0, BIG, ALU.add, ALU.mult))
        V.settle()
        m_fix = vv(v.tensor_copy(pcoi[:, 1:2], fixf))
        nsamep = pcol[:, 4:5]
        firsti, fixi = pcoi[:, 0:1], pcoi[:, 1:2]
        S.wait(m_fix, m_samp)
        c_set.did(sp.dma_start(samp_d, samp))
        c_set.did(sp.dma_start(cont_d, contc))
        m_s1 = c_set.did(sp.dma_start(first_d, firsti))
        c_zero.did(sp.dma_start(end_d[0:1].unsqueeze(0), pcol[0:1, 7:8]))
        m_typ = None

        S.wait(m_s1, m_z)
        fr = fx[:, 0:P].bitcast(I32)
        c_set.did(sp.dma_start(fr, first_d.rearrange("p o -> o p")[0].partition_broadcast(P)))
        m_s2 = c_set.did(sp.dma_start(contT[:, :], cont_d.rearrange("p o -> o p")[0].partition_broadcast(64)))
        S.wait(m_same)
        m_typ = c_typ.did(sp.dma_start(typi[:, :], typ))
        for k in range(NCH):
            c_zero.did(sp.dma_start(rows(xe2a, 12)[:, k * TC:(k + 1) * TC, :], v3(zero[:, :], 12)))
        xe2bv = xe2b.rearrange("(p t) f -> p (t f)", p=P)
        for k in range(0, T, TC * 12):
            n = min(TC * 12, T - k)
            m_zero = c_zero.did(sp.dma_start(xe2bv[:, k:k + n], zero[:, 0:n]))

        V.wait(m_s2)
        vv(v.tensor_scalar(nbT[:, :], contT[0:4, :], -1.0, BIG, ALU.add, ALU.mult))
        rank, blk, cum = nt[:, 0:NJ], nt[:, NJ:2 * NJ], nt[:, 2 * NJ:3 * NJ]

        def count_le(dest, j0, nj, width, vals):
            cmp = v3(arena[:, 0:nj * width], width)
            V.settle()
            vv(v.tensor_tensor(cmp, vals, bc(nid[:, j0:j0 + nj], 2, width), ALU.is_le))
            V.settle()
            return vv(v.tensor_reduce(dest[:, j0:j0 + nj], cmp, AX.X, ALU.add))

        def search1():
            for j0 in range(0, NJ, 14):
                count_le(rank, j0, 14, P, bc(fr, 1, 14))
            V.settle()
            vv(v.tensor_scalar(rank, rank, -1.0, 0.0, ALU.add, ALU.max))
            V.settle()
            return vv(v.tensor_copy(fndi[:, :], rank))

        HALF = NJ // 2

        def rows_of(table, width, half, ready):
            G.wait(*ready)
            for j in range(HALF):
                m = c_srch.did(pool.indirect_dma_start(
                    exti[:, j * width:(j + 1) * width], None, table,
                    bass.IndirectOffsetOnAxis(ap=fndi[:, half * HALF + j:half * HALF + j + 1], axis=0)))
            return m

        def count_rows(dest, width, half, arrived):
            V.wait(arrived)
            for j in range(0, HALF, 7):
                m = count_le(dest, half * HALF + j, 7, width, v3(exti[:, j * width:(j + 7) * width], width))
            return m

        def search_blocks(half_marks):
            V.settle()
            vv(v.scalar_tensor_tensor(blk, rank, float(NS), blk, ALU.mult, ALU.add))
            V.settle()
            vv(v.tensor_scalar(blk, blk, -1.0, 0.0, ALU.add, ALU.max))
            V.settle()
            return vv(v.tensor_copy(fndi[:, :], blk))

        def search_ends():
            V.settle()
            vv(v.scalar_tensor_tensor(cum, blk, float(SW), cum, ALU.mult, ALU.add))
            V.settle()
            e = vv(v.tensor_scalar(cum, cum, -1.0, None, ALU.add))
            S.wait(e)
            m = c_set.did(sp.dma_start(end_d[1:NP + 1].rearrange("(p j) -> p j", p=P), cum))
            S.wait(m, m_zero)
            m = c_set.did(sp.dma_start(nt[:, 3 * NJ:4 * NJ], end_d[0:NP].rearrange("(p j) -> p j", p=P)))
            V.wait(m)
            before = nt[:, 3 * NJ:4 * NJ]
            vv(v.tensor_tensor(mask[:, :], cum, before, ALU.subtract))
            vv(v.tensor_scalar(rank, cum, 0.0, None, ALU.max))
            V.settle()
            vv(v.tensor_scalar(mask[:, :], mask[:, :], 1.0, None, ALU.min))
            vv(v.tensor_copy(endi[:, :], rank))
            V.settle()
            vv(v.tensor_scalar(blk, mask[:, :], -1.0e6, 1.0e6 + 1.0, ALU.mult, ALU.add))
            vv(v.tensor_scalar(nmask[:, :], mask[:, :], -1.0, BIG, ALU.add, ALU.mult))
            V.settle()
            vv(v.tensor_tensor(blk, blk, before, ALU.add))
            V.settle()
            return vv(v.tensor_copy(stai[:, :], blk))

        free_g = [None, None]
        sent = [None, None]

        def gather(k, table, idx, width, c, ready):
            s = c % 2
            G.wait(free_g[s], *ready)
            for i in range(TC):
                t = c * TC + i
                o = s * TC * 36 + i * width
                m = c_g[k][s].did(pool.indirect_dma_start(
                    gb[:, o:o + width], None, table, bass.IndirectOffsetOnAxis(ap=idx[:, t:t + 1], axis=0)))
            return m

        def got(c, width):
            o = (c % 2) * TC * 36
            return v3(gb[:, o:o + TC * width], width)

        def state(c, f):
            o = (c % 2) * TC * 56
            return v3(Sb[:, o:o + TC * f], f)

        def put(c, f, dest, done):
            S.wait(done)
            sent[c % 2] = c_out[c % 2].did(sp.dma_start(rows(dest, f)[:, c * TC:(c + 1) * TC, :], state(c, f)))

        def span(c):
            return slice(c * TC, (c + 1) * TC)

        def sums(c, f, data, decay=None, cols=None):
            V.wait(sent[c % 2])
            V.settle()
            now, old = state(c, f), state(c + 1, f)
            for k in (cols or range(f)):
                init = old[:, TC - 1, k:k + 1] if c else 0.0
                d0 = same[:, span(c)] if decay is None else decay(k)
                m = vv(v.tensor_tensor_scan(now[:, :, k], d0, data(k), init, ALU.mult, ALU.add))
            return m

        def message_pass(k, table, idx, width, f, dest, messages, ready, hooks=None):
            arrived = {}
            for c in range(2):
                arrived[c] = gather(k, table, idx, width, c, ready)
            for c in range(NCH):
                V.wait(arrived[c])
                done = messages(c)
                put(c, f, dest, done)
                if c + 2 < NCH:
                    arrived[c + 2] = gather(k, table, idx, width, c + 2, ready)
                if hooks and c in hooks:
                    hooks[c]()

        def turned(dst_ps, col, inp, width):
            return M.did(pe.transpose(dst_ps[0:width, col:col + P], inp, ident))

        def to_rows(f, final, out_cols):
            M.wait(freeA[0], (V.sem, V.n))
            m = turned(psA[0], 0, final, f)
            V.wait(m)
            freeA[0] = vv(v.tensor_copy(fx[0:f, out_cols:out_cols + P], psA[0][0:f, 0:P]))

        def to_cols(f, rows_ap, dest):
            M.wait(freeA[1], (V.sem, V.n))
            m = M.did(pe.transpose(psA[1][0:P, 0:f], rows_ap, ident[0:f, 0:f]))
            V.wait(m)
            freeA[1] = vv(v.tensor_copy(dest, psA[1][0:P, 0:f]))

        W0 = 256

        def fix_gather(f, dest):
            row = fx[:, W0:W0 + f]
            G.wait(sent[0], sent[1], m_fix, (V.sem, V.n))
            return c_fix.did(pool.indirect_dma_start(row, None, dest, bass.IndirectOffsetOnAxis(ap=fixi, axis=0)))

        def fix_scatter(f, dest):
            G.wait((V.sem, V.n))
            return c_fix.did(pool.indirect_dma_start(dest, bass.IndirectOffsetOnAxis(ap=fixi, axis=0),
                                                     fx[:, W0:W0 + f], None))

        def fix_sums(f, dest):
            m = fix_gather(f, dest)
            final = state(NCH - 1, f)[:, TC - 1, :]
            to_rows(f, final, 128)
            V.settle()
            vv(v.tensor_tensor_scan(fC[0:f, 1:129], contT[0:f, :], fx[0:f, 128:256], 0.0, ALU.mult, ALU.add))
            V.settle()
            carry = fx[:, W0 + 64:W0 + 64 + f]
            to_cols(f, fC[0:f, 0:P], carry)
            V.wait(m)
            V.settle()
            vv(v.scalar_tensor_tensor(fx[:, W0:W0 + f], carry, samep, fx[:, W0:W0 + f], ALU.mult, ALU.add))
            return fix_scatter(f, dest)

        def fix_softmax(H, D, dest):
            f, w = H * (2 + D), 1 + D
            m = fix_gather(f, dest)
            final = state(NCH - 1, f)[:, TC - 1, :]
            mrow, arow = fx[:, W0:W0 + H], fx[:, W0 + H:W0 + f]
            o = W0 + 64
            mx, mp, f1, f0, bb = (fx[:, o + 4 * i:o + 4 * i + H] for i in range(5))
            d0, d1 = fx[:, o + 32:o + 32 + H * w], fx[:, o + 96:o + 96 + H * w]
            cprev = fx[:, o + 160:o + 160 + H * w]
            to_rows(H, final[:, 0:H], 128)
            V.settle()
            vv(v.tensor_tensor_scan(fM[0:H, 1:129], nbT[0:H, :], fx[0:H, 128:256], -BIG, ALU.add, ALU.max))
            V.settle()
            to_cols(H, fM[0:H, 1:129], mx)
            V.settle()
            to_cols(H, fM[0:H, 0:P], mp)
            V.settle()
            vv(v.tensor_tensor(f1, final[:, 0:H], mx, ALU.subtract))
            vv(v.tensor_tensor(f0, mp, mx, ALU.subtract))
            V.settle()
            e = vv(v.tensor_scalar(f0, f0, 0.0, None, ALU.min))
            A.wait(e)
            A.did(a.activation(f1, f1, ACT.Exp))
            e = A.did(a.activation(f0, f0, ACT.Exp))
            V.wait(e)
            vv(v.tensor_scalar(f0, f0, contc, None, ALU.mult))
            V.settle()
            vv(v.tensor_tensor(v3(d1, w), v3(final[:, H:f], w), bc(f1, 2, w), ALU.mult))
            vv(v.tensor_copy(v3(d0, w), bc(f0, 2, w)))
            V.settle()
            to_rows(H * w, d0, 0)
            to_rows(H * w, d1, 128)
            V.settle()
            vv(v.tensor_tensor_scan(fC[0:H * w, 1:129], fx[0:H * w, 0:P], fx[0:H * w, 128:256], 0.0, ALU.mult, ALU.add))
            V.settle()
            to_cols(H * w, fC[0:H * w, 0:P], cprev)
            V.wait(m)
            V.settle()
            vv(v.tensor_scalar(mp, mp, nsamep, None, ALU.add))
            V.settle()
            vv(v.tensor_tensor(mx, mrow, mp, ALU.max))
            V.settle()
            vv(v.tensor_tensor(f1, mrow, mx, ALU.subtract))
            vv(v.tensor_tensor(bb, mp, mx, ALU.subtract))
            V.settle()
            vv(v.tensor_copy(mrow, mx))
            A.wait((V.sem, V.n))
            A.did(a.activation(f1, f1, ACT.Exp))
            e = A.did(a.activation(bb, bb, ACT.Exp))
            V.wait(e)
            vv(v.tensor_scalar(bb, bb, samep, None, ALU.mult))
            vv(v.tensor_tensor(v3(arow, w), v3(arow, w), bc(f1, 2, w), ALU.mult))
            V.settle()
            vv(v.tensor_tensor(v3(cprev, w), v3(cprev, w), bc(bb, 2, w), ALU.mult))
            V.settle()
            vv(v.tensor_tensor(arow, arow, cprev, ALU.add))
            return fix_scatter(f, dest)

        xT_used = {}

        def node_product(inp, K, ones, xT, W, width, evac, J):
            per = 512 // width
            n = min(4, 2 * per)
            groups = [(j, min(n, J.stop - j)) for j in range(J.start, J.stop, n)]
            M.wait((V.sem, V.n), (A.sem, A.n))
            used = xT_used.setdefault(id(xT), [None, None])
            copied = {}
            for g in range(len(groups) + 1):
                if g < len(groups):
                    j0, cnt = groups[g]
                    M.wait(freeA[g % 2])
                    for i in range(cnt):
                        m = turned(psA[g % 2], i * P, inp(j0 + i), K)
                    A.wait(m, used[g % 2])
                    o = (g % 2) * 512
                    copied[g] = A.did(a.activation(xT[0:K, o:o + cnt * P], psA[g % 2][0:K, 0:cnt * P], ACT.Copy))
                    freeA[g % 2] = copied[g]
                if g > 0:
                    j0, cnt = groups[g - 1]
                    b = (g - 1) % 3
                    M.wait(copied[g - 1], freeB[b])
                    o = ((g - 1) % 2) * 512
                    for i in range(cnt):
                        at = (i // per) * 512 + (i % per) * width
                        m = M.did(pe.matmul(psB[b][:, at:at + width], xT[0:K + ones, o + i * P:o + (i + 1) * P], W,
                                            start=True, stop=True))
                    used[(g - 1) % 2] = m
                    for i in range(0, cnt, per):
                        q = min(per, cnt - i)
                        at = (i // per) * 512
                        freeB[b] = evac(j0 + i, q, psB[b][:, at:at + q * width].rearrange("p (j w) -> p j w", w=width), m)

        def layernorm(dest, r, J):
            d = v3(Sb[:, 0:NJ * 16], 16)[:, J, :]
            q = v3(Sb[:, NJ * 16:NJ * 32], 16)[:, J, :]
            s, t = nt[:, J], nt[:, NJ + J.start:NJ + J.stop]
            V.settle()
            vv(v.tensor_reduce(s, r, AX.X, ALU.add))
            V.settle()
            vv(v.tensor_scalar(s, s, 1.0 / 16, None, ALU.mult))
            V.settle()
            vv(v.tensor_tensor(d, r, bc(s, 2, 16), ALU.subtract))
            V.settle()
            vv(v.tensor_tensor(q, d, d, ALU.mult))
            V.settle()
            vv(v.tensor_reduce(t, q, AX.X, ALU.add))
            V.settle()
            e = vv(v.tensor_scalar(t, t, 1.0 / 16, 1.0e-5, ALU.mult, ALU.add))
            A.wait(e)
            e = A.did(a.activation(s, t, ACT.Sqrt))
            V.wait(e)
            vv(v.reciprocal(t, s))
            V.settle()
            vv(v.tensor_tensor(dest[:, J, :], d, bc(t, 2, 16), ALU.mult))
            V.settle()

        xv, hv = v3(xcur[:, :], 16), v3(hcur[:, :], 16)

        for i in range(2):
            vv(v.tensor_tensor(vtmp[0:16, :], l2ws[:, :], avec[:, 96 * i:96 * i + 96], ALU.mult))
            V.settle()
            vv(v.tensor_reduce(v1[:, 3 * i:3 * i + 3], v3(vtmp[0:16, :], 32), AX.X, ALU.add))
            V.settle()
        for i in range(2):
            vv(v.tensor_tensor(vtmp[:, 0:32], w2x[:, 0:32], a2vec[:, 32 * i:32 * i + 32], ALU.mult))
            V.settle()
            vv(v.tensor_reduce(w2x[:, 32 + i:33 + i], vtmp[:, 0:32], AX.X, ALU.add))
            V.settle()

        m_fnd = search1()

        def messages0(c):
            s = c % 2
            V.wait(m_ew[s], m_typ)
            V.settle()
            pr = v3(prod[:, 0:TC * 24], 24)
            vv(v.tensor_tensor(pr[:, :, 16:24], bc(typi[:, span(c)], 2, 8), bc(io8, 1, TC), ALU.is_equal))
            free_g[s] = vv(v.tensor_tensor(pr[:, :, 0:16], got(c, 16), bc(ewc[:, s * TC:(s + 1) * TC], 2, 16), ALU.mult))
            if c + 2 < NCH:
                S.wait(free_g[s])
                m_ew[s] = c_ew[s].did(sp.dma_start(ewc[:, s * TC:(s + 1) * TC], ew[:, span(c + 2)]))
            return sums(c, 24, lambda k: pr[:, :, k])

        m_ew = [c_ew[i].did(sp.dma_start(ewc[:, i * TC:(i + 1) * TC], ew[:, span(i)])) for i in range(2)]
        st = {}

        def hook(fn, *args):
            return lambda: st.__setitem__(fn.__name__ + str(len(st)), fn(*args))

        def h1():
            st["a"] = rows_of(samp_d, NS, 0, (m_fnd, m_s1))

        def h2():
            st["a"] = count_rows(blk, NS, 0, st["a"])

        def h3():
            st["b"] = rows_of(samp_d, NS, 1, (st["a"],))

        def h4():
            st["b"] = search_blocks(count_rows(blk, NS, 1, st["b"]))

        def h5():
            st["a"] = rows_of(dst.rearrange("p (s w) -> (p s) w", w=SW), SW, 0, (st["b"],))

        def h6():
            st["a"] = count_rows(cum, SW, 0, st["a"])

        def h7():
            st["b"] = rows_of(dst.rearrange("p (s w) -> (p s) w", w=SW), SW, 1, (st["a"],))

        def h8():
            count_rows(cum, SW, 1, st["b"])
            st["e"] = search_ends()

        message_pass(0, x, srci, 16, 24, S0, messages0, (m_src,),
                     {4 + 2 * i: h for i, h in enumerate((h1, h2, h3, h4, h5, h6, h7, h8))})
        ends = st["e"]
        G.wait(ends)
        xt12 = v3(XT[:, :], 12)
        lg3, lg1 = v3(lg[:, 0:NJ * 3], 3), lg[:, NJ * 3:NJ * 4]
        wk = v3(Sb[:, NJ * 32:NJ * 48], 16)

        def blocks(f, dest, fixed, stage):
            G.wait(fixed, (V.sem, V.n), (M.sem, M.n))
            for b in range(NB):
                for j in range(b * JB, (b + 1) * JB):
                    m = c_ext[b].did(pool.indirect_dma_start(
                        ext[:, j * f:(j + 1) * f], None, dest,
                        bass.IndirectOffsetOnAxis(ap=endi[:, j:j + 1], axis=0)))
                arrived[b] = m
            for b in range(NB):
                V.wait(arrived[b])
                J = slice(b * JB, (b + 1) * JB)
                stage(J, v3(ext[:, 0:NJ * f], f)[:, J, :])

        arrived = [None] * NB

        def save(table, tile, f, J):
            S.wait((V.sem, V.n), (A.sem, A.n))
            return c_tab.did(sp.dma_start(table.rearrange("(p j) f -> p j f", p=P)[:, J, :], v3(tile[:, 0:NJ * f], f)[:, J, :]))

        def nodes0(J, ex):
            vv(v.tensor_tensor(ex, ex, bc(mask[:, J], 2, 24), ALU.mult))
            V.settle()
            deg, w = invdeg[:, J], wk[:, J, :]
            vv(v.tensor_reduce(deg, ex[:, :, 16:24], AX.X, ALU.add))
            vv(v.tensor_tensor(w, ex[:, :, 0:16], bc(l0wb[:, :], 1, JB), ALU.mult))
            vv(v.tensor_scalar(xt12[:, J, 4:12], ex[:, :, 16:24], 1.0, None, ALU.max))
            V.settle()
            vv(v.tensor_scalar(deg, deg, 1.0, None, ALU.max))
            vv(v.scalar_tensor_tensor(w, xv[:, J, :], l0sb[:, 0:1], w, ALU.mult, ALU.add))
            vv(v.reciprocal(xt12[:, J, 4:12], xt12[:, J, 4:12]))
            V.settle()
            vv(v.reciprocal(deg, deg))
            vv(v.tensor_tensor(w, w, xv[:, J, :], ALU.add))
            V.settle()
            vv(v.tensor_scalar(w, w, 0.0, 1.0, ALU.max, ALU.min))
            V.settle()
            vv(v.tensor_tensor(w, w, xv[:, J, :], ALU.add))
            layernorm(xv, w, J)
            st["ready"] = save(tab1[0], xcur, 16, J)
            vv(v.tensor_copy(hv[:, J, :], xv[:, J, :]))

        vv(v.memset(XT[:, :], 0.0))
        blocks(24, S0, fix_sums(24, S0), nodes0)

        NG = T // 4
        NQ = (T // 8 + 1) // 2
        atts = [ext[0:26, i * 1024:(i + 1) * 1024] for i in range(3)]
        pr1 = [prod[:, i * 1024:(i + 1) * 1024] for i in range(2)]
        msg = v3(prod[:, 2048:2048 + TC * 16], 16)

        def message_net(rep):
            M.wait((V.sem, V.n))
            m_att, used_att = {}, {}
            hid_ready, hid_used, w_ready = {}, {}, {}

            def att_load(q):
                n = min(1024, T // 8 * 512 - q * 1024)
                S.wait(used_att.get(q - 3), (V.sem, V.n) if q == 0 else None)
                m_att[q] = c_att[q % 3].did(sp.dma_start(atts[q % 3][:, 0:n], attrT[:, q * 1024:q * 1024 + n]))

            def hidden(h):
                q, o, s = h // 2, (h % 2) * 512, h % 2
                M.wait(m_att[q], freeA[s])
                used_att[q] = m = M.did(pe.matmul(psA[s][:, :], w1s[:, :], atts[q % 3][:, o:o + 512], start=True, stop=True))
                A.wait(m, hid_used.get(h - 2))
                hid_ready[h] = freeA[s] = A.did(a.activation(hid[:, s * 512:(s + 1) * 512], psA[s][:, :], ACT.Relu,
                                                             bias=b1s[:, 0:1]))

            def weights(k):
                h, at = k // 2, 64 * (k % 2)
                M.wait(hid_ready[h], freeB[k % 3])
                for i in range(4):
                    o = (h % 2) * 512 + i * P
                    m = M.did(pe.matmul(psB[k % 3][:, i * 256:(i + 1) * 256], hid[at:at + 33, o:o + P],
                                        w2as[at:at + 33, :], start=True, stop=True))
                hid_used[h] = w_ready[k] = m

            def step(k):
                if k % 2 == 0 and k // 2 + 1 < T // 8:
                    h = k // 2 + 1
                    if h % 2 == 0 and h // 2 + 2 < NQ:
                        att_load(h // 2 + 2)
                    hidden(h)
                weights(k)

            def messages1(c):
                gv = got(c, 16)
                base = c * TC // 4
                reduced = [None, None]
                V.settle()

                def reduce(i):
                    V.wait(multiplied[i])
                    reduced[i % 2] = vv(v.tensor_reduce(msg[:, 4 * i:4 * i + 4, :], pr1[i % 2].rearrange(
                        "p (t o i) -> p t o i", t=4, o=16), AX.X, ALU.add))

                multiplied = {}
                for i in range(TC // 4):
                    k = base + i
                    step(k)
                    V.wait(w_ready[k], reduced[i % 2])
                    multiplied[i] = vv(v.tensor_tensor(
                        pr1[i % 2].rearrange("p (t o i) -> p t o i", t=4, o=16),
                        psB[k % 3][:, :].rearrange("p (t o i) -> p t o i", t=4, o=16),
                        bc(gv[:, 4 * i:4 * i + 4, :], 2, 16), ALU.mult))
                    freeB[k % 3] = multiplied[i]
                    if i:
                        reduce(i - 1)
                reduce(TC // 4 - 1)
                free_g[c % 2] = multiplied[TC // 4 - 1]
                return sums(c, 16, lambda k: msg[:, :, k])

            for q in range(3):
                att_load(q)
            hidden(0)
            return messages1

        t2 = v3(prod[:, 0:NJ * 20], 20)

        def gru(rep):
            cat = v3(gb[:, 0:NJ * 32], 32)
            rz = v3(arena[:, 0:NJ * 32], 32)
            nn = v3(arena[:, NJ * 32:NJ * 48], 16)

            def gates(J, ex):
                vv(v.tensor_tensor(cat[:, J, 0:16], ex, bc(mask[:, J], 2, 16), ALU.mult))
                vv(v.tensor_copy(cat[:, J, 16:32], hv[:, J, :]))
                V.settle()
                vv(v.tensor_tensor(cat[:, J, 0:16], cat[:, J, 0:16], bc(invdeg[:, J], 2, 16), ALU.mult))

                def evac(j0, q, ps, m):
                    A.wait(m)
                    e = A.did(a.activation(rz[:, j0:j0 + q, :], ps[:, :, 0:32], ACT.Sigmoid))
                    V.wait(e)
                    vv(v.tensor_tensor(nn[:, j0:j0 + q, :], rz[:, j0:j0 + q, 0:16], ps[:, :, 48:64], ALU.mult))
                    V.settle()
                    return vv(v.tensor_tensor(nn[:, j0:j0 + q, :], nn[:, j0:j0 + q, :], ps[:, :, 32:48], ALU.add))

                node_product(lambda j: cat[:, j, :], 32, 2, xT32, gws[:, :], 64, evac, J)
                A.wait((V.sem, V.n))
                e = A.did(a.activation(nn[:, J, :], nn[:, J, :], ACT.Tanh))
                V.wait(e)
                vv(v.tensor_tensor(hv[:, J, :], hv[:, J, :], nn[:, J, :], ALU.subtract))
                V.settle()
                vv(v.tensor_tensor(hv[:, J, :], hv[:, J, :], rz[:, J, 16:32], ALU.mult))
                V.settle()
                vv(v.tensor_tensor(hv[:, J, :], hv[:, J, :], nn[:, J, :], ALU.add))
                if rep == 0:
                    st["ready"] = save(tab1[1], hcur, 16, J)
                    return
                V.settle()
                vv(v.tensor_tensor(wk[:, J, :], xv[:, J, :], hv[:, J, :], ALU.add))
                layernorm(xv, wk[:, J, :], J)
                vv(v.tensor_copy(t2[:, J, 0:16], xv[:, J, :]))
                vv(v.memset(t2[:, J, 19:20], 0.0))

                def logits(j0, q, ps, m):
                    V.wait(m)
                    vv(v.tensor_copy(t2[:, j0:j0 + q, 16:19], ps[:, :, 0:3]))
                    return vv(v.tensor_copy(xt12[:, j0:j0 + q, 0:3], ps[:, :, 3:6]))

                node_product(lambda j: xv[:, j, :], 16, 0, xT16, v1[:, :], 6, logits, J)
                self_logits(lg3[:, J, :], t2[:, J, 16:19], xt12[:, J, 0:3])
                save(tab2a, prod, 20, J)
                spread_block(J, XT, 12, xe2a)
                st["ready"] = save(xn2a, XT, 12, J)

            return gates

        def self_logits(dest, s, d):
            V.settle()
            vv(v.tensor_tensor(dest, s, d, ALU.add))
            V.settle()
            vv(v.scalar_tensor_tensor(dest, dest, 0.2, dest, ALU.mult, ALU.max))
            V.settle()

        def spread_block(J, tile, f, edges):
            G.wait((V.sem, V.n), m_zero)
            for j in range(J.start, J.stop):
                c_sct.did(pool.indirect_dma_start(
                    edges, bass.IndirectOffsetOnAxis(ap=stai[:, j:j + 1], axis=0), tile[:, j * f:(j + 1) * f], None,
                    bounds_check=EP - 1, oob_is_err=False))

        def spread_first(nodes, f, saved):
            G.wait(saved)
            return c_sct.did(pool.indirect_dma_start(x0[:, 0:f], None, nodes,
                                                     bass.IndirectOffsetOnAxis(ap=firsti, axis=0)))

        for rep in range(2):
            message_pass(1 + rep, tab1[rep], srci, 16, 16, S1[rep], message_net(rep), (st["ready"],))
            blocks(16, S1[rep], fix_sums(16, S1[rep]), gru(rep))

        def softmax_pass(k, table, H, D, width, dest, edges, ef, used, spread_done, ready, extra=None):
            f, w = H * (2 + D), 1 + D
            zz, d0, nb = sub[:, 0:TC * H], sub[:, TC * H:2 * TC * H], sub[:, 2 * TC * H:2 * TC * H + TC]
            da = sub[:, TC * 7:TC * (7 + 2 * H)]
            e, p = da[:, 0:TC * H], da[:, TC * H:2 * TC * H]
            xes = [arena[:, i * TC * 12:i * TC * 12 + TC * ef] for i in range(2)]
            exs = [arena[:, (2 + i) * TC * 12:(2 + i) * TC * 12 + TC * ef] for i in range(2)]
            ev = rows(edges, ef)
            m_xe = [None, None]

            def load(c):
                m_xe[c % 2] = c_xe[c % 2].did(sp.dma_start(v3(xes[c % 2], ef), ev[:, span(c), :]))

            S.wait((V.sem, V.n), (A.sem, A.n), (M.sem, M.n), spread_done)
            load(0)
            load(1)

            def messages(c):
                s = c % 2
                xe, xs, xo = v3(xes[s], ef), v3(exs[s], ef), v3(exs[1 - s], ef)
                gv, now, old = got(c, width), state(c, f), state(c + 1, f)
                pr = v3(prod[:, 0:TC * H * w], H * w)
                V.wait(m_xe[s], sent[s], spread_done)
                V.settle()
                for i in used:
                    m = vv(v.tensor_tensor_scan(xs[:, :, i], same[:, span(c)], xe[:, :, i],
                                                xo[:, TC - 1, i:i + 1] if c else x0[:, i:i + 1], ALU.mult, ALU.add))
                if c + 2 < NCH:
                    S.wait(m)
                    load(c + 2)
                vv(v.tensor_scalar(nb, same[:, span(c)], -1.0, BIG, ALU.add, ALU.mult))
                V.settle()
                vv(v.tensor_tensor(v3(zz, H), gv[:, :, D:D + H], xs[:, :, 0:H], ALU.add))
                if extra:
                    extra(c, xs)
                V.settle()
                vv(v.scalar_tensor_tensor(e, zz, 0.2, zz, ALU.mult, ALU.max))
                V.settle()
                for h in range(H):
                    vv(v.tensor_tensor_scan(now[:, :, h], nb, v3(e, H)[:, :, h], old[:, TC - 1, h:h + 1] if c else -BIG,
                                            ALU.add, ALU.max))
                V.settle()
                z3 = v3(zz, H)
                vv(v.tensor_tensor(z3[:, 1:TC, :], now[:, 0:TC - 1, 0:H], now[:, 1:TC, 0:H], ALU.subtract))
                if c:
                    vv(v.tensor_tensor(z3[:, 0, :], old[:, TC - 1, 0:H], now[:, 0, 0:H], ALU.subtract))
                else:
                    vv(v.memset(z3[:, 0, :], 0.0))
                vv(v.tensor_tensor(v3(p, H), v3(e, H), now[:, :, 0:H], ALU.subtract))
                V.settle()
                m = vv(v.tensor_scalar(e, zz, 0.0, None, ALU.min))
                A.wait(m)
                m = A.did(a.activation(da, da, ACT.Exp))
                V.wait(m)
                vv(v.tensor_tensor(v3(d0, H), v3(e, H), bc(same[:, span(c)], 2, H), ALU.mult))
                for h in range(H):
                    vv(v.tensor_copy(pr[:, :, h * w], v3(p, H)[:, :, h]))
                    free_g[s] = vv(v.tensor_tensor(pr[:, :, h * w + 1:(h + 1) * w], gv[:, :, 0:D],
                                                   bc(v3(p, H)[:, :, h], 2, D), ALU.mult))
                return sums(c, f, lambda i: pr[:, :, i - H], lambda i: v3(d0, H)[:, :, (i - H) // w], range(H, f))

            message_pass(k, table, srci, width, f, dest, messages, ready)

        def softmax_nodes(H, D, J, ex, logits, feats):
            f, w = H * (2 + D), 1 + D
            m, z = ex[:, :, 0:H], ex[:, :, H:f].rearrange("p j (h w) -> p j h w", w=w)
            o = J.start * 3 * H
            n = JB * H
            t = [v3(Sb[:, o + i * n:o + (i + 1) * n], H) for i in range(3)]
            V.settle()
            vv(v.tensor_tensor(ex, ex, bc(mask[:, J], 2, f), ALU.mult))
            V.settle()
            vv(v.tensor_tensor(m, m, bc(nmask[:, J], 2, H), ALU.add))
            V.settle()
            vv(v.tensor_tensor(t[0], m, logits, ALU.max))
            V.settle()
            vv(v.tensor_tensor(t[1], m, t[0], ALU.subtract))
            vv(v.tensor_tensor(t[2], logits, t[0], ALU.subtract))
            A.wait((V.sem, V.n))
            e = A.did(a.activation(Sb[:, o + n:o + 3 * n], Sb[:, o + n:o + 3 * n], ACT.Exp))
            tmp = [v3(Sb[:, NJ * 9 + h * JB * D:NJ * 9 + (h + 1) * JB * D], D) for h in range(H)]
            V.wait(e)
            for h in range(H):
                vv(v.tensor_tensor(z[:, :, h, :], z[:, :, h, :], bc(t[1][:, :, h], 2, w), ALU.mult))
                vv(v.tensor_tensor(tmp[h], feats, bc(t[2][:, :, h], 2, D), ALU.mult))
            V.settle()
            for h in range(H):
                vv(v.tensor_tensor(z[:, :, h, 0], z[:, :, h, 0], t[2][:, :, h], ALU.add))
                vv(v.tensor_tensor(z[:, :, h, 1:w], z[:, :, h, 1:w], tmp[h], ALU.add))
            V.settle()
            vv(v.tensor_scalar(t[0], z[:, :, :, 0], 1.0e-16, None, ALU.add))
            V.settle()
            vv(v.reciprocal(t[0], t[0]))
            V.settle()
            return z, t[0]

        def edge_weight(c, xs):
            oh = v3(prod[:, 0:TC * 8], 8)
            tc = typi[:, span(c)]
            vv(v.tensor_tensor(oh, bc(tc, 2, 8), bc(io8, 1, TC), ALU.is_equal))
            V.settle()
            vv(v.tensor_tensor(oh, oh, xs[:, :, 4:12], ALU.mult))
            vv(v.scalar_tensor_tensor(tc, srci[:, span(c)], 8.0, tc, ALU.mult, ALU.add))
            V.settle()
            vv(v.tensor_reduce(wE[:, span(c)], oh, AX.X, ALU.add))

        def selu(dest, src_ap, tmp):
            e = vv(v.tensor_scalar(tmp, src_ap, 0.0, None, ALU.min))
            A.wait(e)
            e = A.did(a.activation(tmp, tmp, ACT.Exp))
            vv(v.tensor_scalar(dest, src_ap, 0.0, SELU_S, ALU.max, ALU.mult))
            V.wait(e)
            vv(v.tensor_scalar(tmp, tmp, SELU_S * SELU_A, -SELU_S * SELU_A, ALU.mult, ALU.add))
            V.settle()
            return vv(v.tensor_tensor(dest, dest, tmp, ALU.add))

        spread_done = spread_first(xn2a, 12, st["ready"])
        softmax_pass(3, tab2a, 3, 16, 20, S2a, xe2a, 12, (0, 1, 2) + tuple(range(4, 12)), spread_done, (st["ready"],),
                     edge_weight)
        an = v3(arena[:, :], 48)
        t2b = v3(gb[:, 0:NJ * 36], 36)
        ad2t = XT[:, 0:NJ]
        hT = [prod[0:96, i * 512:(i + 1) * 512] for i in range(2)]
        hE = [prod[0:96, (2 + i) * 512:(3 + i) * 512] for i in range(2)]
        hT_used = [None, None]

        def nodes2a(J, ex):
            z, r = softmax_nodes(3, 16, J, ex, lg3[:, J, :], xv[:, J, :])
            for h in range(3):
                vv(v.tensor_tensor(an[:, J, 16 * h:16 * h + 16], z[:, :, h, 1:17], bc(r[:, :, h], 2, 16), ALU.mult))
            vv(v.memset(t2b[:, J, 33:36], 0.0))
            M.wait((V.sem, V.n), (A.sem, A.n))
            groups = [(j, min(4, J.stop - j)) for j in range(J.start, J.stop, 4)]
            for g, (j0, cnt) in enumerate(groups):
                s = g % 2
                M.wait(freeA[s])
                for i in range(cnt):
                    m = turned(psA[s], i * P, an[:, j0 + i, :], 48)
                A.wait(m, hT_used[s])
                freeA[s] = A.did(a.activation(xT48[0:48, s * 512:s * 512 + cnt * P], psA[s][0:48, 0:cnt * P], ACT.Copy))
                M.wait(freeA[s], freeB[0])
                m = M.did(pe.matmul(psB[0][0:96, 0:cnt * P], l2bs[:, :], xT48[0:49, s * 512:s * 512 + cnt * P],
                                    start=True, stop=True))
                V.wait(m, hT_used[s])
                freeB[0] = selu(hT[s][:, 0:cnt * P], psB[0][0:96, 0:cnt * P], hE[s][:, 0:cnt * P])
                b = 1 + s
                M.wait(freeB[0], freeB[b])
                for i in range(cnt):
                    m = M.did(pe.matmul(psB[b][:, i * 34:(i + 1) * 34], hT[s][:, i * P:(i + 1) * P], w2x[:, :],
                                        start=True, stop=True))
                hT_used[s] = m
                V.wait(m)
                pv = psB[b][:, 0:cnt * 34].rearrange("p (j w) -> p j w", w=34)
                vv(v.tensor_copy(t2b[:, j0:j0 + cnt, 0:33], pv[:, :, 0:33]))
                freeB[b] = vv(v.tensor_copy(ad2t[:, j0:j0 + cnt], pv[:, :, 33]))
            self_logits(lg1[:, J], t2b[:, J, 32], ad2t[:, J])
            save(tab2b, gb, 36, J)
            spread_block(J, XT, 1, xe2b)
            st["ready"] = save(xn2b, XT, 1, J)

        blocks(54, S2a, fix_softmax(3, 16, S2a), nodes2a)
        spread_done = spread_first(xn2b, 1, st["ready"])
        softmax_pass(4, tab2b, 1, 32, 36, S2b, xe2b, 1, (0,), spread_done, (st["ready"],))
        f32v = v3(gb[:, 0:NJ * 32], 32)
        S.wait((V.sem, V.n))
        m_feats = c_tab.did(sp.dma_start(f32v, tab2b.rearrange("(p j) f -> p j f", p=P)[:, :, 0:32]))
        h2 = v3(arena[:, 0:NJ * 32], 32)

        stage = [prod[:, i * 1024:(i + 1) * 1024] for i in range(2)]
        m_y = [None, None]
        turn = [0]

        def table3(inp, K, W, width, xT, table, J):
            tv = table.rearrange("(p j r) w -> p j (r w)", p=P, r=8)
            size = 1024 // (8 * width)

            def evac(j0, q, ps, m):
                at = (j0 - J.start) % size
                if at == 0:
                    turn[0] += 1
                b = turn[0] % 2
                V.wait(m, m_y[b])
                e = vv(v.tensor_copy(stage[b][:, at * 8 * width:(at + q) * 8 * width].rearrange("p (j w) -> p j w", j=q), ps))
                if at + q == size or j0 + q == J.stop:
                    S.wait(e)
                    m_y[b] = c_y[b].did(sp.dma_start(tv[:, j0 - at:j0 + q, :], stage[b][:, 0:(at + q) * 8 * width].rearrange(
                        "p (j w) -> p j w", w=8 * width)))
                return e

            node_product(inp, K, 0, xT, W, 8 * width, evac, J)

        def nodes2b(J, ex):
            V.wait(m_feats)
            z, r = softmax_nodes(1, 32, J, ex, lg1[:, J].unsqueeze(2), f32v[:, J, :])
            fv, hj = f32v[:, J, :], h2[:, J, :]
            vv(v.tensor_tensor(fv, z[:, :, 0, 1:33], bc(r[:, :, 0], 2, 32), ALU.mult))
            V.settle()
            vv(v.tensor_tensor(fv, fv, bc(b2b[:, :], 1, JB), ALU.add))
            V.settle()
            selu(hj, fv, ex[:, :, 0:32])

            def add_x(j0, q, ps, m):
                V.wait(m)
                return vv(v.tensor_tensor(hv[:, j0:j0 + q, :], ps, xv[:, j0:j0 + q, :], ALU.add))

            node_product(lambda j: h2[:, j, :], 32, 1, xT32, wfs[:, :], 16, add_x, J)
            layernorm(xv, hv[:, J, :], J)
            table3(lambda j: xv[:, j, :], 16, l3w1s[:, :], 32, xT16, tab3a, J)

        blocks(34, S2b, fix_softmax(1, 32, S2b), nodes2b)

        def messages3(width):
            def messages(c):
                V.settle()
                pr = v3(prod[:, 0:TC * width], width)
                free_g[c % 2] = vv(v.tensor_tensor(pr, got(c, width), bc(wE[:, span(c)], 2, width), ALU.mult))
                return sums(c, width, lambda k: pr[:, :, k])
            return messages

        h3 = v3(gb[:, 0:NJ * 32], 32)

        def nodes3(J, ex):
            vv(v.tensor_tensor(ex, ex, bc(mask[:, J], 2, 32), ALU.mult))
            V.settle()

            def add_root(j0, q, ps, m):
                V.wait(m)
                return vv(v.tensor_tensor(h3[:, j0:j0 + q, :], ps, ex[:, j0 - J.start:j0 - J.start + q, :], ALU.add))

            def add_root2(j0, q, ps, m):
                V.wait(m)
                return vv(v.tensor_tensor(hv[:, j0:j0 + q, :], ps, xv[:, j0:j0 + q, :], ALU.add))

            node_product(lambda j: xv[:, j, :], 16, 1, xT16, r1s[:, :], 32, add_root, J)
            V.settle()
            vv(v.tensor_scalar(h3[:, J, :], h3[:, J, :], 0.0, None, ALU.max))
            table3(lambda j: h3[:, j, :], 32, l3w2s[:, :], 16, xT32, tab3b, J)
            node_product(lambda j: h3[:, j, :], 32, 1, xT32, r2s[:, :], 16, add_root2, J)

        message_pass(5, tab3a, typi, 32, 32, S3a, messages3(32), tuple(m_y))
        blocks(32, S3a, fix_sums(32, S3a), nodes3)
        message_pass(6, tab3b, typi, 16, 16, S3b, messages3(16), tuple(m_y) + ((M.sem, M.n),))

        def nodes_out(J, ex):
            vv(v.tensor_tensor(ex, ex, bc(mask[:, J], 2, 16), ALU.mult))
            V.settle()
            vv(v.tensor_tensor(hv[:, J, :], hv[:, J, :], ex, ALU.add))
            layernorm(xv, hv[:, J, :], J)

        blocks(16, S3b, fix_sums(16, S3b), nodes_out)
        full = N // NJ
        S.wait((V.sem, V.n))
        c_fin.did(sp.dma_start(out[0:full * NJ, :].rearrange("(p j) f -> p (j f)", p=full), xcur[0:full, :]))
        m = c_fin.did(sp.dma_start(out[full * NJ:N, :].rearrange("(p j) f -> p (j f)", p=1),
                                   xcur[full:full + 1, 0:(N - full * NJ) * 16]))
        S.wait(m, *((c.sem, c.n) for c in [c_fix, c_srch, c_tab, c_set, c_zero, c_sct] + c_ext + c_out + c_y))


def kernel(**inputs):
    import numpy as np
    import concourse.bacc as bacc
    from concourse.bass_utils import run_bass_kernel_spmd as run

    i = {k: np.asarray(v) for k, v in inputs.items()}

    def padded(a, fill):
        return np.concatenate([a, np.full((EP - E,) + a.shape[1:], fill, a.dtype)])

    d = padded(i["dst"], N)
    f32 = np.float32
    z = lambda *s: np.zeros(s, f32)
    consts = np.concatenate([np.eye(P, dtype=f32), np.arange(0, EP, T, dtype=f32)[:, None],
                             np.broadcast_to(np.arange(8, dtype=f32), (P, 8)),
                             np.arange(NP, dtype=f32).reshape(P, NJ)], 1)
    ih, hh = i["L1_gnn_gru_w_ih"].T, i["L1_gnn_gru_w_hh"].T
    bi, bh = i["L1_gnn_gru_b_ih"][None], i["L1_gnn_gru_b_hh"][None]
    gru = np.concatenate([np.concatenate([ih, z(16, 16)], 1),
                          np.concatenate([hh[:, 0:32], z(16, 16), hh[:, 32:48]], 1),
                          np.concatenate([bi, z(1, 16)], 1),
                          np.concatenate([bh[:, 0:32], z(1, 16), bh[:, 32:48]], 1)])
    oi = lambda a: a.reshape(-1, 16, 16).transpose(0, 2, 1).reshape(-1, 256)
    fw, fb, one = i["L1_gnn_fnet_w1"], i["L1_gnn_fnet_b1"], np.ones(1, f32)
    f2 = np.concatenate([oi(i["L1_gnn_fnet_w2"]), oi(i["L1_gnn_fnet_b2"])])
    w1 = i["L2_gnn_W1"]
    blk = z(49, 96)
    for h in range(3):
        blk[16 * h:16 * h + 16, 32 * h:32 * h + 32] = w1[:, 32 * h:32 * h + 32]
    blk[48] = i["L2_gnn_b1"]
    arrays = {
        "x": np.concatenate([i["x"], z(NP - N, 16)]),
        "src": padded(i["src"], 0).reshape(P, T), "dst": d.reshape(P, T),
        "prv": np.concatenate([np.full(1, -1, d.dtype), d[:-1]]).reshape(P, T),
        "attrT": padded(i["edge_attr_13"], 0).reshape(P, T // 8, 2, 4, 13).transpose(2, 4, 1, 3, 0).reshape(26, EP // 2),
        "typ": padded(i["edge_type_8"], 0).reshape(P, T), "ew": padded(i["edge_weight"], 0).reshape(P, T),
        "consts": consts, "l0w": i["L0_gnn_weight"], "l0s": i["L0_gnn_self_loop_weight"].reshape(1),
        "w1": np.concatenate([np.concatenate([fw, z(13, 96)], 1), np.concatenate([z(13, 64), fw, z(13, 32)], 1)]),
        "b1": np.concatenate([fb, one, z(31), fb, one, z(31)]).reshape(P, 1),
        "w2a": np.concatenate([f2, z(31, 256), f2]), "gw": gru,
        "l2w": w1, "l2blk": blk, "as1": i["L2_gnn_a_src1"].reshape(96), "ad1": i["L2_gnn_a_dst1"].reshape(96),
        "w2s": i["L2_gnn_W2"], "as2": i["L2_gnn_a_src2"].reshape(32), "ad2": i["L2_gnn_a_dst2"].reshape(32),
        "b2": i["L2_gnn_b2"], "wf": np.concatenate([i["L2_gnn_Wf"], i["L2_gnn_bf"][None]]),
        "l3w1": i["L3_gnn_W1"].transpose(1, 0, 2).reshape(16, 256),
        "root1": np.concatenate([i["L3_gnn_root1"], i["L3_gnn_b1"][None]]),
        "l3w2": i["L3_gnn_W2"].transpose(1, 0, 2).reshape(32, 128),
        "root2": np.concatenate([i["L3_gnn_root2"], i["L3_gnn_b2"][None]]),
    }
    arrays = {k: np.ascontiguousarray(v) for k, v in arrays.items()}
    nc = bacc.Bacc("TRN2", target_bir_lowering=False, num_devices=1)
    args = [nc.dram_tensor("in_" + k, v.shape, mybir.dt.from_np(v.dtype), kind="ExternalInput").ap() for k, v in arrays.items()]
    out = nc.dram_tensor("out", (N, 16), F32, kind="ExternalOutput").ap()
    gnn_program(nc, *args, out)
    r = run(nc, [{"in_" + k: v for k, v in arrays.items()}], core_ids=[0])
    return r.results[0]["out"]
```

```python
from contextlib import ExitStack

import concourse.bass as bass
from concourse import mybir

F32 = mybir.dt.float32
I32 = mybir.dt.int32
BF16 = mybir.dt.bfloat16
F16 = mybir.dt.float16
ALU = mybir.AluOpType
ACT = mybir.ActivationFunctionType
AX = mybir.AxisListType

N, E = 12500, 412500
P = 128
NJ = 98
NP = P * NJ
T = 3224
EP = P * T
TC = 52
NCH = T // TC
NS, SW = 62, 52
BIG = 1.0e30
NB = 7
JB = NJ // NB
SELU_A, SELU_S = 1.6732632423543772, 1.0507009873554805
CI, CB, C8, CN = 0, 128, 129, 137
CG, CJ = CN + NJ, CN + NJ + NB
CW = CJ + JB
KM = 18
KT = KM * NCH
OFF = (16, 6, 6, 12, 10, 14, 10)
ROUND = 12582912.0


class Queue:

    def __init__(self, eng, sem):
        self.eng, self.sem, self.n, self.seen = eng, sem, 0, {}

    def wait(self, *marks):
        for m in marks:
            if m is not None and self.seen.get(id(m[0]), 0) < m[1]:
                self.eng.wait_ge(m[0], m[1])
                self.seen[id(m[0])] = m[1]

    def did(self, ins):
        ins.then_inc(self.sem, 1)
        self.n += 1
        return self.sem, self.n

    def settle(self):
        self.wait((self.sem, self.n) if self.n else None)


class Chan:

    def __init__(self, sem):
        self.sem, self.n = sem, 0

    def did(self, ins):
        ins.then_inc(self.sem, 16)
        self.n += 16
        return self.sem, self.n


def gnn_program(nc, x, src, srcT, dst, prv, attrT, typ, ew, consts, l0w, l0s, w1, b1, w2a, gw, l2w, l2blk, as1, ad1, w2s, as2, ad2,
                b2, wf, l3w1, root1, l3w2, root2, out):
    with ExitStack() as ctx:
        def sb(name, shape, dt=F32):
            return ctx.enter_context(nc.sbuf_tensor(name, shape, dt))

        def sem(name):
            return ctx.enter_context(nc.semaphore(name))

        def dram(name, shape, dt=F32):
            return nc.dram_tensor(name, shape, dt).ap()

        V = Queue(nc.vector, sem("s_vec"))
        A = Queue(nc.scalar, sem("s_act"))
        M = Queue(nc.tensor, sem("s_pe"))
        G = Queue(nc.gpsimd, sem("s_pool"))
        S = Queue(nc.sync, None)
        v, a, pe, pool, sp = nc.vector, nc.scalar, nc.tensor, nc.gpsimd, nc.sync

        srci = sb("srci", [P, T], I32)
        typi = sb("typi", [P, T], I32)
        same = sb("same", [P, T])
        wE = sb("wE", [P, T])
        dsti = wE[:, :].bitcast(I32)
        gb = sb("gb", [P, 2 * TC * 36])
        prod = sb("prod", [P, 2944])
        Sb = sb("Sb", [P, 2 * TC * 56])
        ext = sb("ext", [P, NJ * 54])
        exti = ext[:, :].bitcast(I32)
        arena = sb("arena", [P, NJ * 48])
        xcur = sb("xcur", [P, NJ * 16])
        hcur = sb("hcur", [P, NJ * 16])
        XT = sb("XT", [P, NJ * 12])
        zero = XT[:, 0:TC * 12]
        lg = sb("lg", [P, NJ * 4])
        hid = sb("hid", [P, 2 * 512])
        xT16 = sb("xT16", [P, 2 * 512])
        xT32 = sb("xT32", [P, 2 * 512])
        xT48 = sb("xT48", [P, 2 * 512])
        ewc = sb("ewc", [P, 2 * TC])
        sub = sb("sub", [P, TC * 22])
        cst = sb("cst", [P, CW])
        xp = sb("xp", [P, NJ * 24])
        hlk = sb("hlk", [P, KT], BF16)
        hm = sb("hm", [P, KM * JB])
        w1s = sb("w1s", [26, P])
        b1s = sb("b1s", [P, 1])
        w2as = sb("w2as", [P, 512])
        gws = sb("gws", [34, 64])
        l0wb = sb("l0wb", [P, 16])
        l0sb = sb("l0sb", [P, 1])
        l2ws = sb("l2ws", [16, 96])
        l2bs = sb("l2bs", [49, 96])
        avec = sb("avec", [16, 2 * 96])
        a2vec = sb("a2vec", [96, 64])
        vtmp = sb("vtmp", [96, 96])
        v1 = sb("v1", [16, 6])
        w2x = sb("w2x", [96, 34])
        b2b = sb("b2b", [P, 32])
        wfs = sb("wfs", [33, 16])
        l3w1s = sb("l3w1s", [16, 256])
        r1s = sb("r1s", [17, 32])
        l3w2s = sb("l3w2s", [32, 128])
        r2s = sb("r2s", [33, 16])
        endi = sb("endi", [P, NJ], I32)
        stai = sb("stai", [P, NJ], I32)
        fndi = sb("fndi", [P, NJ], I32)
        mask = sb("mask", [P, NJ])
        nmask = sb("nmask", [P, NJ])
        invdeg = sb("invdeg", [P, NJ])
        nt = sb("nt", [P, 4 * NJ])
        pcol = sb("pcol", [P, 8])
        pcoi = sb("pcoi", [P, 2], I32)
        contT = sb("contT", [64, P])
        nbT = sb("nbT", [4, P])
        fx = sb("fx", [P, 640])
        fC = sb("fC", [P, 129])
        fM = sb("fM", [4, 129])
        x0 = sb("x0", [P, 24])

        psA = [ctx.enter_context(nc.psum_tensor(f"psA{i}", [P, 512], F32)) for i in range(2)]
        psB = [ctx.enter_context(nc.psum_tensor(f"psB{i}", [P, 1024], F32)) for i in range(3)]
        freeA, freeB = [None, None], [None, None, None]

        first_d = dram("first_d", [P, 1], I32)
        samp_d = dram("samp_d", [P, NS], I32)
        cont_d = dram("cont_d", [P, 1])
        end_d = dram("end_d", [NP + 1])
        S0 = dram("S0", [EP, 24])
        S1 = [dram("S1a", [EP, 16]), dram("S1b", [EP, 16])]
        S2a = dram("S2a", [EP, 54])
        S2b = dram("S2b", [EP, 34])
        S3a = dram("S3a", [EP, 32])
        S3b = dram("S3b", [EP, 16])
        tab1 = [dram("tab1a", [NP, 16]), dram("tab1b", [NP, 16])]
        tab2a = dram("tab2a", [NP, 20])
        tab2b = dram("tab2b", [NP, 36])
        tab3a = dram("tab3a", [NP * 8, 32])
        tab3b = dram("tab3b", [NP * 8, 16])
        xn2a = dram("xn2a", [NP, 12])
        xn2b = dram("xn2b", [NP, 1])
        xe2a = dram("xe2a", [EP, 12])
        xe2b = dram("xe2b", [EP, 1])
        key_d = dram("key_d", [NCH, KM * P], F16)

        c_src, c_dst, c_prv, c_typ, c_w = (Chan(sem(f"c_{n}")) for n in ("src", "dst", "prv", "typ", "w"))
        c_ew = [Chan(sem(f"c_ew{i}")) for i in range(2)]
        c_att = [Chan(sem(f"c_att{i}")) for i in range(3)]
        c_out = [Chan(sem(f"c_out{i}")) for i in range(2)]
        c_xe = [Chan(sem(f"c_xe{i}")) for i in range(2)]
        c_y = [Chan(sem(f"c_y{i}")) for i in range(2)]
        c_fix, c_srch, c_tab, c_set, c_zero, c_sct, c_fin = (Chan(sem(f"c_{n}")) for n in
                                                            ("fix", "srch", "tab", "set", "zero", "sct", "fin"))
        c_key = [Chan(sem(f"c_key{i}")) for i in range(2)]
        c_kd = Chan(sem("c_kd"))
        c_ext = [Chan(sem(f"c_ext{i}")) for i in range(NB)]
        c_g = [[Chan(sem(f"c_g{k}_{i}")) for i in range(2)] for k in range(7)]

        ident = cst[:, CI:CI + P]
        pbase = cst[:, CB:CB + 1]
        io8 = cst[:, C8:C8 + 8]
        nid = cst[:, CN:CN + NJ]
        io14 = cst[:, CJ:CJ + JB]

        def rows(d, f):
            return d.rearrange("(p t) f -> p t f", p=P)

        def v3(t, f):
            return t.rearrange("p (t f) -> p t f", f=f)

        def bc(ap, axis, n):
            ap = ap.unsqueeze(axis)
            shape = list(ap.shape)
            shape[axis] = n
            return ap.to_broadcast(shape)

        def vv(ins):
            return V.did(ins)

        m_src = c_src.did(sp.dma_start(srci[:, :], src))
        m_dst = c_dst.did(sp.dma_start(dsti, dst))
        m_prv = c_prv.did(sp.dma_start(typi[:, :], prv))
        for t, d in ((cst[:, :], consts), (w1s[:, :], w1), (b1s[:, :], b1), (w2as[:, :], w2a), (gws[:, :], gw),
                     (l0wb[:, :], l0w.partition_broadcast(P)), (l0sb[:, :], l0s.partition_broadcast(P)),
                     (l2ws[:, :], l2w), (l2bs[:, :], l2blk),
                     (avec[:, 0:96], as1.partition_broadcast(16)), (avec[:, 96:192], ad1.partition_broadcast(16)),
                     (a2vec[:, 0:32], as2.partition_broadcast(96)), (a2vec[:, 32:64], ad2.partition_broadcast(96)),
                     (w2x[:, 0:32], w2s), (b2b[:, :], b2.partition_broadcast(P)), (wfs[:, :], wf),
                     (l3w1s[:, :], l3w1), (r1s[:, :], root1), (l3w2s[:, :], l3w2), (r2s[:, :], root2),
                     (xcur[:, :], x.rearrange("(p j) f -> p (j f)", p=P))):
            m_w = c_w.did(a.dma_start(t, d))

        m_z = vv(v.memset(zero, 0.0))
        for t in (xT16, xT32):
            vv(v.memset(t[:, :], 1.0))
        vv(v.memset(hid[:, :], 1.0))
        vv(v.memset(fC[:, :], 0.0))
        vv(v.memset(fM[:, :], -BIG))
        vv(v.memset(pcol[:, 7:8], -1.0))
        V.wait(m_dst, m_prv, m_w)
        m_same = vv(v.tensor_tensor(same[:, :], dsti, typi[:, :], ALU.is_equal))
        samp = hcur[:, 0:NS].bitcast(I32)
        m_samp = vv(v.tensor_copy(samp, wE[:, 0:T:SW].bitcast(I32)))
        firstf, contc, cntf, fixf = (pcol[:, i:i + 1] for i in range(4))
        vv(v.tensor_copy(firstf, dsti[:, 0:1]))
        vv(v.tensor_copy(pcoi[:, 0:1], dsti[:, 0:1]))
        V.settle()
        vv(v.tensor_tensor(contc, firstf, dsti[:, T - 1:T], ALU.is_equal))
        junk = Sb[:, 0:T]
        vv(v.tensor_scalar(junk, dsti, firstf, None, ALU.is_equal))
        V.settle()
        samep = same[:, 0:1]
        vv(v.tensor_tensor(contc, contc, samep, ALU.mult))
        vv(v.tensor_reduce(cntf, junk, AX.X, ALU.add))
        V.settle()
        vv(v.scalar_tensor_tensor(fixf, cntf, -1.0, pbase, ALU.add, ALU.add))
        vv(v.tensor_scalar(pcol[:, 4:5], samep, -1.0, BIG, ALU.add, ALU.mult))
        V.settle()
        m_fix = vv(v.tensor_copy(pcoi[:, 1:2], fixf))
        nsamep = pcol[:, 4:5]
        firsti, fixi = pcoi[:, 0:1], pcoi[:, 1:2]
        S.wait(m_fix, m_samp)
        c_set.did(sp.dma_start(samp_d, samp))
        c_set.did(sp.dma_start(cont_d, contc))
        m_s1 = c_set.did(sp.dma_start(first_d, firsti))
        c_zero.did(sp.dma_start(end_d[0:1].unsqueeze(0), pcol[0:1, 7:8]))
        m_typ = None

        S.wait(m_s1, m_z)
        fr = fx[:, 0:P].bitcast(I32)
        c_set.did(sp.dma_start(fr, first_d.rearrange("p o -> o p")[0].partition_broadcast(P)))
        m_s2 = c_set.did(sp.dma_start(contT[:, :], cont_d.rearrange("p o -> o p")[0].partition_broadcast(64)))
        S.wait(m_same)
        m_typ = c_typ.did(sp.dma_start(typi[:, :], typ))
        for k in range(NCH):
            c_zero.did(sp.dma_start(rows(xe2a, 12)[:, k * TC:(k + 1) * TC, :], v3(zero, 12)))
        xe2bv = xe2b.rearrange("(p t) f -> p (t f)", p=P)
        for k in range(0, T, TC * 12):
            n = min(TC * 12, T - k)
            m_zero = c_zero.did(sp.dma_start(xe2bv[:, k:k + n], zero[:, 0:n]))

        V.wait(m_s2)
        vv(v.tensor_scalar(nbT[:, :], contT[0:4, :], -1.0, BIG, ALU.add, ALU.mult))
        rank, blk, cum = nt[:, 0:NJ], nt[:, NJ:2 * NJ], nt[:, 2 * NJ:3 * NJ]

        def count_le(dest, j0, nj, width, vals):
            cmp = v3(arena[:, 0:nj * width], width)
            V.settle()
            vv(v.tensor_tensor(cmp, vals, bc(nid[:, j0:j0 + nj], 2, width), ALU.is_le))
            V.settle()
            return vv(v.tensor_reduce(dest[:, j0:j0 + nj], cmp, AX.X, ALU.add))

        def search1():
            for j0 in range(0, NJ, 14):
                count_le(rank, j0, 14, P, bc(fr, 1, 14))
            V.settle()
            vv(v.tensor_scalar(rank, rank, -1.0, 0.0, ALU.add, ALU.max))
            V.settle()
            return vv(v.tensor_copy(fndi[:, :], rank))

        HALF = NJ // 2

        def rows_of(table, width, half, ready):
            G.wait(*ready)
            for j in range(HALF):
                m = c_srch.did(pool.indirect_dma_start(
                    exti[:, j * width:(j + 1) * width], None, table,
                    bass.IndirectOffsetOnAxis(ap=fndi[:, half * HALF + j:half * HALF + j + 1], axis=0)))
            return m

        def count_rows(dest, width, half, arrived):
            V.wait(arrived)
            for j in range(0, HALF, 7):
                m = count_le(dest, half * HALF + j, 7, width, v3(exti[:, j * width:(j + 7) * width], width))
            return m

        def search_blocks(half_marks):
            V.settle()
            vv(v.scalar_tensor_tensor(blk, rank, float(NS), blk, ALU.mult, ALU.add))
            V.settle()
            vv(v.tensor_scalar(blk, blk, -1.0, 0.0, ALU.add, ALU.max))
            V.settle()
            return vv(v.tensor_copy(fndi[:, :], blk))

        def search_ends():
            V.settle()
            vv(v.scalar_tensor_tensor(cum, blk, float(SW), cum, ALU.mult, ALU.add))
            V.settle()
            e = vv(v.tensor_scalar(cum, cum, -1.0, None, ALU.add))
            S.wait(e)
            m = c_set.did(sp.dma_start(end_d[1:NP + 1].rearrange("(p j) -> p j", p=P), cum))
            S.wait(m, m_zero)
            m = c_set.did(sp.dma_start(nt[:, 3 * NJ:4 * NJ], end_d[0:NP].rearrange("(p j) -> p j", p=P)))
            V.wait(m)
            before = nt[:, 3 * NJ:4 * NJ]
            vv(v.tensor_tensor(mask[:, :], cum, before, ALU.subtract))
            vv(v.tensor_scalar(rank, cum, 0.0, None, ALU.max))
            V.settle()
            vv(v.tensor_scalar(mask[:, :], mask[:, :], 1.0, None, ALU.min))
            vv(v.tensor_copy(endi[:, :], rank))
            V.settle()
            vv(v.tensor_scalar(blk, mask[:, :], -1.0e6, 1.0e6 + 1.0, ALU.mult, ALU.add))
            vv(v.tensor_scalar(nmask[:, :], mask[:, :], -1.0, BIG, ALU.add, ALU.mult))
            V.settle()
            vv(v.tensor_tensor(blk, blk, before, ALU.add))
            V.settle()
            return vv(v.tensor_copy(stai[:, :], blk))

        def node_parts(tile_i, q, b, r):
            vv(v.tensor_copy(r, tile_i))
            V.settle()
            vv(v.tensor_scalar(q, r, 0.5 - NJ / 2, 1.0 / NJ, ALU.add, ALU.mult))
            V.settle()
            vv(v.tensor_scalar(q, q, ROUND, None, ALU.add))
            V.settle()
            vv(v.tensor_scalar(q, q, -ROUND, None, ALU.add))
            V.settle()
            vv(v.scalar_tensor_tensor(r, q, -float(NJ), r, ALU.mult, ALU.add))
            V.settle()
            vv(v.tensor_scalar(b, r, 0.5 - JB / 2, 1.0 / JB, ALU.add, ALU.mult))
            V.settle()
            vv(v.tensor_scalar(b, b, ROUND, None, ALU.add))
            V.settle()
            vv(v.tensor_scalar(b, b, -ROUND, None, ALU.add))
            V.settle()

        def pick_keys():
            n_i = Sb[:, 0:KT].bitcast(I32)
            q, b, r = (Sb[:, (i + 1) * KT:(i + 2) * KT] for i in range(3))
            k16 = Sb[:, 4 * KT:4 * KT + KT // 2].bitcast(F16)
            m = c_kd.did(sp.dma_start(n_i, srcT))
            V.wait(m, m_src)
            node_parts(n_i, q, b, r)
            e = vv(v.scalar_tensor_tensor(k16, b, float(P), q, ALU.mult, ALU.add))
            S.wait(e)
            m = c_kd.did(sp.dma_start(key_d.rearrange("c k -> (c k)").rearrange("(p k) -> p k", p=P), k16))
            vv(v.tensor_copy(v3(n_i, KM), v3(srci[:, :], TC)[:, :, TC - KM:TC]))
            V.settle()
            node_parts(n_i, q, b, r)
            vv(v.scalar_tensor_tensor(hlk[:, :], b, -float(JB), r, ALU.mult, ALU.add))
            return m

        def split(J, val, F, part):
            g = J.start // JB
            tmp = fx[:, 128:128 + JB * F]
            p1, p2, p3 = (part(g, i) for i in range(3))
            V.settle()
            vv(v.tensor_copy(v3(p1, F), val))
            V.settle()
            vv(v.tensor_tensor(v3(tmp, F), val, v3(p1, F), ALU.subtract))
            V.settle()
            vv(v.tensor_copy(p2, tmp))
            V.settle()
            return vv(v.tensor_tensor(p3, tmp, p2, ALU.subtract))

        def parts(base, stride, F):
            tile = base.bitcast(BF16)
            return lambda g, i: tile[:, g * stride + i * JB * F:g * stride + (i + 1) * JB * F]

        p3b = parts(arena[:, :], 96 * JB, 32)
        xp16 = parts(xp[:, :], 48 * JB, 16)
        p2a = parts(ext[:, NJ * 16:NJ * 46], 60 * JB, 20)
        p2b = parts(ext[:, :], 108 * JB, 33)

        def picker(k, F, part, scratch, slots, typed=None):
            n_off, W = OFF[k], JB * F
            pairs = n_off // 2
            OH = [scratch[:, i * 896:(i + 1) * 896].bitcast(BF16).rearrange("p (g e) -> p g e", g=NB) for i in range(2)]
            keys = [scratch[:, 1792 + i * P:1792 + (i + 1) * P].bitcast(F16) for i in range(2)]
            picked = xT48[:, 0:2 * W].rearrange("p (u j f) -> p u j f", u=2, f=F)
            arrived, coded, placed = {}, {}, {}

            def load(n, c, i):
                S.wait(coded.get(n - 2), m_key)
                o = (KM - n_off + 2 * i) * P
                arrived[n] = c_key[n % 2].did(sp.dma_start(keys[n % 2], key_d[c, o:o + 2 * P].partition_broadcast(P)))

            def code(n):
                V.wait(arrived[n], placed.get(n - 2))
                for g in range(NB):
                    coded[n] = vv(v.tensor_scalar(OH[n % 2][:, g, :], keys[n % 2], cst[:, CG + g:CG + g + 1], None, ALU.is_equal))

            def product(n, us=(0, 1), after=None):
                b = slots[n % len(slots)]
                M.wait(coded[n], freeB[b] if after is None else after)
                for u in us:
                    for g in range(NB):
                        for i in range(3):
                            m = M.did(pe.matmul(psB[b][:, u * 512:u * 512 + W], OH[n % 2][:, g, u * P:(u + 1) * P], part(g, i),
                                                start=g == 0 and i == 0, stop=g == NB - 1 and i == 2))
                    placed[n, u] = m
                placed[n] = m

            def keep(n, i, us=slice(0, 2)):
                b = slots[n % len(slots)]
                V.wait(placed[n, us.stop - 1])
                V.settle()
                freeB[b] = vv(v.tensor_tensor(
                    picked[:, us], psB[b][:, :].rearrange("p (u w) -> p u w", u=2)[:, us, 0:W].rearrange("p u (j f) -> p u j f", f=F),
                    bc(v3(hm[:, 0:n_off * JB], JB)[:, 2 * i + us.start:2 * i + us.stop, :], 3, F), ALU.mult))
                return freeB[b]

            def spot(c, i, width):
                return got(c, width)[:, TC - n_off + 2 * i:TC - n_off + 2 * i + 2, :]

            def place(c, i, width):
                V.settle()
                vv(v.tensor_reduce(spot(c, i, width)[:, :, 0:F], picked.rearrange("p u j f -> p u f j"), AX.X, ALU.add))

            last = NCH * pairs

            def begin(n):
                code(n)
                if n + 2 < last:
                    load(n + 2, (n + 2) // pairs, (n + 2) % pairs)

            def masks(c):
                V.settle()
                vv(v.tensor_tensor(v3(hm[:, 0:n_off * JB], JB), bc(hlk[:, (c + 1) * KM - n_off:(c + 1) * KM], 2, JB),
                                   bc(io14, 1, n_off), ALU.is_equal))

            def typed_steps(width):
                mats, xT, extra = typed
                of_type = v3(extra[:, 0:8 * n_off], 8)
                tcol = extra[:, 8 * n_off:9 * n_off]
                nodes = [extra[:, 200 + i * 2 * F:200 + (i + 1) * 2 * F] for i in range(2)]
                prods = extra[:, 328:328 + 16 * width]
                turn_done, copied, done = {}, {}, {}
                for n in range(last + 3):
                    if n < last:
                        begin(n)
                        product(n)
                    if n >= 3:
                        c, i = divmod(n - 3, pairs)
                        if i == 0:
                            tail = slice((c + 1) * TC - n_off, (c + 1) * TC)
                            V.settle()
                            vv(v.scalar_tensor_tensor(tcol, srci[:, tail], -8.0, typi[:, tail], ALU.mult, ALU.add))
                            V.settle()
                            vv(v.tensor_tensor(of_type, bc(tcol, 2, 8), bc(io8, 1, n_off), ALU.is_equal))
                        V.wait(done[n - 3])
                        V.settle()
                        freeA[1] = vv(v.tensor_tensor(
                            prods.rearrange("p (u r f) -> p u r f", u=2, r=8),
                            psA[1][:, 0:16 * width].rearrange("p (u r f) -> p u r f", u=2, r=8),
                            bc(of_type[:, 2 * i:2 * i + 2, :], 3, width), ALU.mult))
                        V.settle()
                        vv(v.tensor_reduce(spot(c, i, width), prods.rearrange("p (u r f) -> p u f r", u=2, r=8),
                                           AX.X, ALU.add))
                    if 1 <= n <= last:
                        c, i = divmod(n - 1, pairs)
                        if i == 0:
                            masks(c)
                        keep(n - 1, i)
                        V.wait(turn_done.get(n - 3))
                        V.settle()
                        m = vv(v.tensor_reduce(v3(nodes[n % 2], F), picked.rearrange("p u j f -> p u f j"), AX.X, ALU.add))
                    if 2 <= n <= last + 1:
                        M.wait(copied[n - 2], freeA[1])
                        o = (n % 2) * 512
                        for u in range(2):
                            done[n - 2] = M.did(pe.matmul(psA[1][:, 8 * width * u:8 * width * (u + 1)],
                                                          xT[0:F, o + u * P:o + (u + 1) * P], mats, start=True, stop=True))
                    if 1 <= n <= last:
                        M.wait(m, freeA[0])
                        for u in range(2):
                            turn_done[n - 1] = turned(psA[0], u * P, nodes[n % 2][:, u * F:(u + 1) * F], F)
                        A.wait(turn_done[n - 1], done.get(n - 3))
                        o = ((n - 1) % 2) * 512
                        copied[n - 1] = freeA[0] = A.did(a.activation(xT[0:F, o:o + 2 * P], psA[0][0:F, 0:2 * P], ACT.Copy))
                    yield

            def plain_steps(width):
                halves = [slice(0, 2)] if len(slots) > 1 else [slice(0, 1), slice(1, 2)]
                for n in range(last + 1):
                    c, i = divmod(n - 1, pairs)
                    if n < last:
                        begin(n)
                        if len(slots) > 1:
                            product(n)
                    if n and i == 0:
                        masks(c)
                    for us in halves:
                        done = keep(n - 1, i, us) if n else None
                        if n < last and len(slots) == 1:
                            product(n, range(us.start, us.stop), done)
                        if us.stop == 2 and n:
                            place(c, i, width)
                        yield

            def run(width):
                S.wait((V.sem, V.n), (M.sem, M.n))
                for i in range(2):
                    load(i, 0, i)
                yield from typed_steps(width) if typed else plain_steps(width)

            return run, pairs, 3 if typed else 1, 2 if len(slots) == 1 else 1

        class Steps:

            def __init__(self, picker, width):
                run, self.pairs, self.lag, self.per = picker
                self.gen, self.done, self.c = run(width), 0, -1

            def chunk(self, c):
                return (min(c + 1, NCH) * self.pairs + self.lag) * self.per

            def at(self, f):
                lo, hi = self.chunk(self.c) if self.c >= 0 else 0, self.chunk(self.c + 1)
                while self.done < lo + f * (hi - lo):
                    self.done += 1
                    next(self.gen)

            def share(self):
                lo, hi = self.chunk(self.c), self.chunk(self.c + 1)
                return (self.done - lo) / (hi - lo) if hi > lo else 1.0

        steps = [None]

        def between(f):
            steps[0].at(f)

        free_g = [None, None]
        sent = [None, None]

        def gather(k, table, idx, width, c, ready):
            s = c % 2
            G.wait(free_g[s], *ready)
            for i in range(TC - OFF[k]):
                t = c * TC + i
                o = s * TC * 36 + i * width
                m = c_g[k][s].did(pool.indirect_dma_start(
                    gb[:, o:o + width], None, table, bass.IndirectOffsetOnAxis(ap=idx[:, t:t + 1], axis=0)))
            return m

        def got(c, width):
            o = (c % 2) * TC * 36
            return v3(gb[:, o:o + TC * width], width)

        def state(c, f):
            o = (c % 2) * TC * 56
            return v3(Sb[:, o:o + TC * f], f)

        def put(c, f, dest, done):
            S.wait(done)
            sent[c % 2] = c_out[c % 2].did(sp.dma_start(rows(dest, f)[:, c * TC:(c + 1) * TC, :], state(c, f)))

        def span(c):
            return slice(c * TC, (c + 1) * TC)

        def sums(c, f, data, decay=None, cols=None):
            V.wait(sent[c % 2])
            V.settle()
            now, old = state(c, f), state(c + 1, f)
            cols = cols or range(f)
            done = steps[0].share()
            for i, k in enumerate(cols):
                between(done + (0.9 - done) * i / len(cols))
                init = old[:, TC - 1, k:k + 1] if c else 0.0
                d0 = same[:, span(c)] if decay is None else decay(k)
                m = vv(v.tensor_tensor_scan(now[:, :, k], d0, data(k), init, ALU.mult, ALU.add))
            return m

        def message_pass(k, table, idx, width, f, dest, messages, ready, pick, hooks=None):
            arrived = {}
            for c in range(2):
                arrived[c] = gather(k, table, idx, width, c, ready)
            steps[0] = Steps(pick, width)
            between(1)
            for c in range(NCH):
                V.wait(arrived[c])
                steps[0].c = c
                done = messages(c)
                put(c, f, dest, done)
                if c + 2 < NCH:
                    arrived[c + 2] = gather(k, table, idx, width, c + 2, ready)
                if hooks and c in hooks:
                    hooks[c]()
                between(1)

        def turned(dst_ps, col, inp, width):
            return M.did(pe.transpose(dst_ps[0:width, col:col + P], inp, ident))

        def to_rows(f, final, out_cols):
            M.wait(freeA[0], (V.sem, V.n))
            m = turned(psA[0], 0, final, f)
            V.wait(m)
            freeA[0] = vv(v.tensor_copy(fx[0:f, out_cols:out_cols + P], psA[0][0:f, 0:P]))

        def to_cols(f, rows_ap, dest):
            M.wait(freeA[1], (V.sem, V.n))
            m = M.did(pe.transpose(psA[1][0:P, 0:f], rows_ap, ident[0:f, 0:f]))
            V.wait(m)
            freeA[1] = vv(v.tensor_copy(dest, psA[1][0:P, 0:f]))

        W0 = 256

        def fix_gather(f, dest):
            row = fx[:, W0:W0 + f]
            G.wait(sent[0], sent[1], m_fix, (V.sem, V.n))
            return c_fix.did(pool.indirect_dma_start(row, None, dest, bass.IndirectOffsetOnAxis(ap=fixi, axis=0)))

        def fix_scatter(f, dest):
            G.wait((V.sem, V.n))
            return c_fix.did(pool.indirect_dma_start(dest, bass.IndirectOffsetOnAxis(ap=fixi, axis=0),
                                                     fx[:, W0:W0 + f], None))

        def fix_sums(f, dest):
            m = fix_gather(f, dest)
            final = state(NCH - 1, f)[:, TC - 1, :]
            to_rows(f, final, 128)
            V.settle()
            vv(v.tensor_tensor_scan(fC[0:f, 1:129], contT[0:f, :], fx[0:f, 128:256], 0.0, ALU.mult, ALU.add))
            V.settle()
            carry = fx[:, W0 + 64:W0 + 64 + f]
            to_cols(f, fC[0:f, 0:P], carry)
            V.wait(m)
            V.settle()
            vv(v.scalar_tensor_tensor(fx[:, W0:W0 + f], carry, samep, fx[:, W0:W0 + f], ALU.mult, ALU.add))
            return fix_scatter(f, dest)

        def fix_softmax(H, D, dest):
            f, w = H * (2 + D), 1 + D
            m = fix_gather(f, dest)
            final = state(NCH - 1, f)[:, TC - 1, :]
            mrow, arow = fx[:, W0:W0 + H], fx[:, W0 + H:W0 + f]
            o = W0 + 64
            mx, mp, f1, f0, bb = (fx[:, o + 4 * i:o + 4 * i + H] for i in range(5))
            d0, d1 = fx[:, o + 32:o + 32 + H * w], fx[:, o + 96:o + 96 + H * w]
            cprev = fx[:, o + 160:o + 160 + H * w]
            to_rows(H, final[:, 0:H], 128)
            V.settle()
            vv(v.tensor_tensor_scan(fM[0:H, 1:129], nbT[0:H, :], fx[0:H, 128:256], -BIG, ALU.add, ALU.max))
            V.settle()
            to_cols(H, fM[0:H, 1:129], mx)
            V.settle()
            to_cols(H, fM[0:H, 0:P], mp)
            V.settle()
            vv(v.tensor_tensor(f1, final[:, 0:H], mx, ALU.subtract))
            vv(v.tensor_tensor(f0, mp, mx, ALU.subtract))
            V.settle()
            e = vv(v.tensor_scalar(f0, f0, 0.0, None, ALU.min))
            A.wait(e)
            A.did(a.activation(f1, f1, ACT.Exp))
            e = A.did(a.activation(f0, f0, ACT.Exp))
            V.wait(e)
            vv(v.tensor_scalar(f0, f0, contc, None, ALU.mult))
            V.settle()
            vv(v.tensor_tensor(v3(d1, w), v3(final[:, H:f], w), bc(f1, 2, w), ALU.mult))
            vv(v.tensor_copy(v3(d0, w), bc(f0, 2, w)))
            V.settle()
            to_rows(H * w, d0, 0)
            to_rows(H * w, d1, 128)
            V.settle()
            vv(v.tensor_tensor_scan(fC[0:H * w, 1:129], fx[0:H * w, 0:P], fx[0:H * w, 128:256], 0.0, ALU.mult, ALU.add))
            V.settle()
            to_cols(H * w, fC[0:H * w, 0:P], cprev)
            V.wait(m)
            V.settle()
            vv(v.tensor_scalar(mp, mp, nsamep, None, ALU.add))
            V.settle()
            vv(v.tensor_tensor(mx, mrow, mp, ALU.max))
            V.settle()
            vv(v.tensor_tensor(f1, mrow, mx, ALU.subtract))
            vv(v.tensor_tensor(bb, mp, mx, ALU.subtract))
            V.settle()
            vv(v.tensor_copy(mrow, mx))
            A.wait((V.sem, V.n))
            A.did(a.activation(f1, f1, ACT.Exp))
            e = A.did(a.activation(bb, bb, ACT.Exp))
            V.wait(e)
            vv(v.tensor_scalar(bb, bb, samep, None, ALU.mult))
            vv(v.tensor_tensor(v3(arow, w), v3(arow, w), bc(f1, 2, w), ALU.mult))
            V.settle()
            vv(v.tensor_tensor(v3(cprev, w), v3(cprev, w), bc(bb, 2, w), ALU.mult))
            V.settle()
            vv(v.tensor_tensor(arow, arow, cprev, ALU.add))
            return fix_scatter(f, dest)

        xT_used = {}

        def node_product(inp, K, ones, xT, W, width, evac, J):
            per = 512 // width
            n = min(4, 2 * per)
            groups = [(j, min(n, J.stop - j)) for j in range(J.start, J.stop, n)]
            M.wait((V.sem, V.n), (A.sem, A.n))
            used = xT_used.setdefault(id(xT), [None, None])
            copied = {}
            for g in range(len(groups) + 1):
                if g < len(groups):
                    j0, cnt = groups[g]
                    M.wait(freeA[g % 2])
                    for i in range(cnt):
                        m = turned(psA[g % 2], i * P, inp(j0 + i), K)
                    A.wait(m, used[g % 2])
                    o = (g % 2) * 512
                    copied[g] = A.did(a.activation(xT[0:K, o:o + cnt * P], psA[g % 2][0:K, 0:cnt * P], ACT.Copy))
                    freeA[g % 2] = copied[g]
                if g > 0:
                    j0, cnt = groups[g - 1]
                    b = (g - 1) % 3
                    M.wait(copied[g - 1], freeB[b])
                    o = ((g - 1) % 2) * 512
                    for i in range(cnt):
                        at = (i // per) * 512 + (i % per) * width
                        m = M.did(pe.matmul(psB[b][:, at:at + width], xT[0:K + ones, o + i * P:o + (i + 1) * P], W,
                                            start=True, stop=True))
                    used[(g - 1) % 2] = m
                    for i in range(0, cnt, per):
                        q = min(per, cnt - i)
                        at = (i // per) * 512
                        freeB[b] = evac(j0 + i, q, psB[b][:, at:at + q * width].rearrange("p (j w) -> p j w", w=width), m)

        def layernorm(dest, r, J):
            d = v3(Sb[:, 0:NJ * 16], 16)[:, J, :]
            q = v3(Sb[:, NJ * 16:NJ * 32], 16)[:, J, :]
            s, t = nt[:, J], nt[:, NJ + J.start:NJ + J.stop]
            V.settle()
            vv(v.tensor_reduce(s, r, AX.X, ALU.add))
            V.settle()
            vv(v.tensor_scalar(s, s, 1.0 / 16, None, ALU.mult))
            V.settle()
            vv(v.tensor_tensor(d, r, bc(s, 2, 16), ALU.subtract))
            V.settle()
            vv(v.tensor_tensor(q, d, d, ALU.mult))
            V.settle()
            vv(v.tensor_reduce(t, q, AX.X, ALU.add))
            V.settle()
            e = vv(v.tensor_scalar(t, t, 1.0 / 16, 1.0e-5, ALU.mult, ALU.add))
            A.wait(e)
            e = A.did(a.activation(s, t, ACT.Sqrt))
            V.wait(e)
            vv(v.reciprocal(t, s))
            V.settle()
            vv(v.tensor_tensor(dest[:, J, :], d, bc(t, 2, 16), ALU.mult))
            V.settle()

        xv, hv = v3(xcur[:, :], 16), v3(hcur[:, :], 16)

        for i in range(2):
            vv(v.tensor_tensor(vtmp[0:16, :], l2ws[:, :], avec[:, 96 * i:96 * i + 96], ALU.mult))
            V.settle()
            vv(v.tensor_reduce(v1[:, 3 * i:3 * i + 3], v3(vtmp[0:16, :], 32), AX.X, ALU.add))
            V.settle()
        for i in range(2):
            vv(v.tensor_tensor(vtmp[:, 0:32], w2x[:, 0:32], a2vec[:, 32 * i:32 * i + 32], ALU.mult))
            V.settle()
            vv(v.tensor_reduce(w2x[:, 32 + i:33 + i], vtmp[:, 0:32], AX.X, ALU.add))
            V.settle()

        m_fnd = search1()

        def messages0(c):
            s = c % 2
            V.wait(m_ew[s], m_typ)
            V.settle()
            pr = v3(prod[:, 0:TC * 24], 24)
            vv(v.tensor_tensor(pr[:, :, 16:24], bc(typi[:, span(c)], 2, 8), bc(io8, 1, TC), ALU.is_equal))
            free_g[s] = vv(v.tensor_tensor(pr[:, :, 0:16], got(c, 16), bc(ewc[:, s * TC:(s + 1) * TC], 2, 16), ALU.mult))
            if c + 2 < NCH:
                S.wait(free_g[s])
                m_ew[s] = c_ew[s].did(sp.dma_start(ewc[:, s * TC:(s + 1) * TC], ew[:, span(c + 2)]))
            return sums(c, 24, lambda k: pr[:, :, k])

        m_ew = [c_ew[i].did(sp.dma_start(ewc[:, i * TC:(i + 1) * TC], ew[:, span(i)])) for i in range(2)]
        st = {}

        def hook(fn, *args):
            return lambda: st.__setitem__(fn.__name__ + str(len(st)), fn(*args))

        def h1():
            st["a"] = rows_of(samp_d, NS, 0, (m_fnd, m_s1))

        def h2():
            st["a"] = count_rows(blk, NS, 0, st["a"])

        def h3():
            st["b"] = rows_of(samp_d, NS, 1, (st["a"],))

        def h4():
            st["b"] = search_blocks(count_rows(blk, NS, 1, st["b"]))

        def h5():
            st["a"] = rows_of(dst.rearrange("p (s w) -> (p s) w", w=SW), SW, 0, (st["b"],))

        def h6():
            st["a"] = count_rows(cum, SW, 0, st["a"])

        def h7():
            st["b"] = rows_of(dst.rearrange("p (s w) -> (p s) w", w=SW), SW, 1, (st["a"],))

        def h8():
            count_rows(cum, SW, 1, st["b"])
            st["e"] = search_ends()

        V.wait(m_w)
        for b in range(NB):
            split(slice(b * JB, (b + 1) * JB), xv[:, b * JB:(b + 1) * JB, :], 16, xp16)
        m_key = pick_keys()
        low = arena[:, 2496:NJ * 48]
        message_pass(0, x, srci, 16, 24, S0, messages0, (m_src,), picker(0, 16, xp16, low, (0, 1, 2)),
                     {4 + 2 * i: h for i, h in enumerate((h1, h2, h3, h4, h5, h6, h7, h8))})
        ends = st["e"]
        G.wait(ends)
        xt12 = v3(XT[:, :], 12)
        lg3, lg1 = v3(lg[:, 0:NJ * 3], 3), lg[:, NJ * 3:NJ * 4]
        wk = v3(Sb[:, NJ * 32:NJ * 48], 16)

        def blocks(f, dest, fixed, stage):
            G.wait(fixed, (V.sem, V.n), (M.sem, M.n))
            for b in range(NB):
                for j in range(b * JB, (b + 1) * JB):
                    m = c_ext[b].did(pool.indirect_dma_start(
                        ext[:, j * f:(j + 1) * f], None, dest,
                        bass.IndirectOffsetOnAxis(ap=endi[:, j:j + 1], axis=0)))
                arrived[b] = m
            for b in range(NB):
                V.wait(arrived[b])
                J = slice(b * JB, (b + 1) * JB)
                stage(J, v3(ext[:, 0:NJ * f], f)[:, J, :])

        arrived = [None] * NB

        def save(table, tile, f, J):
            S.wait((V.sem, V.n), (A.sem, A.n))
            return c_tab.did(sp.dma_start(table.rearrange("(p j) f -> p j f", p=P)[:, J, :], v3(tile[:, 0:NJ * f], f)[:, J, :]))

        def nodes0(J, ex):
            vv(v.tensor_tensor(ex, ex, bc(mask[:, J], 2, 24), ALU.mult))
            V.settle()
            deg, w = invdeg[:, J], wk[:, J, :]
            vv(v.tensor_reduce(deg, ex[:, :, 16:24], AX.X, ALU.add))
            vv(v.tensor_tensor(w, ex[:, :, 0:16], bc(l0wb[:, :], 1, JB), ALU.mult))
            vv(v.tensor_scalar(xt12[:, J, 4:12], ex[:, :, 16:24], 1.0, None, ALU.max))
            V.settle()
            vv(v.tensor_scalar(deg, deg, 1.0, None, ALU.max))
            vv(v.scalar_tensor_tensor(w, xv[:, J, :], l0sb[:, 0:1], w, ALU.mult, ALU.add))
            vv(v.reciprocal(xt12[:, J, 4:12], xt12[:, J, 4:12]))
            V.settle()
            vv(v.reciprocal(deg, deg))
            vv(v.tensor_tensor(w, w, xv[:, J, :], ALU.add))
            V.settle()
            vv(v.tensor_scalar(w, w, 0.0, 1.0, ALU.max, ALU.min))
            V.settle()
            vv(v.tensor_tensor(w, w, xv[:, J, :], ALU.add))
            layernorm(xv, w, J)
            st["ready"] = save(tab1[0], xcur, 16, J)
            split(J, xv[:, J, :], 16, xp16)
            vv(v.tensor_copy(hv[:, J, :], xv[:, J, :]))

        V.wait(m_zero)
        vv(v.memset(XT[:, :], 0.0))
        blocks(24, S0, fix_sums(24, S0), nodes0)

        NG = T // 4
        NQ = (T // 8 + 1) // 2
        atts = [ext[0:26, i * 1024:(i + 1) * 1024] for i in range(3)]
        pr1 = [prod[:, i * 1024:(i + 1) * 1024] for i in range(2)]
        msg = v3(prod[:, 2048:2048 + TC * 16], 16)

        def message_net(rep):
            M.wait((V.sem, V.n))
            m_att, used_att = {}, {}
            hid_ready, hid_used, w_ready = {}, {}, {}

            def att_load(q):
                n = min(1024, T // 8 * 512 - q * 1024)
                S.wait(used_att.get(q - 3), (V.sem, V.n) if q == 0 else None)
                m_att[q] = c_att[q % 3].did(sp.dma_start(atts[q % 3][:, 0:n], attrT[:, q * 1024:q * 1024 + n]))

            def hidden(h):
                q, o, s = h // 2, (h % 2) * 512, h % 2
                M.wait(m_att[q], freeA[s])
                used_att[q] = m = M.did(pe.matmul(psA[s][:, :], w1s[:, :], atts[q % 3][:, o:o + 512], start=True, stop=True))
                A.wait(m, hid_used.get(h - 2))
                hid_ready[h] = freeA[s] = A.did(a.activation(hid[:, s * 512:(s + 1) * 512], psA[s][:, :], ACT.Relu,
                                                             bias=b1s[:, 0:1]))

            def weights(k):
                h = k // 2
                M.wait(hid_ready[h], freeB[k % 2])
                for i in range(4):
                    o = (h % 2) * 512 + i * P
                    m = M.did(pe.matmul(psB[k % 2][:, i * 256:(i + 1) * 256], hid[:, o:o + P],
                                        w2as[:, 256 * (k % 2):256 * (k % 2) + 256], start=True, stop=True))
                hid_used[h] = w_ready[k] = m

            def step(k):
                if k % 2 == 0 and k // 2 + 1 < T // 8:
                    h = k // 2 + 1
                    if h % 2 == 0 and h // 2 + 2 < NQ:
                        att_load(h // 2 + 2)
                    hidden(h)
                weights(k)

            def messages1(c):
                gv = got(c, 16)
                base = c * TC // 4
                reduced = [None, None]
                V.settle()

                def reduce(i):
                    V.wait(multiplied[i])
                    reduced[i % 2] = vv(v.tensor_reduce(msg[:, 4 * i:4 * i + 4, :], pr1[i % 2].rearrange(
                        "p (t o i) -> p t o i", t=4, o=16), AX.X, ALU.add))

                multiplied = {}
                for i in range(TC // 4):
                    k = base + i
                    if k + 1 < NG:
                        step(k + 1)
                    between(0.9 * i * 4 / TC)
                    V.wait(w_ready[k], reduced[i % 2])
                    multiplied[i] = vv(v.tensor_tensor(
                        pr1[i % 2].rearrange("p (t o i) -> p t o i", t=4, o=16),
                        psB[k % 2][:, :].rearrange("p (t o i) -> p t o i", t=4, o=16),
                        bc(gv[:, 4 * i:4 * i + 4, :], 2, 16), ALU.mult))
                    freeB[k % 2] = multiplied[i]
                    if i:
                        reduce(i - 1)
                reduce(TC // 4 - 1)
                free_g[c % 2] = multiplied[TC // 4 - 1]
                return sums(c, 16, lambda k: msg[:, :, k])

            for q in range(3):
                att_load(q)
            hidden(0)
            step(0)
            return messages1

        t2 = v3(prod[:, 0:NJ * 20], 20)

        def gru(rep):
            cat = v3(gb[:, 0:NJ * 32], 32)
            rz = v3(arena[:, 0:NJ * 32], 32)
            nn = v3(arena[:, NJ * 32:NJ * 48], 16)

            def gates(J, ex):
                vv(v.tensor_tensor(cat[:, J, 0:16], ex, bc(mask[:, J], 2, 16), ALU.mult))
                vv(v.tensor_copy(cat[:, J, 16:32], hv[:, J, :]))
                V.settle()
                vv(v.tensor_tensor(cat[:, J, 0:16], cat[:, J, 0:16], bc(invdeg[:, J], 2, 16), ALU.mult))

                def evac(j0, q, ps, m):
                    A.wait(m)
                    e = A.did(a.activation(rz[:, j0:j0 + q, :], ps[:, :, 0:32], ACT.Sigmoid))
                    V.wait(e)
                    vv(v.tensor_tensor(nn[:, j0:j0 + q, :], rz[:, j0:j0 + q, 0:16], ps[:, :, 48:64], ALU.mult))
                    V.settle()
                    return vv(v.tensor_tensor(nn[:, j0:j0 + q, :], nn[:, j0:j0 + q, :], ps[:, :, 32:48], ALU.add))

                node_product(lambda j: cat[:, j, :], 32, 2, xT32, gws[:, :], 64, evac, J)
                A.wait((V.sem, V.n))
                e = A.did(a.activation(nn[:, J, :], nn[:, J, :], ACT.Tanh))
                V.wait(e)
                vv(v.tensor_tensor(hv[:, J, :], hv[:, J, :], nn[:, J, :], ALU.subtract))
                V.settle()
                vv(v.tensor_tensor(hv[:, J, :], hv[:, J, :], rz[:, J, 16:32], ALU.mult))
                V.settle()
                vv(v.tensor_tensor(hv[:, J, :], hv[:, J, :], nn[:, J, :], ALU.add))
                if rep == 0:
                    st["ready"] = save(tab1[1], hcur, 16, J)
                    split(J, hv[:, J, :], 16, xp16)
                    return
                V.settle()
                vv(v.tensor_tensor(wk[:, J, :], xv[:, J, :], hv[:, J, :], ALU.add))
                layernorm(xv, wk[:, J, :], J)
                vv(v.tensor_copy(t2[:, J, 0:16], xv[:, J, :]))
                vv(v.memset(t2[:, J, 19:20], 0.0))

                def logits(j0, q, ps, m):
                    V.wait(m)
                    vv(v.tensor_copy(t2[:, j0:j0 + q, 16:19], ps[:, :, 0:3]))
                    return vv(v.tensor_copy(xt12[:, j0:j0 + q, 0:3], ps[:, :, 3:6]))

                node_product(lambda j: xv[:, j, :], 16, 0, xT16, v1[:, :], 6, logits, J)
                self_logits(lg3[:, J, :], t2[:, J, 16:19], xt12[:, J, 0:3])
                save(tab2a, prod, 20, J)
                split(J, t2[:, J, :], 20, p2a)
                spread_block(J, XT, 12, xe2a)
                st["ready"] = save(xn2a, XT, 12, J)

            return gates

        def self_logits(dest, s, d):
            V.settle()
            vv(v.tensor_tensor(dest, s, d, ALU.add))
            V.settle()
            vv(v.scalar_tensor_tensor(dest, dest, 0.2, dest, ALU.mult, ALU.max))
            V.settle()

        def spread_block(J, tile, f, edges):
            G.wait((V.sem, V.n), m_zero)
            for j in range(J.start, J.stop):
                c_sct.did(pool.indirect_dma_start(
                    edges, bass.IndirectOffsetOnAxis(ap=stai[:, j:j + 1], axis=0), tile[:, j * f:(j + 1) * f], None,
                    bounds_check=EP - 1, oob_is_err=False))

        def spread_first(nodes, f, saved):
            G.wait(saved)
            return c_sct.did(pool.indirect_dma_start(x0[:, 0:f], None, nodes,
                                                     bass.IndirectOffsetOnAxis(ap=firsti, axis=0)))

        for rep in range(2):
            message_pass(1 + rep, tab1[rep], srci, 16, 16, S1[rep], message_net(rep), (st["ready"],),
                         picker(1 + rep, 16, xp16, low, (2,)))
            blocks(16, S1[rep], fix_sums(16, S1[rep]), gru(rep))

        def softmax_pass(k, table, H, D, width, dest, edges, ef, used, spread_done, ready, pick, extra=None):
            f, w = H * (2 + D), 1 + D
            zz, d0, nb = sub[:, 0:TC * H], sub[:, TC * H:2 * TC * H], sub[:, 2 * TC * H:2 * TC * H + TC]
            da = sub[:, TC * 7:TC * (7 + 2 * H)]
            e, p = da[:, 0:TC * H], da[:, TC * H:2 * TC * H]
            xes = [arena[:, i * TC * 12:i * TC * 12 + TC * ef] for i in range(2)]
            exs = [arena[:, (2 + i) * TC * 12:(2 + i) * TC * 12 + TC * ef] for i in range(2)]
            ev = rows(edges, ef)
            m_xe = [None, None]

            def load(c):
                m_xe[c % 2] = c_xe[c % 2].did(sp.dma_start(v3(xes[c % 2], ef), ev[:, span(c), :]))

            S.wait((V.sem, V.n), (A.sem, A.n), (M.sem, M.n), spread_done)
            load(0)
            load(1)

            def messages(c):
                s = c % 2
                xe, xs, xo = v3(xes[s], ef), v3(exs[s], ef), v3(exs[1 - s], ef)
                gv, now, old = got(c, width), state(c, f), state(c + 1, f)
                pr = v3(prod[:, 0:TC * H * w], H * w)
                V.wait(m_xe[s], sent[s], spread_done)
                V.settle()
                for i in used:
                    m = vv(v.tensor_tensor_scan(xs[:, :, i], same[:, span(c)], xe[:, :, i],
                                                xo[:, TC - 1, i:i + 1] if c else x0[:, i:i + 1], ALU.mult, ALU.add))
                if c + 2 < NCH:
                    S.wait(m)
                    load(c + 2)
                vv(v.tensor_scalar(nb, same[:, span(c)], -1.0, BIG, ALU.add, ALU.mult))
                between(0.15)
                V.settle()
                vv(v.tensor_tensor(v3(zz, H), gv[:, :, D:D + H], xs[:, :, 0:H], ALU.add))
                if extra:
                    extra(c, xs)
                V.settle()
                vv(v.scalar_tensor_tensor(e, zz, 0.2, zz, ALU.mult, ALU.max))
                V.settle()
                for h in range(H):
                    vv(v.tensor_tensor_scan(now[:, :, h], nb, v3(e, H)[:, :, h], old[:, TC - 1, h:h + 1] if c else -BIG,
                                            ALU.add, ALU.max))
                between(0.3)
                V.settle()
                z3 = v3(zz, H)
                vv(v.tensor_tensor(z3[:, 1:TC, :], now[:, 0:TC - 1, 0:H], now[:, 1:TC, 0:H], ALU.subtract))
                if c:
                    vv(v.tensor_tensor(z3[:, 0, :], old[:, TC - 1, 0:H], now[:, 0, 0:H], ALU.subtract))
                else:
                    vv(v.memset(z3[:, 0, :], 0.0))
                vv(v.tensor_tensor(v3(p, H), v3(e, H), now[:, :, 0:H], ALU.subtract))
                V.settle()
                m = vv(v.tensor_scalar(e, zz, 0.0, None, ALU.min))
                A.wait(m)
                m = A.did(a.activation(da, da, ACT.Exp))
                between(0.45)
                V.wait(m)
                vv(v.tensor_tensor(v3(d0, H), v3(e, H), bc(same[:, span(c)], 2, H), ALU.mult))
                for h in range(H):
                    vv(v.tensor_copy(pr[:, :, h * w], v3(p, H)[:, :, h]))
                    free_g[s] = vv(v.tensor_tensor(pr[:, :, h * w + 1:(h + 1) * w], gv[:, :, 0:D],
                                                   bc(v3(p, H)[:, :, h], 2, D), ALU.mult))
                return sums(c, f, lambda i: pr[:, :, i - H], lambda i: v3(d0, H)[:, :, (i - H) // w], range(H, f))

            message_pass(k, table, srci, width, f, dest, messages, ready, pick)

        def softmax_nodes(H, D, J, ex, logits, feats):
            f, w = H * (2 + D), 1 + D
            m, z = ex[:, :, 0:H], ex[:, :, H:f].rearrange("p j (h w) -> p j h w", w=w)
            o = J.start * 3 * H
            n = JB * H
            t = [v3(Sb[:, o + i * n:o + (i + 1) * n], H) for i in range(3)]
            V.settle()
            vv(v.tensor_tensor(ex, ex, bc(mask[:, J], 2, f), ALU.mult))
            V.settle()
            vv(v.tensor_tensor(m, m, bc(nmask[:, J], 2, H), ALU.add))
            V.settle()
            vv(v.tensor_tensor(t[0], m, logits, ALU.max))
            V.settle()
            vv(v.tensor_tensor(t[1], m, t[0], ALU.subtract))
            vv(v.tensor_tensor(t[2], logits, t[0], ALU.subtract))
            A.wait((V.sem, V.n))
            e = A.did(a.activation(Sb[:, o + n:o + 3 * n], Sb[:, o + n:o + 3 * n], ACT.Exp))
            tmp = [v3(Sb[:, NJ * 9 + h * JB * D:NJ * 9 + (h + 1) * JB * D], D) for h in range(H)]
            V.wait(e)
            for h in range(H):
                vv(v.tensor_tensor(z[:, :, h, :], z[:, :, h, :], bc(t[1][:, :, h], 2, w), ALU.mult))
                vv(v.tensor_tensor(tmp[h], feats, bc(t[2][:, :, h], 2, D), ALU.mult))
            V.settle()
            for h in range(H):
                vv(v.tensor_tensor(z[:, :, h, 0], z[:, :, h, 0], t[2][:, :, h], ALU.add))
                vv(v.tensor_tensor(z[:, :, h, 1:w], z[:, :, h, 1:w], tmp[h], ALU.add))
            V.settle()
            vv(v.tensor_scalar(t[0], z[:, :, :, 0], 1.0e-16, None, ALU.add))
            V.settle()
            vv(v.reciprocal(t[0], t[0]))
            V.settle()
            return z, t[0]

        def edge_weight(c, xs):
            oh = v3(prod[:, 0:TC * 8], 8)
            tc = typi[:, span(c)]
            vv(v.tensor_tensor(oh, bc(tc, 2, 8), bc(io8, 1, TC), ALU.is_equal))
            V.settle()
            vv(v.tensor_tensor(oh, oh, xs[:, :, 4:12], ALU.mult))
            vv(v.scalar_tensor_tensor(tc, srci[:, span(c)], 8.0, tc, ALU.mult, ALU.add))
            V.settle()
            vv(v.tensor_reduce(wE[:, span(c)], oh, AX.X, ALU.add))

        def selu(dest, src_ap, tmp):
            e = vv(v.tensor_scalar(tmp, src_ap, 0.0, None, ALU.min))
            A.wait(e)
            e = A.did(a.activation(tmp, tmp, ACT.Exp))
            vv(v.tensor_scalar(dest, src_ap, 0.0, SELU_S, ALU.max, ALU.mult))
            V.wait(e)
            vv(v.tensor_scalar(tmp, tmp, SELU_S * SELU_A, -SELU_S * SELU_A, ALU.mult, ALU.add))
            V.settle()
            return vv(v.tensor_tensor(dest, dest, tmp, ALU.add))

        spread_done = spread_first(xn2a, 12, st["ready"])
        softmax_pass(3, tab2a, 3, 16, 20, S2a, xe2a, 12, (0, 1, 2) + tuple(range(4, 12)), spread_done, (st["ready"],),
                     picker(3, 20, p2a, low, (0, 1, 2)), edge_weight)
        an = v3(arena[:, :], 48)
        t2b = v3(gb[:, 0:NJ * 36], 36)
        ad2t = XT[:, 0:NJ]
        hT = [prod[0:96, i * 512:(i + 1) * 512] for i in range(2)]
        hE = [prod[0:96, (2 + i) * 512:(3 + i) * 512] for i in range(2)]
        hT_used = [None, None]

        def nodes2a(J, ex):
            z, r = softmax_nodes(3, 16, J, ex, lg3[:, J, :], xv[:, J, :])
            for h in range(3):
                vv(v.tensor_tensor(an[:, J, 16 * h:16 * h + 16], z[:, :, h, 1:17], bc(r[:, :, h], 2, 16), ALU.mult))
            vv(v.memset(t2b[:, J, 33:36], 0.0))
            M.wait((V.sem, V.n), (A.sem, A.n))
            groups = [(j, min(4, J.stop - j)) for j in range(J.start, J.stop, 4)]
            for g, (j0, cnt) in enumerate(groups):
                s = g % 2
                M.wait(freeA[s])
                for i in range(cnt):
                    m = turned(psA[s], i * P, an[:, j0 + i, :], 48)
                A.wait(m, hT_used[s])
                freeA[s] = A.did(a.activation(xT48[0:48, s * 512:s * 512 + cnt * P], psA[s][0:48, 0:cnt * P], ACT.Copy))
                M.wait(freeA[s], freeB[0])
                m = M.did(pe.matmul(psB[0][0:96, 0:cnt * P], l2bs[:, :], xT48[0:49, s * 512:s * 512 + cnt * P],
                                    start=True, stop=True))
                V.wait(m, hT_used[s])
                freeB[0] = selu(hT[s][:, 0:cnt * P], psB[0][0:96, 0:cnt * P], hE[s][:, 0:cnt * P])
                b = 1 + s
                M.wait(freeB[0], freeB[b])
                for i in range(cnt):
                    m = M.did(pe.matmul(psB[b][:, i * 34:(i + 1) * 34], hT[s][:, i * P:(i + 1) * P], w2x[:, :],
                                        start=True, stop=True))
                hT_used[s] = m
                V.wait(m)
                pv = psB[b][:, 0:cnt * 34].rearrange("p (j w) -> p j w", w=34)
                vv(v.tensor_copy(t2b[:, j0:j0 + cnt, 0:33], pv[:, :, 0:33]))
                freeB[b] = vv(v.tensor_copy(ad2t[:, j0:j0 + cnt], pv[:, :, 33]))
            self_logits(lg1[:, J], t2b[:, J, 32], ad2t[:, J])
            save(tab2b, gb, 36, J)
            split(J, t2b[:, J, 0:33], 33, p2b)
            spread_block(J, XT, 1, xe2b)
            st["ready"] = save(xn2b, XT, 1, J)

        vv(v.memset(xT48[:, :], 1.0))
        blocks(54, S2a, fix_softmax(3, 16, S2a), nodes2a)
        spread_done = spread_first(xn2b, 1, st["ready"])
        softmax_pass(4, tab2b, 1, 32, 36, S2b, xe2b, 1, (0,), spread_done, (st["ready"],), picker(4, 33, p2b, low, (0, 1, 2)))
        f32v = v3(gb[:, 0:NJ * 32], 32)
        S.wait((V.sem, V.n))
        m_feats = c_tab.did(sp.dma_start(f32v, tab2b.rearrange("(p j) f -> p j f", p=P)[:, :, 0:32]))
        h2 = v3(arena[:, 0:NJ * 32], 32)

        stage = [prod[:, i * 1024:(i + 1) * 1024] for i in range(2)]
        m_y = [None, None]
        turn = [0]

        def table3(inp, K, W, width, xT, table, J):
            tv = table.rearrange("(p j r) w -> p j (r w)", p=P, r=8)
            size = 1024 // (8 * width)

            def evac(j0, q, ps, m):
                at = (j0 - J.start) % size
                if at == 0:
                    turn[0] += 1
                b = turn[0] % 2
                V.wait(m, m_y[b])
                e = vv(v.tensor_copy(stage[b][:, at * 8 * width:(at + q) * 8 * width].rearrange("p (j w) -> p j w", j=q), ps))
                if at + q == size or j0 + q == J.stop:
                    S.wait(e)
                    m_y[b] = c_y[b].did(sp.dma_start(tv[:, j0 - at:j0 + q, :], stage[b][:, 0:(at + q) * 8 * width].rearrange(
                        "p (j w) -> p j w", w=8 * width)))
                return e

            node_product(inp, K, 0, xT, W, 8 * width, evac, J)

        def nodes2b(J, ex):
            V.wait(m_feats)
            z, r = softmax_nodes(1, 32, J, ex, lg1[:, J].unsqueeze(2), f32v[:, J, :])
            fv, hj = f32v[:, J, :], h2[:, J, :]
            vv(v.tensor_tensor(fv, z[:, :, 0, 1:33], bc(r[:, :, 0], 2, 32), ALU.mult))
            V.settle()
            vv(v.tensor_tensor(fv, fv, bc(b2b[:, :], 1, JB), ALU.add))
            V.settle()
            selu(hj, fv, ex[:, :, 0:32])

            def add_x(j0, q, ps, m):
                V.wait(m)
                return vv(v.tensor_tensor(hv[:, j0:j0 + q, :], ps, xv[:, j0:j0 + q, :], ALU.add))

            node_product(lambda j: h2[:, j, :], 32, 1, xT32, wfs[:, :], 16, add_x, J)
            layernorm(xv, hv[:, J, :], J)
            split(J, xv[:, J, :], 16, xp16)
            table3(lambda j: xv[:, j, :], 16, l3w1s[:, :], 32, xT16, tab3a, J)

        blocks(34, S2b, fix_softmax(1, 32, S2b), nodes2b)

        def messages3(width):
            def messages(c):
                V.settle()
                pr = v3(prod[:, 0:TC * width], width)
                free_g[c % 2] = vv(v.tensor_tensor(pr, got(c, width), bc(wE[:, span(c)], 2, width), ALU.mult))
                return sums(c, width, lambda k: pr[:, :, k])
            return messages

        h3 = v3(gb[:, 0:NJ * 32], 32)

        def nodes3(J, ex):
            vv(v.tensor_tensor(ex, ex, bc(mask[:, J], 2, 32), ALU.mult))
            V.settle()

            def add_root(j0, q, ps, m):
                V.wait(m)
                return vv(v.tensor_tensor(h3[:, j0:j0 + q, :], ps, ex[:, j0 - J.start:j0 - J.start + q, :], ALU.add))

            def add_root2(j0, q, ps, m):
                V.wait(m)
                return vv(v.tensor_tensor(hv[:, j0:j0 + q, :], ps, xv[:, j0:j0 + q, :], ALU.add))

            node_product(lambda j: xv[:, j, :], 16, 1, xT16, r1s[:, :], 32, add_root, J)
            V.settle()
            vv(v.tensor_scalar(h3[:, J, :], h3[:, J, :], 0.0, None, ALU.max))
            V.settle()
            split(J, h3[:, J, :], 32, p3b)
            table3(lambda j: h3[:, j, :], 32, l3w2s[:, :], 16, xT32, tab3b, J)
            node_product(lambda j: h3[:, j, :], 32, 1, xT32, r2s[:, :], 16, add_root2, J)

        message_pass(5, tab3a, typi, 32, 32, S3a, messages3(32), tuple(m_y),
                     picker(5, 16, xp16, low, (0, 1, 2), (l3w1s[:, :], xT16, arena[:, 0:2496])))
        blocks(32, S3a, fix_sums(32, S3a), nodes3)
        message_pass(6, tab3b, typi, 16, 16, S3b, messages3(16), tuple(m_y) + ((M.sem, M.n),),
                     picker(6, 32, p3b, ext[:, 0:2208], (0, 1, 2), (l3w2s[:, :], xT32, ext[:, 2208:NJ * 54])))

        def nodes_out(J, ex):
            vv(v.tensor_tensor(ex, ex, bc(mask[:, J], 2, 16), ALU.mult))
            V.settle()
            vv(v.tensor_tensor(hv[:, J, :], hv[:, J, :], ex, ALU.add))
            layernorm(xv, hv[:, J, :], J)

        blocks(16, S3b, fix_sums(16, S3b), nodes_out)
        full = N // NJ
        S.wait((V.sem, V.n))
        c_fin.did(sp.dma_start(out[0:full * NJ, :].rearrange("(p j) f -> p (j f)", p=full), xcur[0:full, :]))
        m = c_fin.did(sp.dma_start(out[full * NJ:N, :].rearrange("(p j) f -> p (j f)", p=1),
                                   xcur[full:full + 1, 0:(N - full * NJ) * 16]))
        S.wait(m, *((c.sem, c.n) for c in [c_fix, c_srch, c_tab, c_set, c_zero, c_sct] + c_ext + c_out + c_y))


def kernel(**inputs):
    import numpy as np
    import concourse.bacc as bacc
    from concourse.bass_utils import run_bass_kernel_spmd as run

    i = {k: np.asarray(v) for k, v in inputs.items()}

    def padded(a, fill):
        return np.concatenate([a, np.full((EP - E,) + a.shape[1:], fill, a.dtype)])

    d = padded(i["dst"], N)
    f32 = np.float32
    z = lambda *s: np.zeros(s, f32)
    consts = np.concatenate([np.eye(P, dtype=f32), np.arange(0, EP, T, dtype=f32)[:, None],
                             np.broadcast_to(np.arange(8, dtype=f32), (P, 8)),
                             np.arange(NP, dtype=f32).reshape(P, NJ),
                             np.arange(P, dtype=f32)[:, None] + P * np.arange(NB, dtype=f32),
                             np.broadcast_to(np.arange(JB, dtype=f32), (P, JB))], 1)
    ih, hh = i["L1_gnn_gru_w_ih"].T, i["L1_gnn_gru_w_hh"].T
    bi, bh = i["L1_gnn_gru_b_ih"][None], i["L1_gnn_gru_b_hh"][None]
    gru = np.concatenate([np.concatenate([ih, z(16, 16)], 1),
                          np.concatenate([hh[:, 0:32], z(16, 16), hh[:, 32:48]], 1),
                          np.concatenate([bi, z(1, 16)], 1),
                          np.concatenate([bh[:, 0:32], z(1, 16), bh[:, 32:48]], 1)])
    oi = lambda a: a.reshape(-1, 16, 16).transpose(0, 2, 1).reshape(-1, 256)
    fw, fb, one = i["L1_gnn_fnet_w1"], i["L1_gnn_fnet_b1"], np.ones(1, f32)
    f2 = np.concatenate([oi(i["L1_gnn_fnet_w2"]), oi(i["L1_gnn_fnet_b2"])])
    w1 = i["L2_gnn_W1"]
    blk = z(49, 96)
    for h in range(3):
        blk[16 * h:16 * h + 16, 32 * h:32 * h + 32] = w1[:, 32 * h:32 * h + 32]
    blk[48] = i["L2_gnn_b1"]
    arrays = {
        "x": np.concatenate([i["x"], z(NP - N, 16)]),
        "src": padded(i["src"], 0).reshape(P, T),
        "srcT": padded(i["src"], 0).reshape(P, NCH, TC)[:, :, TC - KM:].transpose(1, 2, 0).reshape(P, KT), "dst": d.reshape(P, T),
        "prv": np.concatenate([np.full(1, -1, d.dtype), d[:-1]]).reshape(P, T),
        "attrT": padded(i["edge_attr_13"], 0).reshape(P, T // 8, 2, 4, 13).transpose(2, 4, 1, 3, 0).reshape(26, EP // 2),
        "typ": padded(i["edge_type_8"], 0).reshape(P, T), "ew": padded(i["edge_weight"], 0).reshape(P, T),
        "consts": consts, "l0w": i["L0_gnn_weight"], "l0s": i["L0_gnn_self_loop_weight"].reshape(1),
        "w1": np.concatenate([np.concatenate([fw, z(13, 96)], 1), np.concatenate([z(13, 64), fw, z(13, 32)], 1)]),
        "b1": np.concatenate([fb, one, z(31), fb, one, z(31)]).reshape(P, 1),
        "w2a": np.concatenate([np.concatenate([f2, z(95, 256)]), np.concatenate([z(64, 256), f2, z(31, 256)])], 1), "gw": gru,
        "l2w": w1, "l2blk": blk, "as1": i["L2_gnn_a_src1"].reshape(96), "ad1": i["L2_gnn_a_dst1"].reshape(96),
        "w2s": i["L2_gnn_W2"], "as2": i["L2_gnn_a_src2"].reshape(32), "ad2": i["L2_gnn_a_dst2"].reshape(32),
        "b2": i["L2_gnn_b2"], "wf": np.concatenate([i["L2_gnn_Wf"], i["L2_gnn_bf"][None]]),
        "l3w1": i["L3_gnn_W1"].transpose(1, 0, 2).reshape(16, 256),
        "root1": np.concatenate([i["L3_gnn_root1"], i["L3_gnn_b1"][None]]),
        "l3w2": i["L3_gnn_W2"].transpose(1, 0, 2).reshape(32, 128),
        "root2": np.concatenate([i["L3_gnn_root2"], i["L3_gnn_b2"][None]]),
    }
    arrays = {k: np.ascontiguousarray(v) for k, v in arrays.items()}
    nc = bacc.Bacc("TRN2", target_bir_lowering=False, num_devices=1)
    args = [nc.dram_tensor("in_" + k, v.shape, mybir.dt.from_np(v.dtype), kind="ExternalInput").ap() for k, v in arrays.items()]
    out = nc.dram_tensor("out", (N, 16), F32, kind="ExternalOutput").ap()
    gnn_program(nc, *args, out)
    r = run(nc, [{"in_" + k: v for k, v in arrays.items()}], core_ids=[0])
    return r.results[0]["out"]
```
